# Optimizing a Trainium2 kernel written in Bass

```python
import numpy as np
import jax
import jax.numpy as jnp

def _softmax(x, axis=-1):
    return jax.nn.softmax(x, axis=axis)

def _gelu(x):
    return jax.nn.gelu(x, approximate=True)

def _silu(x):
    return jax.nn.silu(x)

def _sigmoid(x):
    return jax.nn.sigmoid(x)

def _layernorm(x, axis=-1, eps=1e-05):
    m = jnp.mean(x, axis=axis, keepdims=True)
    v = jnp.var(x, axis=axis, keepdims=True)
    return (x - m) / jnp.sqrt(v + eps)

def _scatter_add(tgt, idx, src, axis=0):
    return tgt.at[idx].add(src)

def _segment_sum(src, seg, n):
    return jax.ops.segment_sum(src, seg, n)
kernel_name = 'mk_early_fusion_d1_tok_img512_r4_fb4965'

def setup_inputs(seed: int=0):
    np.random.seed(seed)
    _w = jnp.asarray

    def _rec_inputs():
        import jax
        import jax.numpy as jnp
        _rk = jax.random.key(seed)
        x = -0.000372384 + 0.999952 * jax.random.normal(jax.random.fold_in(_rk, 1), (16, 128, 60, 108), jnp.float32)
        txt = -0.00013715 + 0.564753 * jax.random.normal(jax.random.fold_in(_rk, 2), (16, 128, 128), jnp.float32)
        return (x, txt)
    x, txt = _rec_inputs()

    def _L0_tok_setup():
        import jax, jax.numpy as jnp
        import numpy as np
        CHANNEL = 128
        HIDDEN = 128
        KH, KW = (7, 7)
        SH, SW = (3, 3)
        PH, PW = (3, 3)
        C_IN = KH * KW * CHANNEL

        def unfold(x, kh, kw, sh, sw, ph, pw):
            B, C, H, W = x.shape
            xp = jnp.pad(x, ((0, 0), (0, 0), (ph, ph), (pw, pw)))
            Ho = (H + 2 * ph - kh) // sh + 1
            Wo = (W + 2 * pw - kw) // sw + 1
            ih = (jnp.arange(Ho) * sh)[:, None] + jnp.arange(kh)[None, :]
            iw = (jnp.arange(Wo) * sw)[:, None] + jnp.arange(kw)[None, :]
            patches = xp[:, :, ih[:, None, :, None], iw[None, :, None, :]]
            patches = patches.transpose(0, 2, 3, 1, 4, 5)
            return patches.reshape(B, Ho * Wo, C * kh * kw)
        key = jax.random.key(seed)
        kx, kw_, kb = jax.random.split(key, 3)
        x = jax.random.normal(kx, (16, CHANNEL, 60, 108), dtype=jnp.float32)
        bound = 1.0 / np.sqrt(C_IN)
        W = jax.random.uniform(kw_, (HIDDEN, C_IN), minval=-bound, maxval=bound, dtype=jnp.float32)
        b = jax.random.uniform(kb, (HIDDEN,), minval=-bound, maxval=bound, dtype=jnp.float32)
        return {'x': x, 'W': W, 'b': b}
    _L0_tok_all = _L0_tok_setup()
    _L0_tok_in = {k: v for k, v in _L0_tok_all.items() if k in ('W', 'b')}
    del _L0_tok_all

    def _L0_attn_setup():
        import jax, jax.numpy as jnp
        import numpy as np
        LN_EPS = 1e-05
        LOG_HALF = float(np.log(0.5))

        def log_g(x):
            return jnp.where(x >= 0, jnp.log(jax.nn.relu(x) + 0.5), -jax.nn.softplus(-x))

        def layernorm(x, g, b):
            mu = jnp.mean(x, axis=-1, keepdims=True)
            var = jnp.mean(jnp.square(x - mu), axis=-1, keepdims=True)
            return (x - mu) * jax.lax.rsqrt(var + LN_EPS) * g + b

        def causal_conv(x, dw_w, dw_b, pw_w, pw_b):
            B, T, D = x.shape
            K = dw_w.shape[0]
            xp = jnp.pad(x, ((0, 0), (K - 1, 0), (0, 0)))
            y = dw_b
            for j in range(K):
                y = y + xp[:, j:j + T, :] * dw_w[j]
            return jnp.einsum('btd,ed->bte', y, pw_w) + pw_b

        def min_gru(x, fw):
            B, T, D = x.shape
            kh = jnp.einsum('btd,ed->bte', x, fw)
            k, h_x = (kh[..., :D], kh[..., D:])
            log_z = -jax.nn.softplus(-k)
            log_coeffs = -jax.nn.softplus(k)
            log_h0 = jnp.full((B, 1, D), LOG_HALF, dtype=x.dtype)
            log_values = jnp.concatenate([log_h0, log_g(h_x) + log_z], axis=1)
            a_star = jnp.pad(jnp.cumsum(log_coeffs, axis=1), ((0, 0), (1, 0), (0, 0)))
            log_h = a_star + jax.lax.cumlogsumexp(log_values - a_star, axis=1)
            return jnp.exp(log_h)[:, 1:]

        def mlp(x, w1, b1, w2, b2):
            h = jax.nn.relu(jnp.einsum('btd,ed->bte', x, w1) + b1)
            return jnp.einsum('bte,de->btd', h, w2) + b2
        key = jax.random.key(seed)
        ks = jax.random.split(key, 8)
        B, T, D, L, K, H = (8, 1024, 128, 4, 4, 512)
        s = 0.02
        return {'x': jax.random.normal(ks[0], (B, T, D), jnp.float32), 'conv_dw_w': jax.random.normal(ks[1], (L, K, D), jnp.float32) * s, 'conv_dw_b': jnp.zeros((L, D), jnp.float32), 'conv_pw_w': jax.random.normal(ks[2], (L, D, D), jnp.float32) * s, 'conv_pw_b': jnp.zeros((L, D), jnp.float32), 'ln1_g': jnp.ones((D,), jnp.float32), 'ln1_b': jnp.zeros((D,), jnp.float32), 'f_w': jax.random.normal(ks[3], (L, 2 * D, D), jnp.float32) * s, 'ln2_g': jnp.ones((L, D), jnp.float32), 'ln2_b': jnp.zeros((L, D), jnp.float32), 'mlp_w1': jax.random.normal(ks[4], (L, H, D), jnp.float32) * s, 'mlp_b1': jnp.zeros((L, H), jnp.float32), 'mlp_w2': jax.random.normal(ks[5], (L, D, H), jnp.float32) * s, 'mlp_b2': jnp.zeros((L, D), jnp.float32)}
    _L0_attn_all = _L0_attn_setup()
    _L0_attn_in = {k: v for k, v in _L0_attn_all.items() if k in ('conv_dw_w', 'conv_dw_b', 'conv_pw_w', 'conv_pw_b', 'ln1_g', 'ln1_b', 'f_w', 'ln2_g', 'ln2_b', 'mlp_w1', 'mlp_b1', 'mlp_w2', 'mlp_b2')}
    del _L0_attn_all

    def _L0_ffn_setup():
        import jax, jax.numpy as jnp
        import numpy as np
        DIM = 128
        HID = 256
        E = 8
        K = 2
        B, S = (4, 512)
        key = jax.random.key(seed)
        ks = jax.random.split(key, 10)
        sd = DIM ** (-0.5)
        sh = HID ** (-0.5)
        return {'x': jax.random.normal(ks[0], (B, S, DIM), dtype=jnp.float32), 'gate_w': jax.random.normal(ks[1], (E, DIM), dtype=jnp.float32) * sd, 'biases': jnp.zeros((E,), dtype=jnp.float32), 'w1': jax.random.normal(ks[2], (E, DIM, HID), dtype=jnp.float32) * sd, 'w3': jax.random.normal(ks[3], (E, DIM, HID), dtype=jnp.float32) * sd, 'w2': jax.random.normal(ks[4], (E, HID, DIM), dtype=jnp.float32) * sh, 'sw1': jax.random.normal(ks[5], (DIM, HID), dtype=jnp.float32) * sd, 'sw3': jax.random.normal(ks[6], (DIM, HID), dtype=jnp.float32) * sd, 'sw2': jax.random.normal(ks[7], (HID, DIM), dtype=jnp.float32) * sh}
    _L0_ffn_all = _L0_ffn_setup()
    _L0_ffn_in = {k: v for k, v in _L0_ffn_all.items() if k in ('gate_w', 'biases', 'w1', 'w3', 'w2', 'sw1', 'sw3', 'sw2')}
    del _L0_ffn_all
    return {'x': x, 'txt': txt, 'L0_tok_W': _L0_tok_in['W'], 'L0_tok_b': _L0_tok_in['b'], 'L0_attn_conv_dw_w': _L0_attn_in['conv_dw_w'], 'L0_attn_conv_dw_b': _L0_attn_in['conv_dw_b'], 'L0_attn_conv_pw_w': _L0_attn_in['conv_pw_w'], 'L0_attn_conv_pw_b': _L0_attn_in['conv_pw_b'], 'L0_attn_ln1_g': _L0_attn_in['ln1_g'], 'L0_attn_ln1_b': _L0_attn_in['ln1_b'], 'L0_attn_f_w': _L0_attn_in['f_w'], 'L0_attn_ln2_g': _L0_attn_in['ln2_g'], 'L0_attn_ln2_b': _L0_attn_in['ln2_b'], 'L0_attn_mlp_w1': _L0_attn_in['mlp_w1'], 'L0_attn_mlp_b1': _L0_attn_in['mlp_b1'], 'L0_attn_mlp_w2': _L0_attn_in['mlp_w2'], 'L0_attn_mlp_b2': _L0_attn_in['mlp_b2'], 'L0_ffn_gate_w': _L0_ffn_in['gate_w'], 'L0_ffn_biases': _L0_ffn_in['biases'], 'L0_ffn_w1': _L0_ffn_in['w1'], 'L0_ffn_w3': _L0_ffn_in['w3'], 'L0_ffn_w2': _L0_ffn_in['w2'], 'L0_ffn_sw1': _L0_ffn_in['sw1'], 'L0_ffn_sw3': _L0_ffn_in['sw3'], 'L0_ffn_sw2': _L0_ffn_in['sw2']}

def reference(x, txt, L0_tok_W, L0_tok_b, L0_attn_conv_dw_w, L0_attn_conv_dw_b, L0_attn_conv_pw_w, L0_attn_conv_pw_b, L0_attn_ln1_g, L0_attn_ln1_b, L0_attn_f_w, L0_attn_ln2_g, L0_attn_ln2_b, L0_attn_mlp_w1, L0_attn_mlp_b1, L0_attn_mlp_w2, L0_attn_mlp_b2, L0_ffn_gate_w, L0_ffn_biases, L0_ffn_w1, L0_ffn_w3, L0_ffn_w2, L0_ffn_sw1, L0_ffn_sw3, L0_ffn_sw2):
    import jax
    import jax.numpy as jnp

    def _L0_tok_ref(x, W, b):
        import jax, jax.numpy as jnp
        import numpy as np
        CHANNEL = 128
        HIDDEN = 128
        KH, KW = (7, 7)
        SH, SW = (3, 3)
        PH, PW = (3, 3)
        C_IN = KH * KW * CHANNEL

        def unfold(x, kh, kw, sh, sw, ph, pw):
            B, C, H, W = x.shape
            xp = jnp.pad(x, ((0, 0), (0, 0), (ph, ph), (pw, pw)))
            Ho = (H + 2 * ph - kh) // sh + 1
            Wo = (W + 2 * pw - kw) // sw + 1
            ih = (jnp.arange(Ho) * sh)[:, None] + jnp.arange(kh)[None, :]
            iw = (jnp.arange(Wo) * sw)[:, None] + jnp.arange(kw)[None, :]
            patches = xp[:, :, ih[:, None, :, None], iw[None, :, None, :]]
            patches = patches.transpose(0, 2, 3, 1, 4, 5)
            return patches.reshape(B, Ho * Wo, C * kh * kw)
        feat = unfold(x, KH, KW, SH, SW, PH, PW)
        feat = jnp.einsum('blc,hc->blh', feat, W) + b
        return feat

    def _L0_attn_ref(x, conv_dw_w, conv_dw_b, conv_pw_w, conv_pw_b, ln1_g, ln1_b, f_w, ln2_g, ln2_b, mlp_w1, mlp_b1, mlp_w2, mlp_b2):
        import jax, jax.numpy as jnp
        import numpy as np
        LN_EPS = 1e-05
        LOG_HALF = float(np.log(0.5))

        def log_g(x):
            return jnp.where(x >= 0, jnp.log(jax.nn.relu(x) + 0.5), -jax.nn.softplus(-x))

        def layernorm(x, g, b):
            mu = jnp.mean(x, axis=-1, keepdims=True)
            var = jnp.mean(jnp.square(x - mu), axis=-1, keepdims=True)
            return (x - mu) * jax.lax.rsqrt(var + LN_EPS) * g + b

        def causal_conv(x, dw_w, dw_b, pw_w, pw_b):
            B, T, D = x.shape
            K = dw_w.shape[0]
            xp = jnp.pad(x, ((0, 0), (K - 1, 0), (0, 0)))
            y = dw_b
            for j in range(K):
                y = y + xp[:, j:j + T, :] * dw_w[j]
            return jnp.einsum('btd,ed->bte', y, pw_w) + pw_b

        def min_gru(x, fw):
            B, T, D = x.shape
            kh = jnp.einsum('btd,ed->bte', x, fw)
            k, h_x = (kh[..., :D], kh[..., D:])
            log_z = -jax.nn.softplus(-k)
            log_coeffs = -jax.nn.softplus(k)
            log_h0 = jnp.full((B, 1, D), LOG_HALF, dtype=x.dtype)
            log_values = jnp.concatenate([log_h0, log_g(h_x) + log_z], axis=1)
            a_star = jnp.pad(jnp.cumsum(log_coeffs, axis=1), ((0, 0), (1, 0), (0, 0)))
            log_h = a_star + jax.lax.cumlogsumexp(log_values - a_star, axis=1)
            return jnp.exp(log_h)[:, 1:]

        def mlp(x, w1, b1, w2, b2):
            h = jax.nn.relu(jnp.einsum('btd,ed->bte', x, w1) + b1)
            return jnp.einsum('bte,de->btd', h, w2) + b2
        L = conv_dw_w.shape[0]
        x = causal_conv(x, conv_dw_w[0], conv_dw_b[0], conv_pw_w[0], conv_pw_b[0])
        x = layernorm(x, ln1_g, ln1_b)
        x = min_gru(x, f_w[0]) + x
        for i in range(L - 1):
            x = layernorm(x, ln2_g[i], ln2_b[i])
            x = mlp(x, mlp_w1[i], mlp_b1[i], mlp_w2[i], mlp_b2[i])
            x = causal_conv(x, conv_dw_w[i + 1], conv_dw_b[i + 1], conv_pw_w[i + 1], conv_pw_b[i + 1])
            x = min_gru(x, f_w[i + 1]) + x
        x = layernorm(x, ln2_g[L - 1], ln2_b[L - 1])
        x = mlp(x, mlp_w1[L - 1], mlp_b1[L - 1], mlp_w2[L - 1], mlp_b2[L - 1])
        return x

    def _L0_ffn_ref(x, gate_w, biases, w1, w3, w2, sw1, sw3, sw2):
        import jax, jax.numpy as jnp
        import numpy as np
        DIM = 128
        HID = 256
        E = 8
        K = 2
        B, S = (4, 512)
        Bb, Ss, D = x.shape
        xt = x.reshape(Bb * Ss, D)
        shared = jax.nn.silu(xt @ sw1) * (xt @ sw3) @ sw2
        scores = xt @ gate_w.T
        _, idx = jax.lax.top_k(scores + biases, K)
        topv, _ = jax.lax.top_k(scores, K)
        p = jax.nn.sigmoid(topv)
        p = p / jnp.sum(p, axis=-1, keepdims=True)
        h = jax.nn.silu(jnp.einsum('td,edh->eth', xt, w1)) * jnp.einsum('td,edh->eth', xt, w3)
        y = jnp.einsum('eth,ehd->etd', h, w2)
        onehot = jax.nn.one_hot(idx, E, dtype=xt.dtype)
        comb = jnp.einsum('tk,tke->te', p, onehot)
        out = jnp.einsum('te,etd->td', comb, y) + shared
        return out.reshape(Bb, Ss, D)
    h = _L0_tok_ref(x, L0_tok_W, L0_tok_b)
    h = jnp.concatenate([h, txt], axis=1)
    h = h + _L0_attn_ref(_layernorm(h, axis=-1), L0_attn_conv_dw_w, L0_attn_conv_dw_b, L0_attn_conv_pw_w, L0_attn_conv_pw_b, L0_attn_ln1_g, L0_attn_ln1_b, L0_attn_f_w, L0_attn_ln2_g, L0_attn_ln2_b, L0_attn_mlp_w1, L0_attn_mlp_b1, L0_attn_mlp_w2, L0_attn_mlp_b2)
    h = h + _L0_ffn_ref(_layernorm(h, axis=-1), L0_ffn_gate_w, L0_ffn_biases, L0_ffn_w1, L0_ffn_w3, L0_ffn_w2, L0_ffn_sw1, L0_ffn_sw3, L0_ffn_sw2)
    return h

_drawn_inputs = setup_inputs


def setup_inputs(seed=0):
    import zlib

    import numpy as np

    out = dict(_drawn_inputs(seed))
    spreads = {'L0_attn_conv_dw_b': (0.0, 0.1),
     'L0_attn_conv_pw_b': (0.0, 0.1),
     'L0_attn_ln1_g': (1.0, 0.6),
     'L0_attn_ln1_b': (0.0, 0.8),
     'L0_attn_ln2_g': (1.0, 0.2),
     'L0_attn_ln2_b': (0.0, 0.1),
     'L0_attn_mlp_b1': (0.0, 0.1),
     'L0_attn_mlp_b2': (0.0, 0.1),
     'L0_ffn_biases': (0.0, 0.1)}
    factors = {'L0_attn_conv_dw_w': 4.811}
    for name, (base, spread) in spreads.items():
        noise = np.random.default_rng([zlib.crc32(name.encode()), seed]).standard_normal(out[name].shape)
        drawn = base * np.exp(spread * noise) if base else spread * noise
        out[name] = jnp.asarray(drawn.astype(out[name].dtype))
    for name, factor in factors.items():
        out[name] = (out[name] * factor).astype(out[name].dtype)
    return out
```

```python
from contextlib import ExitStack

import concourse.bass as bass
from concourse import mybir

F32 = mybir.dt.float32
F32R = mybir.dt.float32r
I32 = mybir.dt.int32
U32 = mybir.dt.uint32
ALU = mybir.AluOpType
ACT = mybir.ActivationFunctionType

NB, D = 16, 128
HIN, WIN = 60, 108
KSZ, STR, PAD = 7, 3, 3
HO, WO = 20, 36
TXT = 128
NIMG = HO * WO
S = NIMG + TXT
LAYERS, TAPS = 4, 4
HID = 512
HT = HID // D
NE, MH = 8, 256
EPS = 1e-5
RSQRT_SEED = 0x5F3759DF

NH = 2
ROWS_OUT = HO // NH
NHALF = ROWS_OUT * WO
ROWS_PAD = STR * (ROWS_OUT - 1) + KSZ
QW = WO + 2
HALF_IN = [(max(0, STR * ROWS_OUT * h - PAD), min(HIN, STR * ROWS_OUT * h - PAD + ROWS_PAD)) for h in range(NH)]
HALF_AT = [lo - (STR * ROWS_OUT * h - PAD) for h, (lo, _) in enumerate(HALF_IN)]

NCH = 2
CH = S // NCH
G = 106
NG = S // G
GC = CH // G
BANK = 512


def conv_phase(nc, sems, tok, x, txt, tok_w, tok_b):
    ntap = KSZ * KSZ
    wcut = [0, 25, ntap]
    with ExitStack() as mem:
        def sb(name, shape, dt=F32):
            return mem.enter_context(nc.sbuf_tensor(name, shape, dt))

        w_hi = sb("w_hi", [D, ntap, D], F32R)
        w_lo = sb("w_lo", [D, ntap, D], F32R)
        bias = sb("tok_bias", [D, 1])
        stage = [sb(f"x_stage{h}", [D, 33 * WIN]) for h in range(NH)]
        x_hi = [sb(f"x_hi{h}", [D, ROWS_PAD, STR, QW], F32R) for h in range(NH)]
        x_lo = [sb(f"x_lo{h}", [D, ROWS_PAD, STR, QW], F32R) for h in range(NH)]
        conv = [mem.enter_context(nc.psum_tensor(f"conv{h}", [D, BANK], F32)) for h in range(NH)]

        w_in = sems("w_in")
        small_in = sems("conv_small_in")
        x_in = [sems(f"x_in{h}") for h in range(NH)]
        w_hi_done = sems("w_hi_done")
        zeroed = sems("pads_zeroed")
        hi_done = [sems(f"x_hi_done{h}") for h in range(NH)]
        lo_done = [sems(f"x_lo_done{h}") for h in range(NH)]
        conv_done = [sems(f"conv_done{h}") for h in range(NH)]
        evac_done = [sems(f"conv_evacuated{h}") for h in range(NH)]

        nrow = [hi - lo for lo, hi in HALF_IN]
        cuts = [[n * k // 3 for k in range(4)] for n in nrow]

        def staged(h, a, b):
            return stage[h][:, a * WIN:b * WIN].rearrange("p (r s q) -> p r s q", s=STR, q=WO)

        def padded(buf, h, a, b):
            return buf[h][:, HALF_AT[h] + a:HALF_AT[h] + b, :, 1:1 + WO]

        with nc.Block() as block:
            @block.sync
            def _(sp):
                for k in range(2):
                    n = (wcut[k + 1] - wcut[k]) * D
                    sp.dma_start(stage[k][:, 0:n], tok_w[:, wcut[k] * D:wcut[k + 1] * D]).then_inc(w_in, 16)
                sp.dma_start(bias[:], tok_b).then_inc(small_in, 16)
                sp.dma_start(tok[:, :, NIMG:S], txt).then_inc(small_in, 16)
                with sp.Fori(0, NB) as b:
                    for h in range(NH):
                        sp.wait_ge(lo_done[h], b * 3 + 1)
                        r0, r1 = HALF_IN[h]
                        sp.dma_start(stage[h][:, 0:(r1 - r0) * WIN],
                                     x[bass.ds(b, 1), :, r0 * WIN:r1 * WIN].rearrange("o p n -> p (o n)")
                                     ).then_inc(x_in[h], 16)
                sp.wait_ge(small_in, 32)

            @block.gpsimd
            def _(pool):
                for h in range(NH):
                    nc.gpsimd.memset(x_hi[h][:].bitcast(F32), 0.0).then_inc(zeroed, 1)
                    nc.gpsimd.memset(x_lo[h][:].bitcast(F32), 0.0).then_inc(zeroed, 1)

            @block.scalar
            def _(act):
                for k in range(2):
                    act.wait_ge(w_in, 32)
                    n = (wcut[k + 1] - wcut[k]) * D
                    dst = w_hi[:, wcut[k]:wcut[k + 1], :].rearrange("p t c -> p (t c)")
                    nc.scalar.activation(dst, stage[k][:, 0:n], ACT.Copy).then_inc(w_hi_done, 1)

                def split_hi(h, b):
                    act.wait_ge(x_in[h], b * 16 + 16)
                    act.wait_ge(conv_done[h], b)
                    for k in range(3):
                        r0, r1 = cuts[h][k:k + 2]
                        nc.scalar.activation(padded(x_hi, h, r0, r1), staged(h, r0, r1),
                                             ACT.Copy).then_inc(hi_done[h], 1)

                def evacuate(h, b):
                    act.wait_ge(conv_done[h], b + 1)
                    nc.scalar.activation(tok[:, bass.ds(b, 1), h * NHALF:(h + 1) * NHALF].rearrange("p o n -> p (o n)"),
                                         conv[h][:, 0:NHALF], ACT.Identity, bias=bias[:, 0:1]).then_inc(evac_done[h], 1)

                act.wait_ge(small_in, 32)
                act.wait_ge(zeroed, 2 * NH)
                for h in range(NH):
                    act.sem_inc(evac_done[h], 1)
                for h in range(NH):
                    split_hi(h, 0)
                with act.Fori(0, NB - 1) as b:
                    for h in range(NH):
                        evacuate(h, b)
                        split_hi(h, b + 1)
                for h in range(NH):
                    evacuate(h, NB - 1)

            @block.vector
            def _(dve):
                for k in range(2):
                    dve.wait_ge(w_hi_done, k + 1)
                    n = (wcut[k + 1] - wcut[k]) * D
                    hi = w_hi[:, wcut[k]:wcut[k + 1], :].rearrange("p t c -> p (t c)")
                    lo = w_lo[:, wcut[k]:wcut[k + 1], :].rearrange("p t c -> p (t c)")
                    nc.vector.tensor_tensor(lo, stage[k][:, 0:n], hi.bitcast(F32), ALU.subtract).then_inc(lo_done[k], 1)
                dve.wait_ge(zeroed, 2 * NH)
                with dve.Fori(0, NB) as b:
                    for h in range(NH):
                        for k in range(3):
                            r0, r1 = cuts[h][k:k + 2]
                            dve.wait_ge(hi_done[h], b * 3 + k + 1)
                            nc.vector.tensor_tensor(padded(x_lo, h, r0, r1), staged(h, r0, r1),
                                                    padded(x_hi, h, r0, r1).bitcast(F32),
                                                    ALU.subtract).then_inc(lo_done[h], 1)

            @block.tensor
            def _(pe):
                for h in range(NH):
                    pe.wait_ge(lo_done[h], 1)
                with pe.Fori(0, NB) as b:
                    for h in range(NH):
                        pe.wait_ge(lo_done[h], b * 3 + 4)
                        pe.wait_ge(evac_done[h], b + 1)
                        for kh in range(KSZ):
                            for kw in range(KSZ):
                                t = kh * KSZ + kw
                                q, phase = divmod(kw - PAD, STR)
                                rows = slice(kh, kh + STR * (ROWS_OUT - 1) + 1, STR)
                                cols = slice(q + 1, q + 1 + WO)
                                hi, lo = x_hi[h][:, rows, phase, cols], x_lo[h][:, rows, phase, cols]
                                out = conv[h][:, 0:NHALF]
                                nc.tensor.matmul(out, w_hi[:, t, :], hi, start=(t == 0), stop=False)
                                nc.tensor.matmul(out, w_hi[:, t, :], lo, start=False, stop=False)
                                mm = nc.tensor.matmul(out, w_lo[:, t, :], hi, start=False, stop=(t == ntap - 1))
                        mm.then_inc(conv_done[h], 1)


NLN = 2 + LAYERS
COST = {"center": 0.72, "var": 0.36, "turn": 0.1, "spread": 0.36, "pw": 0.54, "kh": 1.08, "up": 0.54, "down": 0.71,
        "newton": 0.08, "pack_hi": 0.08, "pack_lo": 0.08, "taps": 3.1, "turned": 0.18,
        "act": 0.45, "dve": 0.52, "pool": 1.1}
HOP = 0.2


def mixer_steps():
    out, index, done, free = [], {}, {}, {}

    def step(engine, kind, after, i=0, n=0, c=0, j=0):
        what = (kind, i, n, c, j)
        cost = COST[kind] if kind in COST else COST[engine]
        start = max([free.get(engine, 0.0)] + [done[a] + HOP for a in after])
        free[engine] = done[what] = start + cost
        index[what] = len(out)
        out.append((engine, what, [index[a] for a in after], cost, start))
        return what

    def norm(i, n, centered):
        sq = [step("act", "square", [centered[c]], i, n, c) for c in range(NCH)]
        for c in range(NCH):
            var = step("pe", "var", [sq[c]], i, n, c)
        v = step("dve", "newton", [var], i, n, 0, 0)
        for k in range(1, NEWTON):
            v = step("dve", "newton", [v], i, n, 0, k)
        v = step("dve", "pack_lo", [step("dve", "pack_hi", [v], i, n)], i, n)
        t = step("dve", "turned", [step("pe", "turn", [v], i, n)], i, n)
        inv = [step("act", "inv", [step("pe", "spread", [t], i, n, c)], i, n, c) for c in range(NCH)]
        return [step("dve", "normed", [inv[c]], i, n, c) for c in range(NCH)]

    hi = [step("act", "split_hi", [], c=c) for c in range(NCH)]
    lo = [step("dve", "split_lo", [hi[c]], c=c) for c in range(NCH)]
    m = norm(0, 0, [step("pe", "center", [lo[c]], 0, 0, c) for c in range(NCH)])
    for i in range(LAYERS):
        y0 = [step("act", "y0", [m[c]], i, c=c) for c in range(NCH)]
        taps = step("dve", "taps", y0, i)
        hi = [step("act", "y_hi", [taps], i, c=c) for c in range(NCH)]
        lo = [step("dve", "y_lo", [hi[c]], i, c=c) for c in range(NCH)]
        pw = [step("pe", "pw", [lo[c]], i, c=c) for c in range(NCH)]
        if i == 0:
            xn = norm(0, 1, pw)
            hi = [step("act", "n_hi", [xn[c]], 0, 1, c) for c in range(NCH)]
            lo = [step("dve", "x1_lo", [hi[c]], 0, 1, c) for c in range(NCH)]
        else:
            hi = [step("act", "x_hi", [pw[c]], i, c=c) for c in range(NCH)]
            lo = [step("dve", "x_lo", [hi[c]], i, c=c) for c in range(NCH)]
        kh = [step("pe", "kh", [lo[c]], i, c=c) for c in range(NCH)]
        scan = []
        for c in range(NCH):
            cand = step("dve", "cand", [step("act", "g_cand", [kh[c]], i, c=c)], i, c=c)
            take = step("dve", "take", [step("act", "g_take", [kh[c]], i, c=c), cand], i, c=c)
            scan.append(step("dve", "scan", [step("act", "g_keep", [kh[c]], i, c=c), take], i, c=c))
        hi = [step("act", "s_hi", [scan[c]], i, c=c) for c in range(NCH)]
        lo = [step("dve", "s_lo", [hi[c]], i, c=c) for c in range(NCH)]
        xn = norm(i, 2 + i, [step("pe", "center", [lo[c]], i, 2 + i, c) for c in range(NCH)])
        hi = [step("act", "n_hi", [xn[c]], i, 2 + i, c) for c in range(NCH)]
        lo = [step("pool", "n_lo", [hi[c]], i, 2 + i, c) for c in range(NCH)]
        tiles = [(c, j) for c in range(NCH) for j in range(HT)]
        relu = {}
        for q in range(len(tiles) + 2):
            if q >= 2:
                c, j = tiles[q - 2]
                down = step("pe", "down", [relu[c, j]], i, c=c, j=j)
                if j == HT - 1:
                    m_c = step(*(("act", "out") if i < LAYERS - 1 else ("dve", "final")), [down], i, c=c)
                    m = [m_c] if c == 0 else m + [m_c]
            if q < len(tiles):
                c, j = tiles[q]
                relu[c, j] = step("dve" if j % 2 else "act", "relu", [step("pe", "up", [lo[c]], i, c=c, j=j)], i, c=c, j=j)
    return out


def two_streams():
    steps = mixer_steps()
    busy, reached, ends, placed = {}, {}, {}, {}
    for _, s, k in sorted((st[4] + LAG * s, s, k) for k, st in enumerate(steps) for s in range(2)):
        engine, what, after, cost, _ = steps[k]
        t = max([LAG * s, reached.get((s, engine), 0.0)] + [ends[s, a] + HOP for a in after])
        moved = True
        while moved:
            moved = False
            for b0, b1 in busy.setdefault(engine, []):
                for turn in (-PERIOD, 0.0, PERIOD):
                    at = t % PERIOD
                    if at < b1 + turn - 1e-9 and at + cost > b0 + turn + 1e-9:
                        t += b1 + turn - at
                        moved = True
        busy[engine].append((t % PERIOD, t % PERIOD + cost))
        ends[s, k] = reached[s, engine] = t + cost
        placed.setdefault(engine, []).append((t % PERIOD, s, t >= PERIOD, what))
    assert all(ends[s, k] <= PERIOD + LAG * s for s, k in ends)
    return {e: [x[1:] for x in sorted(v)] for e, v in placed.items()}


def run_pairs(order, fori, do):
    for s, wraps, what in order:
        if not wraps:
            do(s, 0, *what)
    with fori(1, NB // 2) as it:
        for s, wraps, what in order:
            do(s, it - 1 if wraps else it, *what)
    for s, wraps, what in order:
        if wraps:
            do(s, NB // 2 - 1, *what)


PERIOD, LAG = 217.9, 8.0
NEWTON = 11


def rsqrt_step(eng, k, var, small):
    v, y, t = small
    if k == 0:
        return eng.tensor_scalar(v[:], var, EPS, None, ALU.add)
    if k == 1:
        return eng.tensor_scalar(y[:].bitcast(I32), v[:].bitcast(I32), -0.5, float(RSQRT_SEED), ALU.mult, ALU.add)
    k = (k - 2) % 3
    if k == 0:
        return eng.tensor_tensor(t[:], y[:], y[:], ALU.mult)
    if k == 1:
        return eng.scalar_tensor_tensor(out=t[:], in0=t[:], scalar=-0.5, in1=v[:], op0=ALU.mult, op1=ALU.mult)
    return eng.scalar_tensor_tensor(out=y[:], in0=t[:], scalar=1.5, in1=y[:], op0=ALU.add, op1=ALU.mult)


def mixer_phase(nc, sems, tok, p):
    order = two_streams()
    with ExitStack() as mem:
        def sb(name, shape, dt=F32):
            return mem.enter_context(nc.sbuf_tensor(name, shape, dt))

        pw_hi, pw_lo = sb("pw_hi", [D, LAYERS, D], F32R), sb("pw_lo", [D, LAYERS, D], F32R)
        f_hi, f_lo = sb("f_hi", [D, LAYERS, 2 * D], F32R), sb("f_lo", [D, LAYERS, 2 * D], F32R)
        w1_hi, w1_lo = sb("w1_hi", [D, LAYERS, HID], F32R), sb("w1_lo", [D, LAYERS, HID], F32R)
        w2 = sb("w2", [D, LAYERS, HT, D])
        cen32, cen = sb("cen32", [D, D]), sb("cen", [D, D], F32R)
        mean1 = sb("mean1", [D, 1])
        ident = sb("ident", [D, D])
        sel = sb("sel", [40, NG, D], F32R)
        dw, dwb = sb("dw", [D, LAYERS, TAPS]), sb("dwb", [D, LAYERS])
        pwb, pwb_c = sb("pwb", [D, LAYERS]), sb("pwb_c", [D, 1])
        ln1g, ln1b = sb("ln1g", [D, 1]), sb("ln1b", [D, 1])
        ln2g, ln2b = sb("ln2g", [D, LAYERS]), sb("ln2b", [D, LAYERS])
        b1, b1f = sb("b1", [D, LAYERS * HT]), sb("b1f", [D, LAYERS * HT])
        b2 = sb("b2", [D, LAYERS])

        psum = [[mem.enter_context(nc.psum_tensor(f"ps{s}_{k}", [D, BANK], F32)) for k in range(4)] for s in range(2)]

        with ExitStack() as tmp:
            def sbt(name, shape, dt=F32):
                return tmp.enter_context(nc.sbuf_tensor(name, shape, dt))

            pw32, pw0n = sbt("pw32", [D, LAYERS, D]), sbt("pw0n", [D, D])
            f32, w132 = sbt("f32", [D, LAYERS, 2 * D]), sbt("w132", [D, LAYERS, HID])
            sel32 = sbt("sel32", [40, NG, D])
            loads = [(pw32, "pw"), (pw0n, "pw0n"), (f32, "f"), (w132, "w1"), (w2, "w2"), (cen32, "cen"),
                     (mean1, "mean1"), (ident, "ident"), (sel32, "sel"), (dw, "dw"), (dwb, "dwb"), (pwb, "pwb"),
                     (ln1g, "ln1g"), (ln1b, "ln1b"), (ln2g, "ln2g"), (ln2b, "ln2b"), (b1, "b1"), (b2, "b2")]
            loaded = sems("mixer_weights_in")
            folded = sems("mixer_folded_psum")
            hi_done = sems("mixer_w_hi")
            with nc.Block() as block:
                @block.sync
                def _(sp):
                    for dst, name in loads:
                        sp.dma_start(dst[:], p[name]).then_inc(loaded, 16)

                @block.tensor
                def _(pe):
                    pe.wait_ge(loaded, 16 * len(loads))
                    nc.tensor.matmul(psum[0][0][:, 0:D], pw0n[:], cen32[:], start=True, stop=True)
                    nc.tensor.matmul(psum[0][1][:, 0:1], cen32[:], pwb[:, 0:1], start=True, stop=True)
                    for i in range(LAYERS):
                        for j in range(HT):
                            mm = nc.tensor.matmul(psum[0][2][:, i * HT + j:i * HT + j + 1],
                                                  w132[:, i, j * D:(j + 1) * D], ln2b[:, i:i + 1], start=True, stop=True)
                    mm.then_inc(folded, 1)

                @block.scalar
                def _(act):
                    act.wait_ge(loaded, 16 * len(loads))
                    nc.scalar.activation(cen[:], cen32[:], ACT.Copy)
                    nc.scalar.activation(sel[:], sel32[:], ACT.Copy)
                    nc.scalar.activation(pw_hi[:, 1:LAYERS, :], pw32[:, 1:LAYERS, :], ACT.Copy)
                    nc.scalar.activation(f_hi[:], f32[:], ACT.Copy)
                    for i in range(LAYERS):
                        nc.scalar.activation(w1_hi[:, i, :], w132[:, i, :], ACT.Copy, scale=ln2g[:, i:i + 1])
                    act.wait_ge(folded, 1)
                    nc.scalar.activation(pw_hi[:, 0, :], psum[0][0][:, 0:D], ACT.Copy)
                    nc.scalar.activation(pwb_c[:], psum[0][1][:, 0:1], ACT.Copy).then_inc(hi_done, 1)

                @block.vector
                def _(dve):
                    dve.wait_ge(hi_done, 1)
                    nc.vector.tensor_tensor(pw_lo[:, 1:LAYERS, :], pw32[:, 1:LAYERS, :],
                                            pw_hi[:, 1:LAYERS, :].bitcast(F32), ALU.subtract)
                    nc.vector.tensor_tensor(f_lo[:], f32[:], f_hi[:].bitcast(F32), ALU.subtract)
                    for i in range(LAYERS):
                        nc.vector.scalar_tensor_tensor(out=w1_lo[:, i, :], in0=w132[:, i, :], scalar=ln2g[:, i:i + 1],
                                                       in1=w1_hi[:, i, :].bitcast(F32), op0=ALU.mult, op1=ALU.subtract)
                    nc.vector.tensor_tensor(pw_lo[:, 0, :], psum[0][0][:, 0:D], pw_hi[:, 0, :].bitcast(F32), ALU.subtract)
                    nc.vector.tensor_tensor(b1f[:], psum[0][2][:, 0:LAYERS * HT], b1[:], ALU.add)

        class Stream:
            pass

        streams = []
        for s in range(2):
            w = Stream()
            w.m = sb(f"m{s}", [D, TAPS - 1 + S])
            w.y = sb(f"y{s}", [D, S])
            w.y_hi, w.y_lo = sb(f"y_hi{s}", [D, S], F32R), sb(f"y_lo{s}", [D, S], F32R)
            w.x_hi, w.x_lo = sb(f"xx_hi{s}", [D, S], F32R), sb(f"xx_lo{s}", [D, S], F32R)
            w.keep = sb(f"keep{s}", [D, S])
            w.take = sb(f"take{s}", [D, S])
            w.cand = sb(f"cand{s}", [D, S])
            w.hid = sb(f"hid{s}", [D, HT, CH])
            w.small = [sb(f"rs{k}_{s}", [G, NG]) for k in range(3)]
            w.packed = sb(f"packed{s}", [G, D], F32R)
            w.turned = sb(f"turned{s}", [40, G], F32R)
            w.bank = psum[s]
            w.split_hi = sems(f"s{s}_split_hi")
            w.split_lo = sems(f"s{s}_split_lo")
            w.centered = sems(f"s{s}_centered")
            w.squared = sems(f"s{s}_squared")
            w.var = sems(f"s{s}_var")
            w.newton = sems(f"s{s}_newton")
            w.packed_done = sems(f"s{s}_packed")
            w.turned_ps = sems(f"s{s}_turned_psum")
            w.turned_done = sems(f"s{s}_turned")
            w.spread = sems(f"s{s}_spread")
            w.spread_done = sems(f"s{s}_spread_copied")
            w.m_norm = sems(f"s{s}_input_normed")
            w.normed = sems(f"s{s}_normed")
            w.n_hi = sems(f"s{s}_normed_hi")
            w.n_lo = sems(f"s{s}_normed_lo")
            w.dw0 = sems(f"s{s}_dw_first")
            w.dw = sems(f"s{s}_dw_taps")
            w.y_hi_done = sems(f"s{s}_y_hi")
            w.y_lo_done = sems(f"s{s}_y_lo")
            w.pw = sems(f"s{s}_pointwise")
            w.x_hi_done = sems(f"s{s}_x_hi")
            w.x_lo_done = sems(f"s{s}_x_lo")
            w.kh = sems(f"s{s}_kh")
            w.gates = sems(f"s{s}_gates")
            w.cand_done = sems(f"s{s}_candidate")
            w.take_done = sems(f"s{s}_taken")
            w.scan = sems(f"s{s}_scan")
            w.s_hi = sems(f"s{s}_scan_hi")
            w.s_lo = sems(f"s{s}_scan_lo")
            w.up = sems(f"s{s}_mlp_up")
            w.relu_a = sems(f"s{s}_relu_act")
            w.relu_v = sems(f"s{s}_relu_dve")
            w.down = sems(f"s{s}_mlp_down")
            w.m_done = sems(f"s{s}_mlp_out")
            w.tok_done = sems(f"s{s}_tok_updated")
            streams.append(w)
        pads = sems("mixer_pads")

        CUT = [slice(c * CH, (c + 1) * CH) for c in range(NCH)]
        M = [slice(TAPS - 1 + c * CH, TAPS - 1 + (c + 1) * CH) for c in range(NCH)]
        NL, NN = 2 * LAYERS, 2 * NLN

        def tok_chunk(it, s, c):
            return tok[:, bass.ds(it * 2 + s, 1), c * CH:(c + 1) * CH].rearrange("p o n -> p (o n)")

        def newton(eng, w, it, n, k):
            if k == 0:
                eng.wait_ge(w.var, it * NN + 2 * n + 2)
            else:
                eng.wait_ge(w.newton, it * (NEWTON * NLN) + n * NEWTON + k)
            rsqrt_step(eng, k, w.bank[2][0:G, 0:NG], w.small).then_inc(w.newton, 1)

        def pack(eng, w, it, n, lo):
            if not lo:
                eng.wait_ge(w.newton, it * (NEWTON * NLN) + n * NEWTON + NEWTON)
                eng.tensor_copy(w.packed[:, 0:NG], w.small[1][:]).then_inc(w.packed_done, 1)
            else:
                eng.wait_ge(w.packed_done, it * NN + 2 * n + 1)
                eng.tensor_tensor(w.packed[:, 32:32 + NG], w.small[1][:], w.packed[:, 0:NG].bitcast(F32), ALU.subtract
                                  ).then_inc(w.packed_done, 1)

        with nc.Block() as block:
            @block.gpsimd
            def _(pool):
                for w in streams:
                    nc.gpsimd.memset(w.m[:, 0:TAPS - 1], 0.0).then_inc(pads, 1)
                    nc.gpsimd.memset(w.packed[:].bitcast(F32), 0.0).then_inc(pads, 1)

                def do(s, it, kind, i, n, c, j):
                    w = streams[s]
                    pool.wait_ge(w.n_hi, it * NL + 2 * i + c + 1)
                    nc.gpsimd.tensor_tensor(w.x_lo[:, CUT[c]], w.cand[:, CUT[c]], w.x_hi[:, CUT[c]].bitcast(F32),
                                            ALU.subtract).then_inc(w.n_lo, 1)

                run_pairs(order["pool"], pool.Fori, do)

            @block.tensor
            def _(pe):
                def three(out, w_hi, w_lo, hi, lo):
                    nc.tensor.matmul(out, w_hi, hi, start=True, stop=False)
                    nc.tensor.matmul(out, w_hi, lo, start=False, stop=False)
                    return nc.tensor.matmul(out, w_lo, hi, start=False, stop=True)

                def do(s, it, kind, i, n, c, j):
                    w = streams[s]
                    e = it * NL + 2 * i + c
                    bank = w.bank[c][:, 0:CH]
                    if kind == "center":
                        if n == 0:
                            pe.wait_ge(w.split_lo, it * 2 + c + 1)
                            parts = [w.y_hi, w.y_lo]
                        else:
                            pe.wait_ge(w.s_lo, e + 1)
                            parts = [w.y_hi, w.y_lo, w.x_hi, w.x_lo]
                        for k, part in enumerate(parts):
                            mm = nc.tensor.matmul(bank, cen[:], part[:, CUT[c]], start=(k == 0), stop=(k == len(parts) - 1))
                        mm.then_inc(w.centered, 1)
                    elif kind == "var":
                        pe.wait_ge(w.squared, it * NN + 2 * n + c + 1)
                        for g in range(c * GC, (c + 1) * GC):
                            mm = nc.tensor.matmul(w.bank[2][0:G, g:g + 1], w.keep[:, g * G:(g + 1) * G], mean1[:],
                                                  start=True, stop=True)
                        mm.then_inc(w.var, 1)
                    elif kind == "turn":
                        pe.wait_ge(w.packed_done, it * NN + 2 * n + 2)
                        nc.tensor.matmul(w.bank[3][:, 0:G], w.packed[:].bitcast(F32), ident[0:G, 0:G], is_transpose=True,
                                         start=True, stop=True).then_inc(w.turned_ps, 1)
                    elif kind == "spread":
                        if c == 0:
                            pe.wait_ge(w.turned_done, it * NLN + n + 1)
                        for g in range(GC):
                            mm = nc.tensor.matmul(w.bank[2 + c][:, g * G:(g + 1) * G], sel[:, c * GC + g, :], w.turned[:],
                                                  start=True, stop=True)
                        mm.then_inc(w.spread, 1)
                    elif kind == "pw":
                        pe.wait_ge(w.y_lo_done, e + 1)
                        mm = three(bank, pw_hi[:, i, :], pw_lo[:, i, :], w.y_hi[:, CUT[c]], w.y_lo[:, CUT[c]])
                        mm.then_inc(w.centered if i == 0 else w.pw, 1)
                    elif kind == "kh":
                        pe.wait_ge(w.x_hi_done, e + 1)
                        pe.wait_ge(w.x_lo_done, e + 1)
                        for out, cols in ((w.bank[2 + c][:, 0:CH], slice(0, D)), (bank, slice(D, 2 * D))):
                            mm = three(out, f_hi[:, i, cols], f_lo[:, i, cols], w.x_hi[:, CUT[c]], w.x_lo[:, CUT[c]])
                        mm.then_inc(w.kh, 1)
                    elif kind == "up":
                        if j == 0:
                            pe.wait_ge(w.n_lo, e + 1)
                        if c == 0 and j == 1:
                            pe.wait_ge(w.spread_done, it * NN + 2 * (2 + i) + 2)
                        cols = slice(j * D, (j + 1) * D)
                        three(w.bank[2 + j % 2][:, 0:CH], w1_hi[:, i, cols], w1_lo[:, i, cols], w.x_hi[:, CUT[c]],
                              w.x_lo[:, CUT[c]]).then_inc(w.up, 1)
                    elif kind == "down":
                        pe.wait_ge(w.relu_v if j % 2 else w.relu_a, e * (HT // 2) + j // 2 + 1)
                        mm = nc.tensor.matmul(bank, w2[:, i, j, :], w.hid[:, j, :], start=(j == 0), stop=(j == HT - 1))
                        if j == HT - 1:
                            mm.then_inc(w.down, 1)

                pe.wait_ge(pads, 4)
                run_pairs(order["pe"], pe.Fori, do)

            @block.scalar
            def _(act):
                def do(s, it, kind, i, n, c, j):
                    w = streams[s]
                    e, en = it * NL + 2 * i + c, it * NN + 2 * n + c
                    bank, kbank = w.bank[c][:, 0:CH], w.bank[2 + c][:, 0:CH]
                    op = nc.scalar.activation
                    if kind == "split_hi":
                        op(w.y_hi[:, CUT[c]], tok_chunk(it, s, c), ACT.Copy).then_inc(w.split_hi, 1)
                    elif kind == "square":
                        act.wait_ge(w.centered, en + 1)
                        op(w.keep[:, CUT[c]], bank, ACT.Square, bias=pwb_c[:, 0:1] if n == 1 else 0.0).then_inc(w.squared, 1)
                    elif kind == "inv":
                        act.wait_ge(w.spread, en + 1)
                        op(w.take[:, CUT[c]], kbank, ACT.Copy, scale=ln1g[:, 0:1] if n == 1 else 1.0).then_inc(w.spread_done, 1)
                    elif kind == "n_hi" and n == 1:
                        act.wait_ge(w.normed, it * (NN - 2) + c + 1)
                        op(w.x_hi[:, CUT[c]], w.cand[:, CUT[c]], ACT.Identity, bias=ln1b[:, 0:1]).then_inc(w.x_hi_done, 1)
                    elif kind == "n_hi":
                        act.wait_ge(w.normed, it * (NN - 2) + 2 * (n - 1) + c + 1)
                        op(w.x_hi[:, CUT[c]], w.cand[:, CUT[c]], ACT.Copy).then_inc(w.n_hi, 1)
                    elif kind == "y0":
                        if i == 0:
                            act.wait_ge(w.m_norm, it * 2 + c + 1)
                        else:
                            act.wait_ge(w.m_done, it * (NL - 2) + 2 * (i - 1) + c + 1)
                        op(w.y[:, CUT[c]], w.m[:, M[c]], ACT.Identity, scale=dw[:, i, TAPS - 1:TAPS], bias=dwb[:, i:i + 1]
                           ).then_inc(w.dw0, 1)
                    elif kind == "y_hi":
                        act.wait_ge(w.dw, (it * NL + 2 * i) * 3 + 5 + c)
                        op(w.y_hi[:, CUT[c]], w.y[:, CUT[c]], ACT.Copy).then_inc(w.y_hi_done, 1)
                    elif kind == "x_hi":
                        act.wait_ge(w.pw, it * (NL - 2) + 2 * (i - 1) + c + 1)
                        op(w.x_hi[:, CUT[c]], bank, ACT.Identity, bias=pwb[:, i:i + 1]).then_inc(w.x_hi_done, 1)
                    elif kind == "g_cand":
                        act.wait_ge(w.kh, e + 1)
                        op(w.cand[:, CUT[c]], bank, ACT.Sigmoid).then_inc(w.gates, 1)
                    elif kind == "g_take":
                        op(w.take[:, CUT[c]], kbank, ACT.Sigmoid).then_inc(w.gates, 1)
                    elif kind == "g_keep":
                        op(w.keep[:, CUT[c]], kbank, ACT.Sigmoid, scale=-1.0).then_inc(w.gates, 1)
                    elif kind == "s_hi":
                        act.wait_ge(w.scan, e + 1)
                        op(w.y_hi[:, CUT[c]], w.y[:, CUT[c]], ACT.Copy).then_inc(w.s_hi, 1)
                    elif kind == "relu":
                        act.wait_ge(w.up, e * HT + j + 1)
                        op(w.hid[:, j, :], w.bank[2 + j % 2][:, 0:CH], ACT.Relu, bias=b1f[:, i * HT + j:i * HT + j + 1]
                           ).then_inc(w.relu_a, 1)
                    elif kind == "out":
                        act.wait_ge(w.down, e + 1)
                        op(w.m[:, M[c]], bank, ACT.Identity, bias=b2[:, i:i + 1]).then_inc(w.m_done, 1)

                act.wait_ge(pads, 4)
                run_pairs(order["act"], act.Fori, do)

            @block.vector
            def _(dve):
                def do(s, it, kind, i, n, c, j):
                    w = streams[s]
                    e, en = it * NL + 2 * i + c, it * NN + 2 * n + c
                    bank = w.bank[c][:, 0:CH]
                    tt, stt = nc.vector.tensor_tensor, nc.vector.scalar_tensor_tensor
                    if kind == "split_lo":
                        dve.wait_ge(w.split_hi, it * 2 + c + 1)
                        tt(w.y_lo[:, CUT[c]], tok_chunk(it, s, c), w.y_hi[:, CUT[c]].bitcast(F32), ALU.subtract
                           ).then_inc(w.split_lo, 1)
                    elif kind == "newton":
                        newton(dve, w, it, n, j)
                    elif kind in ("pack_hi", "pack_lo"):
                        pack(dve, w, it, n, kind == "pack_lo")
                    elif kind == "turned":
                        dve.wait_ge(w.turned_ps, it * NLN + n + 1)
                        nc.vector.tensor_copy(w.turned[:], w.bank[3][0:40, 0:G]).then_inc(w.turned_done, 1)
                    elif kind == "normed":
                        dve.wait_ge(w.spread_done, en + 1)
                        inv = w.take[:, CUT[c]]
                        if n == 0:
                            tt(w.m[:, M[c]], bank, inv, ALU.mult).then_inc(w.m_norm, 1)
                        elif n == 1:
                            stt(out=w.cand[:, CUT[c]], in0=bank, scalar=pwb_c[:, 0:1], in1=inv, op0=ALU.add, op1=ALU.mult
                                ).then_inc(w.normed, 1)
                        else:
                            tt(w.cand[:, CUT[c]], bank, inv, ALU.mult).then_inc(w.normed, 1)
                    elif kind == "x1_lo":
                        dve.wait_ge(w.x_hi_done, e + 1)
                        stt(out=w.x_lo[:, CUT[c]], in0=w.cand[:, CUT[c]], scalar=ln1b[:, 0:1],
                            in1=w.x_hi[:, CUT[c]].bitcast(F32), op0=ALU.add, op1=ALU.subtract).then_inc(w.x_lo_done, 1)
                    elif kind == "taps":
                        for k in range(TAPS - 1):
                            for c in range(NCH):
                                if k == 0:
                                    dve.wait_ge(w.dw0, it * NL + 2 * i + c + 1)
                                else:
                                    dve.wait_ge(w.dw, (it * NL + 2 * i) * 3 + 2 * (k - 1) + c + 1)
                                stt(out=w.y[:, CUT[c]], in0=w.m[:, c * CH + k:c * CH + k + CH], scalar=dw[:, i, k:k + 1],
                                    in1=w.y[:, CUT[c]], op0=ALU.mult, op1=ALU.add).then_inc(w.dw, 1)
                    elif kind == "y_lo":
                        dve.wait_ge(w.y_hi_done, e + 1)
                        tt(w.y_lo[:, CUT[c]], w.y[:, CUT[c]], w.y_hi[:, CUT[c]].bitcast(F32), ALU.subtract
                           ).then_inc(w.y_lo_done, 1)
                    elif kind == "x_lo":
                        dve.wait_ge(w.x_hi_done, e + 1)
                        stt(out=w.x_lo[:, CUT[c]], in0=bank, scalar=pwb[:, i:i + 1], in1=w.x_hi[:, CUT[c]].bitcast(F32),
                            op0=ALU.add, op1=ALU.subtract).then_inc(w.x_lo_done, 1)
                    elif kind == "cand":
                        dve.wait_ge(w.gates, e * 3 + 1)
                        stt(out=w.cand[:, CUT[c]], in0=bank, scalar=0.5, in1=w.cand[:, CUT[c]], op0=ALU.add, op1=ALU.max
                            ).then_inc(w.cand_done, 1)
                    elif kind == "take":
                        dve.wait_ge(w.gates, e * 3 + 2)
                        dve.wait_ge(w.cand_done, e + 1)
                        tt(w.take[:, CUT[c]], w.take[:, CUT[c]], w.cand[:, CUT[c]], ALU.mult).then_inc(w.take_done, 1)
                    elif kind == "scan":
                        dve.wait_ge(w.gates, e * 3 + 3)
                        dve.wait_ge(w.take_done, e + 1)
                        if c:
                            dve.wait_ge(w.scan, e)
                        first = 0.5 if c == 0 else w.y[:, c * CH - 1:c * CH]
                        nc.vector.tensor_tensor_scan(w.y[:, CUT[c]], w.keep[:, CUT[c]], w.take[:, CUT[c]], first, ALU.mult,
                                                     ALU.add).then_inc(w.scan, 1)
                    elif kind == "s_lo":
                        dve.wait_ge(w.s_hi, e + 1)
                        tt(w.y_lo[:, CUT[c]], w.y[:, CUT[c]], w.y_hi[:, CUT[c]].bitcast(F32), ALU.subtract
                           ).then_inc(w.s_lo, 1)
                    elif kind == "relu":
                        dve.wait_ge(w.up, e * HT + j + 1)
                        nc.vector.tensor_scalar(w.hid[:, j, :], w.bank[2 + j % 2][:, 0:CH],
                                                b1f[:, i * HT + j:i * HT + j + 1], 0.0, ALU.add, ALU.max).then_inc(w.relu_v, 1)
                    elif kind == "final":
                        dve.wait_ge(w.down, e + 1)
                        stt(out=tok_chunk(it, s, c), in0=bank, scalar=b2[:, i:i + 1], in1=tok_chunk(it, s, c), op0=ALU.add,
                            op1=ALU.add).then_inc(w.tok_done, 1)

                dve.wait_ge(pads, 4)
                run_pairs(order["dve"], dve.Fori, do)


def moe_phase(nc, sems, tok, out, p):
    NX = NE + 1
    NU, NW = NX * NCH * 2, NX * NCH
    order = [NE] + list(range(NE))
    HALVES = MH // D
    with ExitStack() as mem:
        def sb(name, shape, dt=F32):
            return mem.enter_context(nc.sbuf_tensor(name, shape, dt))

        w1_hi, w1_lo = sb("e1_hi", [D, NX, MH], F32R), sb("e1_lo", [D, NX, MH], F32R)
        w3_hi, w3_lo = sb("e3_hi", [D, NX, MH], F32R), sb("e3_lo", [D, NX, MH], F32R)
        w2 = sb("e2", [D, NX, HALVES, D])
        gate_w, gate_b = sb("gate_w", [D, NE]), sb("gate_b", [G, NG, NE])
        iota = sb("iota_e", [G, NG, NE])
        cen32, cen = sb("mcen32", [D, D]), sb("mcen", [D, D], F32R)
        mean1, ident = sb("mmean1", [D, 1]), sb("mident", [D, D])
        sel = sb("msel", [40, NG, D], F32R)
        t_hi, t_lo = sb("t_hi", [D, S], F32R), sb("t_lo", [D, S], F32R)
        t_in = sb("t_in", [D, S])
        sq, inv, xn = sb("msq", [D, S]), sb("minv", [D, S]), sb("mxn", [D, S])
        n_hi, n_lo = sb("mn_hi", [D, S], F32R), sb("mn_lo", [D, S], F32R)
        small = [sb(f"mrs{k}", [G, NG]) for k in range(3)]
        packed, turned_sb = sb("mpacked", [G, D], F32R), sb("mturned", [40, G], F32R)
        biased, raw = sb("biased", [G, NG, NE]), sb("raw", [G, NG, NE])
        top_b, top_r = sb("top_biased", [G, NG, NE]), sb("top_raw", [G, NG, NE])
        index, indexf = sb("top_index", [G, NG, NE], U32), sb("top_indexf", [G, NG, NE])
        prob, psumt, prec = sb("prob", [G, NG, 2]), sb("prob_sum", [G, NG]), sb("prob_rec", [G, NG])
        pn = sb("prob_n", [G, NG, 2])
        fence = sb("fence", [G, 2])
        comb, comb2 = sb("comb", [G, NG, NE]), sb("comb2", [G, NG, NE])
        silu = sb("silu", [D, 4, CH])
        prod = sb("prod", [D, 4, CH])
        acc = sb("acc", [G, NG, D])
        bank = [mem.enter_context(nc.psum_tensor(f"mb{k}", [D, BANK], F32)) for k in range(8)]

        s_w = sems("moe_weights_in")
        s_whi = sems("moe_w_hi")
        s_wlo = sems("moe_w_lo")
        s_in = sems("moe_t_in")
        s_thi, s_tlo = sems("moe_t_hi"), sems("moe_t_lo")
        s_cen, s_sq, s_var = sems("moe_centered"), sems("moe_squared"), sems("moe_var")
        s_newton, s_packed = sems("moe_newton"), sems("moe_packed")
        s_turnps, s_turn = sems("moe_turned_psum"), sems("moe_turned")
        s_spread, s_inv = sems("moe_spread"), sems("moe_inv")
        s_xn, s_nhi, s_nlo = sems("moe_normed"), sems("moe_n_hi"), sems("moe_n_lo")
        s_gate, s_route, s_prob = sems("moe_gate"), sems("moe_route_steps"), sems("moe_prob")
        s_up, s_silu, s_prod = sems("moe_up"), sems("moe_silu"), sems("moe_prod")
        s_down, s_comb, s_out = sems("moe_down"), sems("moe_combined"), sems("moe_out_stored")
        s_pad = sems("moe_pad")

        with ExitStack() as tmp:
            w132 = tmp.enter_context(nc.sbuf_tensor("e1_32", [D, NX, MH], F32))
            w332 = tmp.enter_context(nc.sbuf_tensor("e3_32", [D, NX, MH], F32))
            sel32 = tmp.enter_context(nc.sbuf_tensor("msel32", [40, NG, D], F32))
            loads = [(w132, "e1"), (w332, "e3"), (w2, "e2"), (gate_w, "gate_w"), (gate_b, "gate_b"), (iota, "iota"),
                     (cen32, "cen"), (mean1, "mean1"), (ident, "ident"), (sel32, "sel")]
            with nc.Block() as block:
                @block.sync
                def _(sp):
                    for dst, name in loads:
                        sp.dma_start(dst[:], p[name]).then_inc(s_w, 16)

                @block.gpsimd
                def _(pool):
                    nc.gpsimd.memset(packed[:].bitcast(F32), 0.0).then_inc(s_pad, 1)
                    pool.wait_ge(s_pad, 1)

                @block.scalar
                def _(act):
                    act.wait_ge(s_w, 16 * len(loads))
                    nc.scalar.activation(w1_hi[:], w132[:], ACT.Copy).then_inc(s_whi, 1)
                    nc.scalar.activation(w3_hi[:], w332[:], ACT.Copy).then_inc(s_whi, 1)
                    nc.scalar.activation(cen[:], cen32[:], ACT.Copy)
                    nc.scalar.activation(sel[:], sel32[:], ACT.Copy)

                @block.vector
                def _(dve):
                    dve.wait_ge(s_w, 16 * len(loads))
                    dve.wait_ge(s_whi, 1)
                    nc.vector.tensor_tensor(w1_lo[:], w132[:], w1_hi[:].bitcast(F32), ALU.subtract)
                    dve.wait_ge(s_whi, 2)
                    nc.vector.tensor_tensor(w3_lo[:], w332[:], w3_hi[:].bitcast(F32), ALU.subtract)

        CUT = [slice(c * CH, (c + 1) * CH) for c in range(NCH)]

        with nc.Block() as block:
            @block.sync
            def _(sp):
                sp.sem_inc(s_out, 16)
                with sp.Fori(0, NB) as b:
                    sp.wait_ge(s_comb, (b + 1) * NW + 1)
                    sp.dma_start(out[bass.ds(b, 1), :, :].rearrange("o (g t) d -> t (o g) d", t=G), acc[:]
                                 ).then_inc(s_out, 16)
                sp.wait_ge(s_out, 16 * NB + 16)

            @block.scalar
            def _(act):
                with act.Fori(0, NB) as b:
                    act.wait_ge(s_down, b * NW + 1)
                    nc.scalar.activation(t_in[:], tok[:, bass.ds(b, 1), :].rearrange("p o n -> p (o n)"), ACT.Copy
                                         ).then_inc(s_in, 1)
                    act.wait_ge(s_in, b + 1)
                    for c in range(NCH):
                        nc.scalar.activation(t_hi[:, CUT[c]], t_in[:, CUT[c]], ACT.Copy).then_inc(s_thi, 1)
                    for c in range(NCH):
                        act.wait_ge(s_cen, b * NCH + c + 1)
                        nc.scalar.activation(sq[:, CUT[c]], bank[c][:, 0:CH], ACT.Square).then_inc(s_sq, 1)
                    for c in range(NCH):
                        act.wait_ge(s_spread, b * NCH + c + 1)
                        nc.scalar.activation(inv[:, CUT[c]], bank[2 + c][:, 0:CH], ACT.Copy).then_inc(s_inv, 1)
                    for c in range(NCH):
                        act.wait_ge(s_xn, b * NCH + c + 1)
                        nc.scalar.activation(n_hi[:, CUT[c]], xn[:, CUT[c]], ACT.Copy).then_inc(s_nhi, 1)
                    act.wait_ge(s_route, b * ROUTE + SORTED)
                    nc.scalar.activation(prob[:], top_r[:, :, 0:2], ACT.Sigmoid).then_inc(s_prob, 1)
                    for u in range(NU):
                        act.wait_ge(s_up, b * NU + u + 1)
                        act.wait_ge(s_prod, b * NU + max(u - 3, 0) + 1)
                        nc.scalar.activation(silu[:, u % 4, :], bank[4 + 2 * (u % 2)][:, 0:CH], ACT.Silu).then_inc(s_silu, 1)

            @block.vector
            def _(dve):
                dve.sem_inc(s_prod, 1)
                dve.sem_inc(s_comb, 1)
                with dve.Fori(0, NB) as b:
                    for c in range(NCH):
                        dve.wait_ge(s_thi, b * NCH + c + 1)
                        nc.vector.tensor_tensor(t_lo[:, CUT[c]], t_in[:, CUT[c]], t_hi[:, CUT[c]].bitcast(F32), ALU.subtract
                                                ).then_inc(s_tlo, 1)
                    for k in range(NEWTON):
                        if k == 0:
                            dve.wait_ge(s_var, b + 1)
                        else:
                            dve.wait_ge(s_newton, b * NEWTON + k)
                        rsqrt_step(nc.vector, k, bank[2][0:G, 0:NG], small).then_inc(s_newton, 1)
                    dve.wait_ge(s_newton, b * NEWTON + NEWTON)
                    nc.vector.tensor_copy(packed[:, 0:NG], small[1][:]).then_inc(s_packed, 1)
                    dve.wait_ge(s_packed, b * 2 + 1)
                    nc.vector.tensor_tensor(packed[:, 32:32 + NG], small[1][:], packed[:, 0:NG].bitcast(F32), ALU.subtract
                                            ).then_inc(s_packed, 1)
                    dve.wait_ge(s_turnps, b + 1)
                    nc.vector.tensor_copy(turned_sb[:], bank[3][0:40, 0:G]).then_inc(s_turn, 1)
                    for c in range(NCH):
                        dve.wait_ge(s_inv, b * NCH + c + 1)
                        nc.vector.tensor_tensor(xn[:, CUT[c]], bank[c][:, 0:CH], inv[:, CUT[c]], ALU.mult).then_inc(s_xn, 1)
                    for c in range(NCH):
                        dve.wait_ge(s_nhi, b * NCH + c + 1)
                        nc.vector.tensor_tensor(n_lo[:, CUT[c]], xn[:, CUT[c]], n_hi[:, CUT[c]].bitcast(F32), ALU.subtract
                                                ).then_inc(s_nlo, 1)
                    dve.wait_ge(s_gate, b + 1)
                    scores = bank[4][0:G, 0:NG * NE].rearrange("t (g e) -> t g e", e=NE)
                    k = [0]

                    def link(ins):
                        k[0] += 1
                        ins.then_inc(s_route, 1)
                        dve.wait_ge(s_route, b * ROUTE + k[0])

                    def one(col, like=NE):
                        return col.unsqueeze(2).to_broadcast([G, NG, like])

                    nc.vector.tensor_tensor(biased[:], scores, gate_b[:], ALU.add)
                    link(nc.vector.tensor_copy(raw[:], scores))
                    nc.vector.memset(fence[:, 0:1], 0.0)
                    for g in range(NG):
                        nc.vector.max(top_b[:, g, :], biased[:, g, :])
                        ins = nc.vector.max(top_r[:, g, :], raw[:, g, :])
                    link(ins)
                    assert k[0] == SORTED
                    nc.vector.memset(fence[:, 1:2], 0.0)
                    for g in range(NG):
                        ins = nc.vector.max_index(index[:, g, :], top_b[:, g, :], biased[:, g, :])
                    link(ins)
                    link(nc.vector.tensor_copy(indexf[:], index[:]))
                    nc.vector.tensor_tensor(comb[:], iota[:], one(indexf[:, :, 0]), ALU.is_equal)
                    nc.vector.tensor_tensor(comb2[:], iota[:], one(indexf[:, :, 1]), ALU.is_equal)
                    dve.wait_ge(s_prob, b + 1)
                    link(nc.vector.tensor_tensor(psumt[:], prob[:, :, 0], prob[:, :, 1], ALU.add))
                    link(nc.vector.reciprocal(prec[:], psumt[:]))
                    link(nc.vector.tensor_tensor(pn[:], prob[:], one(prec[:], 2), ALU.mult))
                    nc.vector.tensor_tensor(comb[:], comb[:], one(pn[:, :, 0]), ALU.mult)
                    link(nc.vector.tensor_tensor(comb2[:], comb2[:], one(pn[:, :, 1]), ALU.mult))
                    link(nc.vector.tensor_tensor(comb[:], comb[:], comb2[:], ALU.add))
                    assert k[0] == ROUTE

                    def combine(w):
                        e, c = order[w // NCH], w % NCH
                        dve.wait_ge(s_down, b * NW + w + 1 + 1)
                        y = bank[w % 2][0:G, 0:GC * D].rearrange("t (g d) -> t g d", d=D)
                        if w < NCH:
                            dve.wait_ge(s_out, b * 16 + 16)
                            nc.vector.tensor_copy(acc[:, c * GC:(c + 1) * GC, :], y).then_inc(s_comb, 1)
                            return
                        dve.wait_ge(s_comb, b * NW + w - 1 + 1)
                        for g in range(GC):
                            a = acc[:, c * GC + g, :]
                            ins = nc.vector.scalar_tensor_tensor(out=a, in0=y[:, g, :], scalar=comb[:, c * GC + g, e:e + 1],
                                                                 in1=a, op0=ALU.mult, op1=ALU.add)
                        ins.then_inc(s_comb, 1)

                    for w in range(NW):
                        for u in (2 * w, 2 * w + 1):
                            dve.wait_ge(s_silu, b * NU + u + 1)
                            dve.wait_ge(s_down, b * NW + max(w - 1, 0) + 1)
                            nc.vector.tensor_tensor(prod[:, u % 4, :], bank[5 + 2 * (u % 2)][:, 0:CH], silu[:, u % 4, :],
                                                    ALU.mult).then_inc(s_prod, 1)
                        if w:
                            combine(w - 1)
                    combine(NW - 1)

            @block.tensor
            def _(pe):
                def up(b, u):
                    e, c, r = order[u // 4], (u // 2) % 2, u % 2
                    pe.wait_ge(s_prod, b * NU + max(u - 1, 0) + 1)
                    cols = slice(r * D, (r + 1) * D)
                    for hi, lo, k in ((w1_hi, w1_lo, 4), (w3_hi, w3_lo, 5)):
                        o = bank[k + 2 * (u % 2)][:, 0:CH]
                        nc.tensor.matmul(o, hi[:, e, cols], n_hi[:, CUT[c]], start=True, stop=False)
                        nc.tensor.matmul(o, hi[:, e, cols], n_lo[:, CUT[c]], start=False, stop=False)
                        mm = nc.tensor.matmul(o, lo[:, e, cols], n_hi[:, CUT[c]], start=False, stop=True)
                    mm.then_inc(s_up, 1)

                def down(b, w):
                    e, c = order[w // NCH], w % NCH
                    pe.wait_ge(s_prod, b * NU + 2 * w + 2 + 1)
                    pe.wait_ge(s_comb, b * NW + max(w - 1, 0) + 1)
                    for g in range(GC):
                        y = bank[w % 2][0:G, g * D:(g + 1) * D]
                        for r in range(HALVES):
                            slot = (2 * w + r) % 4
                            mm = nc.tensor.matmul(y, prod[:, slot, g * G:(g + 1) * G], w2[:, e, r, :], start=(r == 0),
                                                  stop=(r == HALVES - 1 and e != NE))
                        if e == NE:
                            t0 = c * CH + g * G
                            mm = nc.tensor.matmul(y, t_in[:, t0:t0 + G], ident[:], start=False, stop=True)
                    mm.then_inc(s_down, 1)

                pe.sem_inc(s_down, 1)
                with pe.Fori(0, NB) as b:
                    for c in range(NCH):
                        pe.wait_ge(s_tlo, b * NCH + c + 1)
                        pe.wait_ge(s_comb, b * NW + 1)
                        o = bank[c][:, 0:CH]
                        nc.tensor.matmul(o, cen[:], t_hi[:, CUT[c]], start=True, stop=False)
                        nc.tensor.matmul(o, cen[:], t_lo[:, CUT[c]], start=False, stop=True).then_inc(s_cen, 1)
                    for c in range(NCH):
                        pe.wait_ge(s_sq, b * NCH + c + 1)
                        for g in range(c * GC, (c + 1) * GC):
                            mm = nc.tensor.matmul(bank[2][0:G, g:g + 1], sq[:, g * G:(g + 1) * G], mean1[:], start=True,
                                                  stop=True)
                    mm.then_inc(s_var, 1)
                    pe.wait_ge(s_packed, b * 2 + 2)
                    nc.tensor.matmul(bank[3][:, 0:G], packed[:].bitcast(F32), ident[0:G, 0:G], is_transpose=True,
                                     start=True, stop=True).then_inc(s_turnps, 1)
                    pe.wait_ge(s_turn, b + 1)
                    for c in range(NCH):
                        for g in range(GC):
                            mm = nc.tensor.matmul(bank[2 + c][:, g * G:(g + 1) * G], sel[:, c * GC + g, :], turned_sb[:],
                                                  start=True, stop=True)
                        mm.then_inc(s_spread, 1)
                    for c in range(NCH):
                        pe.wait_ge(s_xn, b * NCH + c + 1)
                        for g in range(c * GC, (c + 1) * GC):
                            mm = nc.tensor.matmul(bank[4][0:G, g * NE:(g + 1) * NE], xn[:, g * G:(g + 1) * G], gate_w[:],
                                                  start=True, stop=True)
                    mm.then_inc(s_gate, 1)
                    pe.wait_ge(s_nlo, b * NCH + 2)
                    pe.wait_ge(s_route, b * ROUTE + 1)
                    up(b, 0)
                    up(b, 1)
                    for w in range(NW):
                        if w + 1 < NW:
                            up(b, 2 * w + 2)
                            up(b, 2 * w + 3)
                        down(b, w)


SORTED, ROUTE = 2, 9


def early_fusion(nc, x, txt, tok_w, tok_b, p, out):
    with ExitStack() as ctx:
        def sems(name):
            return ctx.enter_context(nc.semaphore(name))

        tok = ctx.enter_context(nc.sbuf_tensor("tok", [D, NB, S], F32))
        conv_phase(nc, sems, tok, x, txt, tok_w, tok_b)
        mixer_phase(nc, sems, tok, p)
        moe_phase(nc, sems, tok, out, p)


def kernel(**inputs):
    import numpy as np
    import concourse.bacc as _bacc
    from concourse.bass_utils import run_bass_kernel_spmd as _run

    a = {k: np.asarray(v) for k, v in inputs.items()}
    at = {k[len("L0_attn_"):]: v for k, v in a.items() if k.startswith("L0_attn_")}
    ff = {k[len("L0_ffn_"):]: v for k, v in a.items() if k.startswith("L0_ffn_")}
    sel = np.zeros((40, NG, D), np.float32)
    for g in range(NG):
        sel[g, g] = sel[32 + g, g] = 1.0
    arrays = {
        "x": a["x"].reshape(NB, D, HIN, WO, STR).transpose(0, 1, 2, 4, 3).reshape(NB, D, HIN * WIN),
        "txt": a["txt"].transpose(2, 0, 1),
        "tok_w": a["L0_tok_W"].reshape(D, D, KSZ * KSZ).transpose(1, 2, 0).reshape(D, KSZ * KSZ * D),
        "tok_b": a["L0_tok_b"].reshape(D, 1),
    }
    small = {
        "pw": at["conv_pw_w"].transpose(2, 0, 1),
        "pw0n": at["conv_pw_w"][0],
        "f": at["f_w"].transpose(2, 0, 1),
        "w1": at["mlp_w1"].transpose(2, 0, 1),
        "w2": at["mlp_w2"].reshape(LAYERS, D, HT, D).transpose(3, 0, 2, 1),
        "cen": (np.eye(D) - 1.0 / D).astype(np.float32),
        "mean1": np.full((D, 1), 1.0 / D, np.float32),
        "ident": np.eye(D, dtype=np.float32),
        "sel": sel,
        "dw": at["conv_dw_w"].transpose(2, 0, 1),
        "dwb": at["conv_dw_b"].T,
        "pwb": at["conv_pw_b"].T,
        "ln1g": at["ln1_g"].reshape(D, 1),
        "ln1b": at["ln1_b"].reshape(D, 1),
        "ln2g": at["ln2_g"].T,
        "ln2b": at["ln2_b"].T,
        "b1": at["mlp_b1"].reshape(LAYERS * HT, D).T,
        "b2": at["mlp_b2"].T,
        "e1": np.concatenate([ff["w1"], ff["sw1"][None]]).transpose(1, 0, 2),
        "e3": np.concatenate([ff["w3"], ff["sw3"][None]]).transpose(1, 0, 2),
        "e2": np.concatenate([ff["w2"], ff["sw2"][None]]).reshape(NE + 1, MH // D, D, D).transpose(2, 0, 1, 3),
        "gate_w": ff["gate_w"].T,
        "gate_b": np.broadcast_to(ff["biases"], (G, NG, NE)),
        "iota": np.broadcast_to(np.arange(NE, dtype=np.float32), (G, NG, NE)),
    }
    nc = _bacc.Bacc("TRN2", target_bir_lowering=False, num_devices=1)
    feed, aps = {}, {}
    for name, v in {**arrays, **small}.items():
        feed["in_" + name] = np.ascontiguousarray(v)
        aps[name] = nc.dram_tensor("in_" + name, feed["in_" + name].shape, F32, kind="ExternalInput").ap()
    out = nc.dram_tensor("out", (NB, S, D), F32, kind="ExternalOutput").ap()
    early_fusion(nc, aps["x"], aps["txt"], aps["tok_w"], aps["tok_b"], aps, out)
    r = _run(nc, [feed], core_ids=[0])
    return r.results[0]["out"]
```

```python
from contextlib import ExitStack

import concourse.bass as bass
from concourse import mybir

F32 = mybir.dt.float32
F32R = mybir.dt.float32r
I32 = mybir.dt.int32
U32 = mybir.dt.uint32
ALU = mybir.AluOpType
ACT = mybir.ActivationFunctionType

NB, D = 16, 128
HIN, WIN = 60, 108
KSZ, STR, PAD = 7, 3, 3
HO, WO = 20, 36
TXT = 128
NIMG = HO * WO
S = NIMG + TXT
LAYERS, TAPS = 4, 4
HID = 512
HT = HID // D
NE, MH = 8, 256
EPS = 1e-5
RSQRT_SEED = 0x5F3759DF

NH = 2
ROWS_OUT = HO // NH
NHALF = ROWS_OUT * WO
ROWS_PAD = STR * (ROWS_OUT - 1) + KSZ
QW = WO + 2
HALF_IN = [(max(0, STR * ROWS_OUT * h - PAD), min(HIN, STR * ROWS_OUT * h - PAD + ROWS_PAD)) for h in range(NH)]
HALF_AT = [lo - (STR * ROWS_OUT * h - PAD) for h, (lo, _) in enumerate(HALF_IN)]

NCH = 2
CH = S // NCH
G = 106
NG = S // G
GC = CH // G
BANK = 512


def conv_phase(nc, sems, tok, x, txt, tok_w, tok_b):
    ntap = KSZ * KSZ
    wcut = [0, 25, ntap]
    with ExitStack() as mem:
        def sb(name, shape, dt=F32):
            return mem.enter_context(nc.sbuf_tensor(name, shape, dt))

        w_hi = sb("w_hi", [D, ntap, D], F32R)
        w_lo = sb("w_lo", [D, ntap, D], F32R)
        bias = sb("tok_bias", [D, 1])
        stage = [sb(f"x_stage{h}", [D, 33 * WIN]) for h in range(NH)]
        x_hi = [sb(f"x_hi{h}", [D, ROWS_PAD, STR, QW], F32R) for h in range(NH)]
        x_lo = [sb(f"x_lo{h}", [D, ROWS_PAD, STR, QW], F32R) for h in range(NH)]
        conv = [mem.enter_context(nc.psum_tensor(f"conv{h}", [D, BANK], F32)) for h in range(NH)]

        w_in = sems("w_in")
        small_in = sems("conv_small_in")
        x_in = [sems(f"x_in{h}") for h in range(NH)]
        w_hi_done = sems("w_hi_done")
        zeroed = sems("pads_zeroed")
        hi_done = [sems(f"x_hi_done{h}") for h in range(NH)]
        lo_done = [sems(f"x_lo_done{h}") for h in range(NH)]
        conv_done = [sems(f"conv_done{h}") for h in range(NH)]
        evac_done = [sems(f"conv_evacuated{h}") for h in range(NH)]

        nrow = [hi - lo for lo, hi in HALF_IN]
        cuts = [[n * k // 3 for k in range(4)] for n in nrow]

        def staged(h, a, b):
            return stage[h][:, a * WIN:b * WIN].rearrange("p (r s q) -> p r s q", s=STR, q=WO)

        def padded(buf, h, a, b):
            return buf[h][:, HALF_AT[h] + a:HALF_AT[h] + b, :, 1:1 + WO]

        with nc.Block() as block:
            @block.sync
            def _(sp):
                for k in range(2):
                    n = (wcut[k + 1] - wcut[k]) * D
                    sp.dma_start(stage[k][:, 0:n], tok_w[:, wcut[k] * D:wcut[k + 1] * D]).then_inc(w_in, 16)
                sp.dma_start(bias[:], tok_b).then_inc(small_in, 16)
                sp.dma_start(tok[:, :, NIMG:S], txt).then_inc(small_in, 16)
                with sp.Fori(0, NB) as b:
                    for h in range(NH):
                        sp.wait_ge(lo_done[h], b * 3 + 1)
                        r0, r1 = HALF_IN[h]
                        sp.dma_start(stage[h][:, 0:(r1 - r0) * WIN],
                                     x[bass.ds(b, 1), :, r0 * WIN:r1 * WIN].rearrange("o p n -> p (o n)")
                                     ).then_inc(x_in[h], 16)
                sp.wait_ge(small_in, 32)

            @block.gpsimd
            def _(pool):
                for h in range(NH):
                    nc.gpsimd.memset(x_hi[h][:].bitcast(F32), 0.0).then_inc(zeroed, 1)
                    nc.gpsimd.memset(x_lo[h][:].bitcast(F32), 0.0).then_inc(zeroed, 1)

            @block.scalar
            def _(act):
                for k in range(2):
                    act.wait_ge(w_in, 32)
                    n = (wcut[k + 1] - wcut[k]) * D
                    dst = w_hi[:, wcut[k]:wcut[k + 1], :].rearrange("p t c -> p (t c)")
                    nc.scalar.activation(dst, stage[k][:, 0:n], ACT.Copy).then_inc(w_hi_done, 1)

                def split_hi(h, b):
                    act.wait_ge(x_in[h], b * 16 + 16)
                    act.wait_ge(conv_done[h], b)
                    for k in range(3):
                        r0, r1 = cuts[h][k:k + 2]
                        nc.scalar.activation(padded(x_hi, h, r0, r1), staged(h, r0, r1),
                                             ACT.Copy).then_inc(hi_done[h], 1)

                def evacuate(h, b):
                    act.wait_ge(conv_done[h], b + 1)
                    nc.scalar.activation(tok[:, bass.ds(b, 1), h * NHALF:(h + 1) * NHALF].rearrange("p o n -> p (o n)"),
                                         conv[h][:, 0:NHALF], ACT.Identity, bias=bias[:, 0:1]).then_inc(evac_done[h], 1)

                act.wait_ge(small_in, 32)
                act.wait_ge(zeroed, 2 * NH)
                for h in range(NH):
                    act.sem_inc(evac_done[h], 1)
                for h in range(NH):
                    split_hi(h, 0)
                with act.Fori(0, NB - 1) as b:
                    for h in range(NH):
                        evacuate(h, b)
                        split_hi(h, b + 1)
                for h in range(NH):
                    evacuate(h, NB - 1)

            @block.vector
            def _(dve):
                for k in range(2):
                    dve.wait_ge(w_hi_done, k + 1)
                    n = (wcut[k + 1] - wcut[k]) * D
                    hi = w_hi[:, wcut[k]:wcut[k + 1], :].rearrange("p t c -> p (t c)")
                    lo = w_lo[:, wcut[k]:wcut[k + 1], :].rearrange("p t c -> p (t c)")
                    nc.vector.tensor_tensor(lo, stage[k][:, 0:n], hi.bitcast(F32), ALU.subtract).then_inc(lo_done[k], 1)
                dve.wait_ge(zeroed, 2 * NH)
                with dve.Fori(0, NB) as b:
                    for h in range(NH):
                        for k in range(3):
                            r0, r1 = cuts[h][k:k + 2]
                            dve.wait_ge(hi_done[h], b * 3 + k + 1)
                            nc.vector.tensor_tensor(padded(x_lo, h, r0, r1), staged(h, r0, r1),
                                                    padded(x_hi, h, r0, r1).bitcast(F32),
                                                    ALU.subtract).then_inc(lo_done[h], 1)

            @block.tensor
            def _(pe):
                for h in range(NH):
                    pe.wait_ge(lo_done[h], 1)
                with pe.Fori(0, NB) as b:
                    for h in range(NH):
                        pe.wait_ge(lo_done[h], b * 3 + 4)
                        pe.wait_ge(evac_done[h], b + 1)
                        for kh in range(KSZ):
                            for kw in range(KSZ):
                                t = kh * KSZ + kw
                                q, phase = divmod(kw - PAD, STR)
                                rows = slice(kh, kh + STR * (ROWS_OUT - 1) + 1, STR)
                                cols = slice(q + 1, q + 1 + WO)
                                hi, lo = x_hi[h][:, rows, phase, cols], x_lo[h][:, rows, phase, cols]
                                out = conv[h][:, 0:NHALF]
                                nc.tensor.matmul(out, w_hi[:, t, :], hi, start=(t == 0), stop=False)
                                nc.tensor.matmul(out, w_hi[:, t, :], lo, start=False, stop=False)
                                mm = nc.tensor.matmul(out, w_lo[:, t, :], hi, start=False, stop=(t == ntap - 1))
                        mm.then_inc(conv_done[h], 1)


NLN = 2 + LAYERS
COST = {"center": 0.72, "var": 0.36, "turn": 0.1, "spread": 0.36, "pw": 0.54, "kh": 1.08, "up": 0.54, "down": 0.71,
        "newton": 0.08, "pack_hi": 0.08, "pack_lo": 0.08, "taps": 3.1, "turned": 0.18,
        "act": 0.45, "dve": 0.52, "pool": 1.1}
HOP = 0.2


def mixer_steps():
    out, index, done, free = [], {}, {}, {}

    def step(engine, kind, after, i=0, n=0, c=0, j=0):
        what = (kind, i, n, c, j)
        cost = COST[kind] if kind in COST else COST[engine]
        start = max([free.get(engine, 0.0)] + [done[a] + HOP for a in after])
        free[engine] = done[what] = start + cost
        index[what] = len(out)
        out.append((engine, what, [index[a] for a in after], cost, start))
        return what

    def norm(i, n, centered):
        sq = [step("act", "square", [centered[c]], i, n, c) for c in range(NCH)]
        for c in range(NCH):
            var = step("pe", "var", [sq[c]], i, n, c)
        v = step("dve", "newton", [var], i, n, 0, 0)
        for k in range(1, NEWTON):
            v = step("dve", "newton", [v], i, n, 0, k)
        v = step("dve", "pack_lo", [step("dve", "pack_hi", [v], i, n)], i, n)
        t = step("dve", "turned", [step("pe", "turn", [v], i, n)], i, n)
        inv = [step("act", "inv", [step("pe", "spread", [t], i, n, c)], i, n, c) for c in range(NCH)]
        return [step("dve", "normed", [inv[c]], i, n, c) for c in range(NCH)]

    hi = [step("act", "split_hi", [], c=c) for c in range(NCH)]
    lo = [step("dve", "split_lo", [hi[c]], c=c) for c in range(NCH)]
    m = norm(0, 0, [step("pe", "center", [lo[c]], 0, 0, c) for c in range(NCH)])
    for i in range(LAYERS):
        y0 = [step("act", "y0", [m[c]], i, c=c) for c in range(NCH)]
        taps = step("dve", "taps", y0, i)
        hi = [step("act", "y_hi", [taps], i, c=c) for c in range(NCH)]
        lo = [step("dve", "y_lo", [hi[c]], i, c=c) for c in range(NCH)]
        pw = [step("pe", "pw", [lo[c]], i, c=c) for c in range(NCH)]
        if i == 0:
            xn = norm(0, 1, pw)
            hi = [step("act", "n_hi", [xn[c]], 0, 1, c) for c in range(NCH)]
            lo = [step("dve", "x1_lo", [hi[c]], 0, 1, c) for c in range(NCH)]
        else:
            hi = [step("act", "x_hi", [pw[c]], i, c=c) for c in range(NCH)]
            lo = [step("dve", "x_lo", [hi[c]], i, c=c) for c in range(NCH)]
        kh = [step("pe", "kh", [lo[c]], i, c=c) for c in range(NCH)]
        scan = []
        for c in range(NCH):
            cand = step("dve", "cand", [step("act", "g_cand", [kh[c]], i, c=c)], i, c=c)
            take = step("dve", "take", [step("act", "g_take", [kh[c]], i, c=c), cand], i, c=c)
            scan.append(step("dve", "scan", [step("act", "g_keep", [kh[c]], i, c=c), take], i, c=c))
        hi = [step("act", "s_hi", [scan[c]], i, c=c) for c in range(NCH)]
        lo = [step("dve", "s_lo", [hi[c]], i, c=c) for c in range(NCH)]
        xn = norm(i, 2 + i, [step("pe", "center", [lo[c]], i, 2 + i, c) for c in range(NCH)])
        hi = [step("act", "n_hi", [xn[c]], i, 2 + i, c) for c in range(NCH)]
        lo = [step("pool", "n_lo", [hi[c]], i, 2 + i, c) for c in range(NCH)]
        tiles = [(c, j) for c in range(NCH) for j in range(HT)]
        relu = {}
        for q in range(len(tiles) + 2):
            if q >= 2:
                c, j = tiles[q - 2]
                down = step("pe", "down", [relu[c, j]], i, c=c, j=j)
                if j == HT - 1:
                    m_c = step(*(("act", "out") if i < LAYERS - 1 else ("dve", "final")), [down], i, c=c)
                    m = [m_c] if c == 0 else m + [m_c]
            if q < len(tiles):
                c, j = tiles[q]
                relu[c, j] = step("dve" if j % 2 else "act", "relu", [step("pe", "up", [lo[c]], i, c=c, j=j)], i, c=c, j=j)
    return out


def two_streams():
    steps = mixer_steps()
    busy, reached, ends, placed = {}, {}, {}, {}
    for _, s, k in sorted((st[4] + LAG * s, s, k) for k, st in enumerate(steps) for s in range(2)):
        engine, what, after, cost, _ = steps[k]
        t = max([LAG * s, reached.get((s, engine), 0.0)] + [ends[s, a] + HOP for a in after])
        moved = True
        while moved:
            moved = False
            for b0, b1 in busy.setdefault(engine, []):
                for turn in (-PERIOD, 0.0, PERIOD):
                    at = t % PERIOD
                    if at < b1 + turn - 1e-9 and at + cost > b0 + turn + 1e-9:
                        t += b1 + turn - at
                        moved = True
        busy[engine].append((t % PERIOD, t % PERIOD + cost))
        ends[s, k] = reached[s, engine] = t + cost
        placed.setdefault(engine, []).append((t % PERIOD, s, t >= PERIOD, what))
    assert all(ends[s, k] <= PERIOD + LAG * s for s, k in ends)
    return {e: [x[1:] for x in sorted(v)] for e, v in placed.items()}


def run_pairs(order, fori, do):
    for s, wraps, what in order:
        if not wraps:
            do(s, 0, *what)
    with fori(1, NB // 2) as it:
        for s, wraps, what in order:
            do(s, it - 1 if wraps else it, *what)
    for s, wraps, what in order:
        if wraps:
            do(s, NB // 2 - 1, *what)


PERIOD, LAG = 217.9, 8.0
NEWTON = 11


def rsqrt_step(eng, k, var, small):
    v, y, t = small
    if k == 0:
        return eng.tensor_scalar(v[:], var, EPS, None, ALU.add)
    if k == 1:
        return eng.tensor_scalar(y[:].bitcast(I32), v[:].bitcast(I32), -0.5, float(RSQRT_SEED), ALU.mult, ALU.add)
    k = (k - 2) % 3
    if k == 0:
        return eng.tensor_tensor(t[:], y[:], y[:], ALU.mult)
    if k == 1:
        return eng.scalar_tensor_tensor(out=t[:], in0=t[:], scalar=-0.5, in1=v[:], op0=ALU.mult, op1=ALU.mult)
    return eng.scalar_tensor_tensor(out=y[:], in0=t[:], scalar=1.5, in1=y[:], op0=ALU.add, op1=ALU.mult)


def mixer_phase(nc, sems, tok, p):
    order = two_streams()
    with ExitStack() as mem:
        def sb(name, shape, dt=F32):
            return mem.enter_context(nc.sbuf_tensor(name, shape, dt))

        pw_hi, pw_lo = sb("pw_hi", [D, LAYERS, D], F32R), sb("pw_lo", [D, LAYERS, D], F32R)
        f_hi, f_lo = sb("f_hi", [D, LAYERS, 2 * D], F32R), sb("f_lo", [D, LAYERS, 2 * D], F32R)
        w1_hi, w1_lo = sb("w1_hi", [D, LAYERS, HID], F32R), sb("w1_lo", [D, LAYERS, HID], F32R)
        w2 = sb("w2", [D, LAYERS, HT, D])
        cen32, cen = sb("cen32", [D, D]), sb("cen", [D, D], F32R)
        mean1 = sb("mean1", [D, 1])
        ident = sb("ident", [D, D])
        sel = sb("sel", [40, NG, D], F32R)
        dw, dwb = sb("dw", [D, LAYERS, TAPS]), sb("dwb", [D, LAYERS])
        pwb, pwb_c = sb("pwb", [D, LAYERS]), sb("pwb_c", [D, 1])
        ln1g, ln1b = sb("ln1g", [D, 1]), sb("ln1b", [D, 1])
        ln2g, ln2b = sb("ln2g", [D, LAYERS]), sb("ln2b", [D, LAYERS])
        b1, b1f = sb("b1", [D, LAYERS * HT]), sb("b1f", [D, LAYERS * HT])
        b2 = sb("b2", [D, LAYERS])

        psum = [[mem.enter_context(nc.psum_tensor(f"ps{s}_{k}", [D, BANK], F32)) for k in range(4)] for s in range(2)]

        with ExitStack() as tmp:
            def sbt(name, shape, dt=F32):
                return tmp.enter_context(nc.sbuf_tensor(name, shape, dt))

            pw32, pw0n = sbt("pw32", [D, LAYERS, D]), sbt("pw0n", [D, D])
            f32, w132 = sbt("f32", [D, LAYERS, 2 * D]), sbt("w132", [D, LAYERS, HID])
            sel32 = sbt("sel32", [40, NG, D])
            loads = [(pw32, "pw"), (pw0n, "pw0n"), (f32, "f"), (w132, "w1"), (w2, "w2"), (cen32, "cen"),
                     (mean1, "mean1"), (ident, "ident"), (sel32, "sel"), (dw, "dw"), (dwb, "dwb"), (pwb, "pwb"),
                     (ln1g, "ln1g"), (ln1b, "ln1b"), (ln2g, "ln2g"), (ln2b, "ln2b"), (b1, "b1"), (b2, "b2")]
            loaded = sems("mixer_weights_in")
            folded = sems("mixer_folded_psum")
            hi_done = sems("mixer_w_hi")
            with nc.Block() as block:
                @block.sync
                def _(sp):
                    for dst, name in loads:
                        sp.dma_start(dst[:], p[name]).then_inc(loaded, 16)

                @block.tensor
                def _(pe):
                    pe.wait_ge(loaded, 16 * len(loads))
                    nc.tensor.matmul(psum[0][0][:, 0:D], pw0n[:], cen32[:], start=True, stop=True)
                    nc.tensor.matmul(psum[0][1][:, 0:1], cen32[:], pwb[:, 0:1], start=True, stop=True)
                    for i in range(LAYERS):
                        for j in range(HT):
                            mm = nc.tensor.matmul(psum[0][2][:, i * HT + j:i * HT + j + 1],
                                                  w132[:, i, j * D:(j + 1) * D], ln2b[:, i:i + 1], start=True, stop=True)
                    mm.then_inc(folded, 1)

                @block.scalar
                def _(act):
                    act.wait_ge(loaded, 16 * len(loads))
                    nc.scalar.activation(cen[:], cen32[:], ACT.Copy)
                    nc.scalar.activation(sel[:], sel32[:], ACT.Copy)
                    nc.scalar.activation(pw_hi[:, 1:LAYERS, :], pw32[:, 1:LAYERS, :], ACT.Copy)
                    nc.scalar.activation(f_hi[:], f32[:], ACT.Copy)
                    for i in range(LAYERS):
                        nc.scalar.activation(w1_hi[:, i, :], w132[:, i, :], ACT.Copy, scale=ln2g[:, i:i + 1])
                    act.wait_ge(folded, 1)
                    nc.scalar.activation(pw_hi[:, 0, :], psum[0][0][:, 0:D], ACT.Copy)
                    nc.scalar.activation(pwb_c[:], psum[0][1][:, 0:1], ACT.Copy).then_inc(hi_done, 1)

                @block.vector
                def _(dve):
                    dve.wait_ge(hi_done, 1)
                    nc.vector.tensor_tensor(pw_lo[:, 1:LAYERS, :], pw32[:, 1:LAYERS, :],
                                            pw_hi[:, 1:LAYERS, :].bitcast(F32), ALU.subtract)
                    nc.vector.tensor_tensor(f_lo[:], f32[:], f_hi[:].bitcast(F32), ALU.subtract)
                    for i in range(LAYERS):
                        nc.vector.scalar_tensor_tensor(out=w1_lo[:, i, :], in0=w132[:, i, :], scalar=ln2g[:, i:i + 1],
                                                       in1=w1_hi[:, i, :].bitcast(F32), op0=ALU.mult, op1=ALU.subtract)
                    nc.vector.tensor_tensor(pw_lo[:, 0, :], psum[0][0][:, 0:D], pw_hi[:, 0, :].bitcast(F32), ALU.subtract)
                    nc.vector.tensor_tensor(b1f[:], psum[0][2][:, 0:LAYERS * HT], b1[:], ALU.add)

        class Stream:
            pass

        streams = []
        for s in range(2):
            w = Stream()
            w.m = sb(f"m{s}", [D, TAPS - 1 + S])
            w.y = sb(f"y{s}", [D, S])
            w.y_hi, w.y_lo = sb(f"y_hi{s}", [D, S], F32R), sb(f"y_lo{s}", [D, S], F32R)
            w.x_hi, w.x_lo = sb(f"xx_hi{s}", [D, S], F32R), sb(f"xx_lo{s}", [D, S], F32R)
            w.keep = sb(f"keep{s}", [D, S])
            w.take = sb(f"take{s}", [D, S])
            w.cand = sb(f"cand{s}", [D, S])
            w.hid = sb(f"hid{s}", [D, HT, CH])
            w.small = [sb(f"rs{k}_{s}", [G, NG]) for k in range(3)]
            w.packed = sb(f"packed{s}", [G, D], F32R)
            w.turned = sb(f"turned{s}", [40, G], F32R)
            w.bank = psum[s]
            w.split_hi = sems(f"s{s}_split_hi")
            w.split_lo = sems(f"s{s}_split_lo")
            w.centered = sems(f"s{s}_centered")
            w.squared = sems(f"s{s}_squared")
            w.var = sems(f"s{s}_var")
            w.newton = sems(f"s{s}_newton")
            w.packed_done = sems(f"s{s}_packed")
            w.turned_ps = sems(f"s{s}_turned_psum")
            w.turned_done = sems(f"s{s}_turned")
            w.spread = sems(f"s{s}_spread")
            w.spread_done = sems(f"s{s}_spread_copied")
            w.m_norm = sems(f"s{s}_input_normed")
            w.normed = sems(f"s{s}_normed")
            w.n_hi = sems(f"s{s}_normed_hi")
            w.n_lo = sems(f"s{s}_normed_lo")
            w.dw0 = sems(f"s{s}_dw_first")
            w.dw = sems(f"s{s}_dw_taps")
            w.y_hi_done = sems(f"s{s}_y_hi")
            w.y_lo_done = sems(f"s{s}_y_lo")
            w.pw = sems(f"s{s}_pointwise")
            w.x_hi_done = sems(f"s{s}_x_hi")
            w.x_lo_done = sems(f"s{s}_x_lo")
            w.kh = sems(f"s{s}_kh")
            w.gates = sems(f"s{s}_gates")
            w.cand_done = sems(f"s{s}_candidate")
            w.take_done = sems(f"s{s}_taken")
            w.scan = sems(f"s{s}_scan")
            w.s_hi = sems(f"s{s}_scan_hi")
            w.s_lo = sems(f"s{s}_scan_lo")
            w.up = sems(f"s{s}_mlp_up")
            w.relu_a = sems(f"s{s}_relu_act")
            w.relu_v = sems(f"s{s}_relu_dve")
            w.down = sems(f"s{s}_mlp_down")
            w.m_done = sems(f"s{s}_mlp_out")
            w.tok_done = sems(f"s{s}_tok_updated")
            streams.append(w)
        pads = sems("mixer_pads")

        CUT = [slice(c * CH, (c + 1) * CH) for c in range(NCH)]
        M = [slice(TAPS - 1 + c * CH, TAPS - 1 + (c + 1) * CH) for c in range(NCH)]
        NL, NN = 2 * LAYERS, 2 * NLN

        def tok_chunk(it, s, c):
            return tok[:, bass.ds(it * 2 + s, 1), c * CH:(c + 1) * CH].rearrange("p o n -> p (o n)")

        def newton(eng, w, it, n, k):
            if k == 0:
                eng.wait_ge(w.var, it * NN + 2 * n + 2)
            else:
                eng.wait_ge(w.newton, it * (NEWTON * NLN) + n * NEWTON + k)
            rsqrt_step(eng, k, w.bank[2][0:G, 0:NG], w.small).then_inc(w.newton, 1)

        def pack(eng, w, it, n, lo):
            if not lo:
                eng.wait_ge(w.newton, it * (NEWTON * NLN) + n * NEWTON + NEWTON)
                eng.tensor_copy(w.packed[:, 0:NG], w.small[1][:]).then_inc(w.packed_done, 1)
            else:
                eng.wait_ge(w.packed_done, it * NN + 2 * n + 1)
                eng.tensor_tensor(w.packed[:, 32:32 + NG], w.small[1][:], w.packed[:, 0:NG].bitcast(F32), ALU.subtract
                                  ).then_inc(w.packed_done, 1)

        with nc.Block() as block:
            @block.gpsimd
            def _(pool):
                for w in streams:
                    nc.gpsimd.memset(w.m[:, 0:TAPS - 1], 0.0).then_inc(pads, 1)
                    nc.gpsimd.memset(w.packed[:].bitcast(F32), 0.0).then_inc(pads, 1)

                def do(s, it, kind, i, n, c, j):
                    w = streams[s]
                    pool.wait_ge(w.n_hi, it * NL + 2 * i + c + 1)
                    nc.gpsimd.tensor_tensor(w.x_lo[:, CUT[c]], w.cand[:, CUT[c]], w.x_hi[:, CUT[c]].bitcast(F32),
                                            ALU.subtract).then_inc(w.n_lo, 1)

                run_pairs(order["pool"], pool.Fori, do)

            @block.tensor
            def _(pe):
                def three(out, w_hi, w_lo, hi, lo):
                    nc.tensor.matmul(out, w_hi, hi, start=True, stop=False)
                    nc.tensor.matmul(out, w_hi, lo, start=False, stop=False)
                    return nc.tensor.matmul(out, w_lo, hi, start=False, stop=True)

                def do(s, it, kind, i, n, c, j):
                    w = streams[s]
                    e = it * NL + 2 * i + c
                    bank = w.bank[c][:, 0:CH]
                    if kind == "center":
                        if n == 0:
                            pe.wait_ge(w.split_lo, it * 2 + c + 1)
                            parts = [w.y_hi, w.y_lo]
                        else:
                            pe.wait_ge(w.s_lo, e + 1)
                            parts = [w.y_hi, w.y_lo, w.x_hi, w.x_lo]
                        for k, part in enumerate(parts):
                            mm = nc.tensor.matmul(bank, cen[:], part[:, CUT[c]], start=(k == 0), stop=(k == len(parts) - 1))
                        mm.then_inc(w.centered, 1)
                    elif kind == "var":
                        pe.wait_ge(w.squared, it * NN + 2 * n + c + 1)
                        for g in range(c * GC, (c + 1) * GC):
                            mm = nc.tensor.matmul(w.bank[2][0:G, g:g + 1], w.keep[:, g * G:(g + 1) * G], mean1[:],
                                                  start=True, stop=True)
                        mm.then_inc(w.var, 1)
                    elif kind == "turn":
                        pe.wait_ge(w.packed_done, it * NN + 2 * n + 2)
                        nc.tensor.matmul(w.bank[3][:, 0:G], w.packed[:].bitcast(F32), ident[0:G, 0:G], is_transpose=True,
                                         start=True, stop=True).then_inc(w.turned_ps, 1)
                    elif kind == "spread":
                        if c == 0:
                            pe.wait_ge(w.turned_done, it * NLN + n + 1)
                        for g in range(GC):
                            mm = nc.tensor.matmul(w.bank[2 + c][:, g * G:(g + 1) * G], sel[:, c * GC + g, :], w.turned[:],
                                                  start=True, stop=True)
                        mm.then_inc(w.spread, 1)
                    elif kind == "pw":
                        pe.wait_ge(w.y_lo_done, e + 1)
                        mm = three(bank, pw_hi[:, i, :], pw_lo[:, i, :], w.y_hi[:, CUT[c]], w.y_lo[:, CUT[c]])
                        mm.then_inc(w.centered if i == 0 else w.pw, 1)
                    elif kind == "kh":
                        pe.wait_ge(w.x_hi_done, e + 1)
                        pe.wait_ge(w.x_lo_done, e + 1)
                        for out, cols in ((w.bank[2 + c][:, 0:CH], slice(0, D)), (bank, slice(D, 2 * D))):
                            mm = three(out, f_hi[:, i, cols], f_lo[:, i, cols], w.x_hi[:, CUT[c]], w.x_lo[:, CUT[c]])
                        mm.then_inc(w.kh, 1)
                    elif kind == "up":
                        if j == 0:
                            pe.wait_ge(w.n_lo, e + 1)
                        if c == 0 and j == 1:
                            pe.wait_ge(w.spread_done, it * NN + 2 * (2 + i) + 2)
                        cols = slice(j * D, (j + 1) * D)
                        three(w.bank[2 + j % 2][:, 0:CH], w1_hi[:, i, cols], w1_lo[:, i, cols], w.x_hi[:, CUT[c]],
                              w.x_lo[:, CUT[c]]).then_inc(w.up, 1)
                    elif kind == "down":
                        pe.wait_ge(w.relu_v if j % 2 else w.relu_a, e * (HT // 2) + j // 2 + 1)
                        mm = nc.tensor.matmul(bank, w2[:, i, j, :], w.hid[:, j, :], start=(j == 0), stop=(j == HT - 1))
                        if j == HT - 1:
                            mm.then_inc(w.down, 1)

                pe.wait_ge(pads, 4)
                run_pairs(order["pe"], pe.Fori, do)

            @block.scalar
            def _(act):
                def do(s, it, kind, i, n, c, j):
                    w = streams[s]
                    e, en = it * NL + 2 * i + c, it * NN + 2 * n + c
                    bank, kbank = w.bank[c][:, 0:CH], w.bank[2 + c][:, 0:CH]
                    op = nc.scalar.activation
                    if kind == "split_hi":
                        op(w.y_hi[:, CUT[c]], tok_chunk(it, s, c), ACT.Copy).then_inc(w.split_hi, 1)
                    elif kind == "square":
                        act.wait_ge(w.centered, en + 1)
                        op(w.keep[:, CUT[c]], bank, ACT.Square, bias=pwb_c[:, 0:1] if n == 1 else 0.0).then_inc(w.squared, 1)
                    elif kind == "inv":
                        act.wait_ge(w.spread, en + 1)
                        op(w.take[:, CUT[c]], kbank, ACT.Copy, scale=ln1g[:, 0:1] if n == 1 else 1.0).then_inc(w.spread_done, 1)
                    elif kind == "n_hi" and n == 1:
                        act.wait_ge(w.normed, it * (NN - 2) + c + 1)
                        op(w.x_hi[:, CUT[c]], w.cand[:, CUT[c]], ACT.Identity, bias=ln1b[:, 0:1]).then_inc(w.x_hi_done, 1)
                    elif kind == "n_hi":
                        act.wait_ge(w.normed, it * (NN - 2) + 2 * (n - 1) + c + 1)
                        op(w.x_hi[:, CUT[c]], w.cand[:, CUT[c]], ACT.Copy).then_inc(w.n_hi, 1)
                    elif kind == "y0":
                        if i == 0:
                            act.wait_ge(w.m_norm, it * 2 + c + 1)
                        else:
                            act.wait_ge(w.m_done, it * (NL - 2) + 2 * (i - 1) + c + 1)
                        op(w.y[:, CUT[c]], w.m[:, M[c]], ACT.Identity, scale=dw[:, i, TAPS - 1:TAPS], bias=dwb[:, i:i + 1]
                           ).then_inc(w.dw0, 1)
                    elif kind == "y_hi":
                        act.wait_ge(w.dw, (it * NL + 2 * i) * 3 + 5 + c)
                        op(w.y_hi[:, CUT[c]], w.y[:, CUT[c]], ACT.Copy).then_inc(w.y_hi_done, 1)
                    elif kind == "x_hi":
                        act.wait_ge(w.pw, it * (NL - 2) + 2 * (i - 1) + c + 1)
                        op(w.x_hi[:, CUT[c]], bank, ACT.Identity, bias=pwb[:, i:i + 1]).then_inc(w.x_hi_done, 1)
                    elif kind == "g_cand":
                        act.wait_ge(w.kh, e + 1)
                        op(w.cand[:, CUT[c]], bank, ACT.Sigmoid).then_inc(w.gates, 1)
                    elif kind == "g_take":
                        op(w.take[:, CUT[c]], kbank, ACT.Sigmoid).then_inc(w.gates, 1)
                    elif kind == "g_keep":
                        op(w.keep[:, CUT[c]], kbank, ACT.Sigmoid, scale=-1.0).then_inc(w.gates, 1)
                    elif kind == "s_hi":
                        act.wait_ge(w.scan, e + 1)
                        op(w.y_hi[:, CUT[c]], w.y[:, CUT[c]], ACT.Copy).then_inc(w.s_hi, 1)
                    elif kind == "relu":
                        act.wait_ge(w.up, e * HT + j + 1)
                        op(w.hid[:, j, :], w.bank[2 + j % 2][:, 0:CH], ACT.Relu, bias=b1f[:, i * HT + j:i * HT + j + 1]
                           ).then_inc(w.relu_a, 1)
                    elif kind == "out":
                        act.wait_ge(w.down, e + 1)
                        op(w.m[:, M[c]], bank, ACT.Identity, bias=b2[:, i:i + 1]).then_inc(w.m_done, 1)

                act.wait_ge(pads, 4)
                run_pairs(order["act"], act.Fori, do)

            @block.vector
            def _(dve):
                def do(s, it, kind, i, n, c, j):
                    w = streams[s]
                    e, en = it * NL + 2 * i + c, it * NN + 2 * n + c
                    bank = w.bank[c][:, 0:CH]
                    tt, stt = nc.vector.tensor_tensor, nc.vector.scalar_tensor_tensor
                    if kind == "split_lo":
                        dve.wait_ge(w.split_hi, it * 2 + c + 1)
                        tt(w.y_lo[:, CUT[c]], tok_chunk(it, s, c), w.y_hi[:, CUT[c]].bitcast(F32), ALU.subtract
                           ).then_inc(w.split_lo, 1)
                    elif kind == "newton":
                        newton(dve, w, it, n, j)
                    elif kind in ("pack_hi", "pack_lo"):
                        pack(dve, w, it, n, kind == "pack_lo")
                    elif kind == "turned":
                        dve.wait_ge(w.turned_ps, it * NLN + n + 1)
                        nc.vector.tensor_copy(w.turned[:], w.bank[3][0:40, 0:G]).then_inc(w.turned_done, 1)
                    elif kind == "normed":
                        dve.wait_ge(w.spread_done, en + 1)
                        inv = w.take[:, CUT[c]]
                        if n == 0:
                            tt(w.m[:, M[c]], bank, inv, ALU.mult).then_inc(w.m_norm, 1)
                        elif n == 1:
                            stt(out=w.cand[:, CUT[c]], in0=bank, scalar=pwb_c[:, 0:1], in1=inv, op0=ALU.add, op1=ALU.mult
                                ).then_inc(w.normed, 1)
                        else:
                            tt(w.cand[:, CUT[c]], bank, inv, ALU.mult).then_inc(w.normed, 1)
                    elif kind == "x1_lo":
                        dve.wait_ge(w.x_hi_done, e + 1)
                        stt(out=w.x_lo[:, CUT[c]], in0=w.cand[:, CUT[c]], scalar=ln1b[:, 0:1],
                            in1=w.x_hi[:, CUT[c]].bitcast(F32), op0=ALU.add, op1=ALU.subtract).then_inc(w.x_lo_done, 1)
                    elif kind == "taps":
                        for k in range(TAPS - 1):
                            for c in range(NCH):
                                if k == 0:
                                    dve.wait_ge(w.dw0, it * NL + 2 * i + c + 1)
                                else:
                                    dve.wait_ge(w.dw, (it * NL + 2 * i) * 3 + 2 * (k - 1) + c + 1)
                                stt(out=w.y[:, CUT[c]], in0=w.m[:, c * CH + k:c * CH + k + CH], scalar=dw[:, i, k:k + 1],
                                    in1=w.y[:, CUT[c]], op0=ALU.mult, op1=ALU.add).then_inc(w.dw, 1)
                    elif kind == "y_lo":
                        dve.wait_ge(w.y_hi_done, e + 1)
                        tt(w.y_lo[:, CUT[c]], w.y[:, CUT[c]], w.y_hi[:, CUT[c]].bitcast(F32), ALU.subtract
                           ).then_inc(w.y_lo_done, 1)
                    elif kind == "x_lo":
                        dve.wait_ge(w.x_hi_done, e + 1)
                        stt(out=w.x_lo[:, CUT[c]], in0=bank, scalar=pwb[:, i:i + 1], in1=w.x_hi[:, CUT[c]].bitcast(F32),
                            op0=ALU.add, op1=ALU.subtract).then_inc(w.x_lo_done, 1)
                    elif kind == "cand":
                        dve.wait_ge(w.gates, e * 3 + 1)
                        stt(out=w.cand[:, CUT[c]], in0=bank, scalar=0.5, in1=w.cand[:, CUT[c]], op0=ALU.add, op1=ALU.max
                            ).then_inc(w.cand_done, 1)
                    elif kind == "take":
                        dve.wait_ge(w.gates, e * 3 + 2)
                        dve.wait_ge(w.cand_done, e + 1)
                        tt(w.take[:, CUT[c]], w.take[:, CUT[c]], w.cand[:, CUT[c]], ALU.mult).then_inc(w.take_done, 1)
                    elif kind == "scan":
                        dve.wait_ge(w.gates, e * 3 + 3)
                        dve.wait_ge(w.take_done, e + 1)
                        if c:
                            dve.wait_ge(w.scan, e)
                        first = 0.5 if c == 0 else w.y[:, c * CH - 1:c * CH]
                        nc.vector.tensor_tensor_scan(w.y[:, CUT[c]], w.keep[:, CUT[c]], w.take[:, CUT[c]], first, ALU.mult,
                                                     ALU.add).then_inc(w.scan, 1)
                    elif kind == "s_lo":
                        dve.wait_ge(w.s_hi, e + 1)
                        tt(w.y_lo[:, CUT[c]], w.y[:, CUT[c]], w.y_hi[:, CUT[c]].bitcast(F32), ALU.subtract
                           ).then_inc(w.s_lo, 1)
                    elif kind == "relu":
                        dve.wait_ge(w.up, e * HT + j + 1)
                        nc.vector.tensor_scalar(w.hid[:, j, :], w.bank[2 + j % 2][:, 0:CH],
                                                b1f[:, i * HT + j:i * HT + j + 1], 0.0, ALU.add, ALU.max).then_inc(w.relu_v, 1)
                    elif kind == "final":
                        dve.wait_ge(w.down, e + 1)
                        stt(out=tok_chunk(it, s, c), in0=bank, scalar=b2[:, i:i + 1], in1=tok_chunk(it, s, c), op0=ALU.add,
                            op1=ALU.add).then_inc(w.tok_done, 1)

                dve.wait_ge(pads, 4)
                run_pairs(order["dve"], dve.Fori, do)


def moe_phase(nc, sems, tok, out, p):
    NX = NE + 1
    HALVES = MH // D
    UNITS = NX * HALVES
    SCALED = NE * HALVES
    HI_LAG, DOWN_LAG, DEPTH = 2, 4, 4
    expert = [NE] + list(range(NE))
    with ExitStack() as mem:
        def sb(name, shape, dt=F32):
            return mem.enter_context(nc.sbuf_tensor(name, shape, dt))

        w1_hi, w1_lo = sb("e1_hi", [D, NX, MH], F32R), sb("e1_lo", [D, NX, MH], F32R)
        w3_hi, w3_lo = sb("e3_hi", [D, NX, MH], F32R), sb("e3_lo", [D, NX, MH], F32R)
        w2_hi, w2_lo = sb("e2_hi", [D, NX, HALVES, D], F32R), sb("e2_lo", [D, NX, HALVES, D], F32R)
        gate_w, gate_b = sb("gate_w", [D, NE]), sb("gate_b", [G, GC, NE])
        iota = sb("iota_e", [G, GC, NE])
        cen32, cen = sb("mcen32", [D, D]), sb("mcen", [D, D], F32R)
        mean1, ident = sb("mmean1", [D, 1]), sb("mident", [D, D])
        sel = sb("msel", [40, NG, D], F32R)
        sel_c = sb("msel_c", [2 * GC * NE, GC * NE, D], F32R)

        s_w = sems("moe_weights_in")
        s_whi = sems("moe_w_hi")
        with ExitStack() as tmp:
            def sbt(name, shape):
                return tmp.enter_context(nc.sbuf_tensor(name, shape, F32))

            w132, w332, w232 = sbt("e1_32", [D, NX, MH]), sbt("e3_32", [D, NX, MH]), sbt("e2_32", [D, NX, HALVES, D])
            sel32, sel_c32 = sbt("msel32", [40, NG, D]), sbt("msel_c32", [2 * GC * NE, GC * NE, D])
            loads = [(w132, "e1"), (w332, "e3"), (w232, "e2"), (gate_w, "gate_w"), (gate_b, "gate_b"), (iota, "iota"),
                     (cen32, "cen"), (mean1, "mean1"), (ident, "ident"), (sel32, "sel"), (sel_c32, "sel_c")]
            with nc.Block() as block:
                @block.sync
                def _(sp):
                    for dst, name in loads:
                        sp.dma_start(dst[:], p[name]).then_inc(s_w, 16)

                @block.scalar
                def _(act):
                    act.wait_ge(s_w, 16 * len(loads))
                    nc.scalar.activation(w1_hi[:], w132[:], ACT.Copy).then_inc(s_whi, 1)
                    nc.scalar.activation(w3_hi[:], w332[:], ACT.Copy).then_inc(s_whi, 1)
                    nc.scalar.activation(w2_hi[:], w232[:], ACT.Copy).then_inc(s_whi, 1)
                    nc.scalar.activation(cen[:], cen32[:], ACT.Copy)

                @block.gpsimd
                def _(pool):
                    pool.wait_ge(s_w, 16 * len(loads))
                    nc.gpsimd.tensor_copy(sel_c[:], sel_c32[:])
                    nc.gpsimd.tensor_copy(sel[:], sel32[:])

                @block.vector
                def _(dve):
                    dve.wait_ge(s_w, 16 * len(loads))
                    for k, (lo, full, hi) in enumerate(((w1_lo, w132, w1_hi), (w3_lo, w332, w3_hi), (w2_lo, w232, w2_hi))):
                        dve.wait_ge(s_whi, k + 1)
                        nc.vector.tensor_tensor(lo[:], full[:], hi[:].bitcast(F32), ALU.subtract)

        t_hi, t_lo = sb("t_hi", [D, CH], F32R), sb("t_lo", [D, CH], F32R)
        xc, sq, xn = sb("xc", [D, CH]), sb("msq", [D, CH]), sb("mxn", [D, CH])
        n_hi = [sb(f"mn_hi{c}", [D, CH], F32R) for c in range(NCH)]
        n_lo = [sb(f"mn_lo{c}", [D, CH], F32R) for c in range(NCH)]
        small = [sb(f"mrs{k}", [G, GC]) for k in range(3)]
        packed, turned = sb("mpacked", [G, D], F32R), sb("mturned", [40, G], F32R)
        biased, raw = sb("biased", [G, GC, NE]), sb("raw", [G, GC, NE])
        top_b, top_r = sb("top_biased", [G, GC, NE]), sb("top_raw", [G, GC, NE])
        index, indexf = sb("top_index", [G, GC, NE], U32), sb("top_indexf", [G, GC, NE])
        prob, psumt, prec = sb("prob", [G, GC, 2]), sb("prob_sum", [G, GC]), sb("prob_rec", [G, GC])
        pn = sb("prob_n", [G, GC, 2])
        fence = sb("fence", [G, 2])
        comb, comb2 = sb("comb", [G, GC, NE]), sb("comb2", [G, GC, NE])
        packed_c, turned_c = sb("packed_c", [G, D], F32R), sb("turned_c", [2 * GC * NE, G], F32R)
        weight = [sb(f"weight{k}", [D, CH]) for k in range(2)]
        silu = [sb(f"silu{k}", [D, CH]) for k in range(2)]
        prod = [sb(f"prod{k}", [D, CH]) for k in range(DEPTH)]
        scaled = [sb(f"scaled{k}", [D, CH]) for k in range(DEPTH)]
        h_hi = [sb(f"h_hi{k}", [D, CH], F32R) for k in range(DEPTH)]
        h_lo = [sb(f"h_lo{k}", [D, CH], F32R) for k in range(DEPTH)]
        total = sb("total", [D, CH])
        rows = [sb(f"rows{c}", [G, GC, D]) for c in range(NCH)]
        acc = [mem.enter_context(nc.psum_tensor(f"acc{c}", [D, BANK], F32)) for c in range(NCH)]
        gate_ps = [mem.enter_context(nc.psum_tensor(f"up1_{k}", [D, BANK], F32)) for k in range(2)]
        lin_ps = [mem.enter_context(nc.psum_tensor(f"up3_{k}", [D, BANK], F32)) for k in range(2)]
        cbank = mem.enter_context(nc.psum_tensor("cbank", [D, BANK], F32))
        nbank = mem.enter_context(nc.psum_tensor("nbank", [D, BANK], F32))

        s_pad = sems("moe_pads")
        s_thi, s_tlo = sems("moe_t_hi"), sems("moe_t_lo")
        s_cen, s_xc, s_sq, s_var = sems("moe_centered"), sems("moe_xc"), sems("moe_squared"), sems("moe_var")
        s_newton, s_packed = sems("moe_newton"), sems("moe_packed")
        s_turnps, s_turn = sems("moe_turned_psum"), sems("moe_turned")
        s_spread, s_xn = sems("moe_spread"), sems("moe_normed")
        s_nhi, s_nlo = sems("moe_n_hi"), sems("moe_n_lo")
        s_gate, s_route, s_prob = sems("moe_scores"), sems("moe_route_steps"), sems("moe_prob")
        s_cturnps, s_cturn = sems("moe_comb_turned_psum"), sems("moe_comb_turned")
        s_cspread, s_weight = sems("moe_comb_spread"), sems("moe_weight")
        s_up, s_silu, s_prod = sems("moe_up"), sems("moe_silu"), sems("moe_prod")
        s_scaled = sems("moe_scaled")
        s_hhi, s_hlo = sems("moe_hidden_hi"), sems("moe_hidden_lo")
        s_acc, s_total = sems("moe_summed"), sems("moe_total")
        s_read = sems("moe_last_buffer_read")
        s_rowps, s_rows = sems("moe_rows_psum"), sems("moe_rows")
        s_out = [sems(f"moe_out_stored{c}") for c in range(NCH)]

        def tok_chunk(b, c):
            return tok[:, bass.ds(b, 1), c * CH:(c + 1) * CH].rearrange("p o n -> p (o n)")

        def before(b, c):
            return (b, 0) if c else (b - 1, 1)

        def after(b, c):
            return (b + 1, 0) if c else (b, 1)

        def run_chunks(fori, chunk):
            chunk(0, 0, True, False)
            with fori(0, NB - 1) as b:
                chunk(b, 1, False, False)
                chunk(b + 1, 0, False, False)
            chunk(NB - 1, 1, False, True)

        SPREAD_AT = {3: 1, **{2 * x: x for x in range(2, NX)}}

        with nc.Block() as block:
            @block.sync
            def _(sp):
                def store(b, c):
                    sp.wait_ge(s_rows, b * 2 + c + 1)
                    sp.dma_start(out[bass.ds(b, 1), c * CH:(c + 1) * CH, :].rearrange("o (g t) d -> t (o g) d", t=G),
                                 rows[c][:]).then_inc(s_out[c], 16)

                for c in range(NCH):
                    sp.sem_inc(s_out[c], 16)
                with sp.Fori(0, NB) as b:
                    for c in range(NCH):
                        store(b, c)
                for c in range(NCH):
                    sp.wait_ge(s_out[c], 16 * NB + 16)

            @block.gpsimd
            def _(pool):
                nc.gpsimd.memset(packed[:].bitcast(F32), 0.0).then_inc(s_pad, 1)
                nc.gpsimd.memset(packed_c[:].bitcast(F32), 0.0).then_inc(s_pad, 1)
                with pool.Fori(0, NB) as b:
                    for c in range(NCH):
                        q = b * 2 + c
                        for u in range(HALVES, UNITS):
                            x, k = u // HALVES, (2 * c + u) % DEPTH
                            pool.wait_ge(s_prod, q * UNITS + u + 1)
                            if u % HALVES == 0:
                                pool.wait_ge(s_weight, q * NE + x)
                            nc.gpsimd.tensor_tensor(scaled[k][:], prod[k][:], weight[x % 2][:], ALU.mult
                                                    ).then_inc(s_scaled, 1)

            @block.scalar
            def _(act):
                op = nc.scalar.activation

                def split(b, c, s):
                    U = (b * 2 + c) * UNITS + s
                    u, k = s % UNITS, (2 * c + s) % DEPTH
                    if u < HALVES:
                        act.wait_ge(s_prod, U + 1)
                        op(h_hi[k][:], prod[k][:], ACT.Copy).then_inc(s_hhi, 1)
                    else:
                        done = (b * 2 + c) * SCALED + (s - HALVES if s >= 0 else s)
                        act.wait_ge(s_scaled, done + 1)
                        op(h_hi[k][:], scaled[k][:], ACT.Copy).then_inc(s_hhi, 1)

                def prepare(b, c, step):
                    q = b * 2 + c
                    if step == "t_hi":
                        op(t_hi[:], tok_chunk(b, c), ACT.Copy).then_inc(s_thi, 1)
                    elif step == "square":
                        act.wait_ge(s_xc, q + 1)
                        op(sq[:], xc[:], ACT.Square).then_inc(s_sq, 1)
                    elif step == "n_hi":
                        act.wait_ge(s_xn, q + 1)
                        op(n_hi[c][:], xn[:], ACT.Copy).then_inc(s_nhi, 1)
                    elif step == "prob":
                        act.wait_ge(s_route, q * ROUTE + SORTED)
                        op(prob[:], top_r[:, :, 0:2], ACT.Sigmoid).then_inc(s_prob, 1)

                at = {0: "t_hi", 3: "square", 12: "n_hi", 14: "prob"}

                def chunk(b, c, first, last):
                    q = b * 2 + c
                    for s in range(UNITS):
                        act.wait_ge(s_up, q * UNITS + s + 1)
                        op(silu[s % 2][:], gate_ps[s % 2][:, 0:CH], ACT.Silu).then_inc(s_silu, 1)
                        if s >= HI_LAG or not first:
                            split(b, c, s - HI_LAG)
                        if s in SPREAD_AT:
                            x = SPREAD_AT[s]
                            act.wait_ge(s_cspread, q * NE + x)
                            op(weight[x % 2][:], cbank[:, 0:CH], ACT.Copy).then_inc(s_weight, 1)
                        if s in at and not last:
                            prepare(*after(b, c), at[s])
                        if s == 7 and not first:
                            send(*before(b, c))

                def send(b, c):
                    q = b * 2 + c
                    act.wait_ge(s_rowps, q + 1)
                    act.wait_ge(s_out[c], b * 16 + 16)
                    op(rows[c][:].rearrange("t g d -> t (g d)"), nbank[0:G, :], ACT.Copy).then_inc(s_rows, 1)

                for step in at.values():
                    prepare(0, 0, step)
                run_chunks(act.Fori, chunk)
                for s in range(UNITS - HI_LAG, UNITS):
                    if s == UNITS - 1:
                        act.wait_ge(s_read, NB * NCH)
                    split(NB - 1, 1, s)
                send(NB - 1, 1)

            @block.vector
            def _(dve):
                tt, stt = nc.vector.tensor_tensor, nc.vector.scalar_tensor_tensor

                def one(col, like=NE):
                    return col.unsqueeze(2).to_broadcast([G, GC, like])

                def make(b, c, s, first):
                    U, k = (b * 2 + c) * UNITS + s, (2 * c + s) % DEPTH
                    if s >= DEPTH or not first:
                        dve.wait_ge(s_hlo, U - DEPTH + 1)
                    dve.wait_ge(s_silu, U + 1)
                    tt(prod[k][:], lin_ps[s % 2][:, 0:CH], silu[s % 2][:], ALU.mult).then_inc(s_prod, 1)

                def rest(b, c, s):
                    k = (2 * c + s) % DEPTH
                    full = prod[k] if s % UNITS < HALVES else scaled[k]
                    dve.wait_ge(s_hhi, (b * 2 + c) * UNITS + s + 1)
                    tt(h_lo[k][:], full[:], h_hi[k][:].bitcast(F32), ALU.subtract).then_inc(s_hlo, 1)

                def newton(b, c, k):
                    q = b * 2 + c
                    if k == 0:
                        dve.wait_ge(s_var, q + 1)
                    elif k <= NEWTON:
                        dve.wait_ge(s_newton, q * NEWTON + k)
                    else:
                        dve.wait_ge(s_packed, q * 2 + 1)
                    if k < NEWTON:
                        rsqrt_step(nc.vector, k, nbank[0:G, 0:GC], small).then_inc(s_newton, 1)
                    elif k == NEWTON:
                        nc.vector.tensor_copy(packed[:, 0:GC], small[1][:]).then_inc(s_packed, 1)
                    else:
                        tt(packed[:, 32:32 + GC], small[1][:], packed[:, 0:GC].bitcast(F32), ALU.subtract
                           ).then_inc(s_packed, 1)

                def route(b, c, part):
                    q = b * 2 + c
                    k = [{0: 0, 1: SORTED, 2: SORTED + 2, 3: SORTED + 5, 4: SORTED + 7}[part]]

                    def link(ins):
                        k[0] += 1
                        ins.then_inc(s_route, 1)
                        dve.wait_ge(s_route, q * ROUTE + k[0])

                    if part == 0:
                        dve.wait_ge(s_gate, q + 1)
                        scores = nbank[0:G, 0:GC * NE].rearrange("t (g e) -> t g e", e=NE)
                        tt(biased[:], scores, gate_b[:], ALU.add)
                        link(nc.vector.tensor_copy(raw[:], scores))
                        nc.vector.memset(fence[:, 0:1], 0.0)
                        for g in range(GC):
                            nc.vector.max(top_b[:, g, :], biased[:, g, :])
                            ins = nc.vector.max(top_r[:, g, :], raw[:, g, :])
                        link(ins)
                        nc.vector.memset(fence[:, 1:2], 0.0)
                    elif part == 1:
                        for g in range(GC):
                            ins = nc.vector.max_index(index[:, g, :], top_b[:, g, :], biased[:, g, :])
                        link(ins)
                        link(nc.vector.tensor_copy(indexf[:], index[:]))
                        tt(comb[:], iota[:], one(indexf[:, :, 0]), ALU.is_equal)
                        tt(comb2[:], iota[:], one(indexf[:, :, 1]), ALU.is_equal)
                    elif part == 2:
                        dve.wait_ge(s_prob, q + 1)
                        link(tt(psumt[:], prob[:, :, 0], prob[:, :, 1], ALU.add))
                        link(nc.vector.reciprocal(prec[:], psumt[:]))
                        link(tt(pn[:], prob[:], one(prec[:], 2), ALU.mult))
                    elif part == 3:
                        tt(comb[:], comb[:], one(pn[:, :, 0]), ALU.mult)
                        link(tt(comb2[:], comb2[:], one(pn[:, :, 1]), ALU.mult))
                        link(tt(comb[:], comb[:], comb2[:], ALU.add))
                    elif part == 4:
                        flat = comb[:].rearrange("t g e -> t (g e)")
                        link(nc.vector.tensor_copy(packed_c[:, 0:GC * NE], flat))
                        link(tt(packed_c[:, GC * NE:2 * GC * NE], flat, packed_c[:, 0:GC * NE].bitcast(F32), ALU.subtract))
                        assert k[0] == ROUTE

                def prepare(b, c, step):
                    q = b * 2 + c
                    if step == "t_lo":
                        dve.wait_ge(s_thi, q + 1)
                        tt(t_lo[:], tok_chunk(b, c), t_hi[:].bitcast(F32), ALU.subtract).then_inc(s_tlo, 1)
                    elif step == "xc":
                        dve.wait_ge(s_cen, q + 1)
                        nc.vector.tensor_copy(xc[:], nbank[:, 0:CH]).then_inc(s_xc, 1)
                    elif step == "turned":
                        dve.wait_ge(s_turnps, q + 1)
                        nc.vector.tensor_copy(turned[:], nbank[0:40, 0:G]).then_inc(s_turn, 1)
                    elif step == "xn":
                        dve.wait_ge(s_spread, q + 1)
                        dve.wait_ge(s_xc, q + 1)
                        tt(xn[:], nbank[:, 0:CH], xc[:], ALU.mult).then_inc(s_xn, 1)
                    elif step == "n_lo":
                        dve.wait_ge(s_nhi, q + 1)
                        tt(n_lo[c][:], xn[:], n_hi[c][:].bitcast(F32), ALU.subtract).then_inc(s_nlo, 1)

                at = {0: "t_lo", 2: "xc", 9: "turned", 11: "xn", 13: "n_lo"}
                NEWTON_AT, A_SLOT, ROUTE_AT = 5, (NEWTON + 2 + 2) // 3, 13

                def finish(b, c):
                    dve.wait_ge(s_acc, b * 2 + c + 1)
                    tt(total[:], acc[c][:, 0:CH], tok_chunk(b, c), ALU.add).then_inc(s_total, 1)

                def chunk(b, c, first, last):
                    q = b * 2 + c
                    for s in range(UNITS):
                        steps = list(range(NEWTON + 2))[max(s - NEWTON_AT, 0) * A_SLOT:max(s - NEWTON_AT + 1, 0) * A_SLOT]
                        if last:
                            steps = []
                        make(b, c, s, first)
                        for k in steps[:A_SLOT // 2]:
                            newton(*after(b, c), k)
                        if s == 1:
                            dve.wait_ge(s_cturnps, q + 1)
                            nc.vector.tensor_copy(turned_c[:], cbank[0:2 * GC * NE, 0:G]).then_inc(s_cturn, 1)
                        if s >= HI_LAG or not first:
                            rest(b, c, s - HI_LAG)
                        for k in steps[A_SLOT // 2:]:
                            newton(*after(b, c), k)
                        if s == 4 and not first:
                            finish(*before(b, c))
                        if not last:
                            if s in at:
                                prepare(*after(b, c), at[s])
                            if s >= ROUTE_AT:
                                route(*after(b, c), s - ROUTE_AT)

                dve.sem_inc(s_total, 1)
                dve.wait_ge(s_pad, 2)
                for step in ("t_lo", "xc"):
                    prepare(0, 0, step)
                for k in range(NEWTON + 2):
                    newton(0, 0, k)
                for step in ("turned", "xn", "n_lo"):
                    prepare(0, 0, step)
                for part in range(5):
                    route(0, 0, part)
                run_chunks(dve.Fori, chunk)
                for s in range(UNITS - HI_LAG, UNITS):
                    rest(NB - 1, 1, s)
                finish(NB - 1, 1)

            @block.tensor
            def _(pe):
                def three(o, hi, lo, v_hi, v_lo, start=True, stop=True):
                    nc.tensor.matmul(o, hi, v_hi, start=start, stop=False)
                    nc.tensor.matmul(o, hi, v_lo, start=False, stop=False)
                    return nc.tensor.matmul(o, lo, v_hi, start=False, stop=stop)

                def up(b, c, s, first):
                    q, x, r = b * 2 + c, s // HALVES, s % HALVES
                    e, cols = expert[x], slice(r * D, (r + 1) * D)
                    if s == 0:
                        pe.wait_ge(s_nlo, q + 1)
                    if s >= 2 or not first:
                        pe.wait_ge(s_prod, q * UNITS + s - 1)
                    three(gate_ps[s % 2][:, 0:CH], w1_hi[:, e, cols], w1_lo[:, e, cols], n_hi[c][:], n_lo[c][:])
                    three(lin_ps[s % 2][:, 0:CH], w3_hi[:, e, cols], w3_lo[:, e, cols], n_hi[c][:], n_lo[c][:]
                          ).then_inc(s_up, 1)

                def down(b, c, s):
                    q, u, k = b * 2 + c, s % UNITS, (2 * c + s) % DEPTH
                    bank = acc[c if s >= 0 else 1 - c]
                    x, r = u // HALVES, u % HALVES
                    if u == 0 and not (isinstance(b, int) and b == 0 and c == 0):
                        pe.wait_ge(s_total, q)
                    pe.wait_ge(s_hlo, q * UNITS + s + 1)
                    mm = three(bank[:, 0:CH], w2_hi[:, expert[x], r, :], w2_lo[:, expert[x], r, :], h_hi[k][:], h_lo[k][:],
                               start=(u == 0), stop=(u == UNITS - 1))
                    if u == UNITS - 1:
                        mm.then_inc(s_acc, 1)
                    if u == UNITS - 1 - DEPTH:
                        mm.then_inc(s_read, 1)

                def prepare(b, c, step):
                    q = b * 2 + c
                    if step == "center":
                        pe.wait_ge(s_tlo, q + 1)
                        nc.tensor.matmul(nbank[:, 0:CH], cen[:], t_hi[:], start=True, stop=False)
                        nc.tensor.matmul(nbank[:, 0:CH], cen[:], t_lo[:], start=False, stop=True).then_inc(s_cen, 1)
                    elif step == "var":
                        pe.wait_ge(s_sq, q + 1)
                        for g in range(GC):
                            mm = nc.tensor.matmul(nbank[0:G, g:g + 1], sq[:, g * G:(g + 1) * G], mean1[:], start=True,
                                                  stop=True)
                        mm.then_inc(s_var, 1)
                    elif step == "turn":
                        pe.wait_ge(s_packed, q * 2 + 2)
                        nc.tensor.matmul(nbank[:, 0:G], packed[:].bitcast(F32), ident[0:G, 0:G], is_transpose=True,
                                         start=True, stop=True).then_inc(s_turnps, 1)
                    elif step == "spread":
                        pe.wait_ge(s_turn, q + 1)
                        for g in range(GC):
                            mm = nc.tensor.matmul(nbank[:, g * G:(g + 1) * G], sel[:, g, :], turned[:], start=True, stop=True)
                        mm.then_inc(s_spread, 1)
                    elif step == "gate":
                        pe.wait_ge(s_xn, q + 1)
                        for g in range(GC):
                            mm = nc.tensor.matmul(nbank[0:G, g * NE:(g + 1) * NE], xn[:, g * G:(g + 1) * G], gate_w[:],
                                                  start=True, stop=True)
                        mm.then_inc(s_gate, 1)

                def spread(q, x):
                    if x > 1:
                        pe.wait_ge(s_weight, q * NE + x - 1)
                    else:
                        pe.wait_ge(s_cturn, q + 1)
                    for g in range(GC):
                        mm = nc.tensor.matmul(cbank[:, g * G:(g + 1) * G], sel_c[:, g * NE + x - 1, :], turned_c[:],
                                              start=True, stop=True)
                    mm.then_inc(s_cspread, 1)

                def by_token(b, c):
                    pe.wait_ge(s_total, b * 2 + c + 2)
                    for g in range(GC):
                        mm = nc.tensor.matmul(nbank[0:G, g * D:(g + 1) * D], total[:, g * G:(g + 1) * G], ident[:],
                                              start=True, stop=True)
                    mm.then_inc(s_rowps, 1)

                at = {2: "center", 5: "var", 9: "turn", 11: "spread", 13: "gate"}

                def chunk(b, c, first, last):
                    q = b * 2 + c
                    for s in range(UNITS):
                        if s == 1:
                            pe.wait_ge(s_route, (q + 1) * ROUTE)
                            if not first:
                                pe.wait_ge(s_weight, q * NE)
                            nc.tensor.matmul(cbank[:, 0:G], packed_c[:].bitcast(F32), ident[0:G, 0:G], is_transpose=True,
                                             start=True, stop=True).then_inc(s_cturnps, 1)
                        if s in SPREAD_AT:
                            spread(q, SPREAD_AT[s])
                        if s in at and not last:
                            if at[s] == "turn" and not first:
                                pe.wait_ge(s_rows, q)
                            prepare(*after(b, c), at[s])
                        if s == 7 and not first:
                            if not last:
                                pe.wait_ge(s_newton, (q + 1) * NEWTON + 1)
                            by_token(*before(b, c))
                        up(b, c, s, first)
                        if s >= DOWN_LAG or not first:
                            down(b, c, s - DOWN_LAG)

                for step in at.values():
                    prepare(0, 0, step)
                run_chunks(pe.Fori, chunk)
                for s in range(UNITS - DOWN_LAG, UNITS):
                    down(NB - 1, 1, s)
                by_token(NB - 1, 1)


SORTED, ROUTE = 2, 11


def early_fusion(nc, x, txt, tok_w, tok_b, p, out):
    with ExitStack() as ctx:
        def sems(name):
            return ctx.enter_context(nc.semaphore(name))

        tok = ctx.enter_context(nc.sbuf_tensor("tok", [D, NB, S], F32))
        conv_phase(nc, sems, tok, x, txt, tok_w, tok_b)
        mixer_phase(nc, sems, tok, p)
        moe_phase(nc, sems, tok, out, p)


def kernel(**inputs):
    import numpy as np
    import concourse.bacc as _bacc
    from concourse.bass_utils import run_bass_kernel_spmd as _run

    a = {k: np.asarray(v) for k, v in inputs.items()}
    at = {k[len("L0_attn_"):]: v for k, v in a.items() if k.startswith("L0_attn_")}
    ff = {k[len("L0_ffn_"):]: v for k, v in a.items() if k.startswith("L0_ffn_")}
    sel = np.zeros((40, NG, D), np.float32)
    for g in range(NG):
        sel[g, g] = sel[32 + g, g] = 1.0
    sel_c = np.zeros((2 * GC * NE, GC * NE, D), np.float32)
    for k in range(GC * NE):
        sel_c[k, k] = sel_c[GC * NE + k, k] = 1.0
    arrays = {
        "x": a["x"].reshape(NB, D, HIN, WO, STR).transpose(0, 1, 2, 4, 3).reshape(NB, D, HIN * WIN),
        "txt": a["txt"].transpose(2, 0, 1),
        "tok_w": a["L0_tok_W"].reshape(D, D, KSZ * KSZ).transpose(1, 2, 0).reshape(D, KSZ * KSZ * D),
        "tok_b": a["L0_tok_b"].reshape(D, 1),
    }
    small = {
        "pw": at["conv_pw_w"].transpose(2, 0, 1),
        "pw0n": at["conv_pw_w"][0],
        "f": at["f_w"].transpose(2, 0, 1),
        "w1": at["mlp_w1"].transpose(2, 0, 1),
        "w2": at["mlp_w2"].reshape(LAYERS, D, HT, D).transpose(3, 0, 2, 1),
        "cen": (np.eye(D) - 1.0 / D).astype(np.float32),
        "mean1": np.full((D, 1), 1.0 / D, np.float32),
        "ident": np.eye(D, dtype=np.float32),
        "sel": sel,
        "sel_c": sel_c,
        "dw": at["conv_dw_w"].transpose(2, 0, 1),
        "dwb": at["conv_dw_b"].T,
        "pwb": at["conv_pw_b"].T,
        "ln1g": at["ln1_g"].reshape(D, 1),
        "ln1b": at["ln1_b"].reshape(D, 1),
        "ln2g": at["ln2_g"].T,
        "ln2b": at["ln2_b"].T,
        "b1": at["mlp_b1"].reshape(LAYERS * HT, D).T,
        "b2": at["mlp_b2"].T,
        "e1": np.concatenate([ff["w1"], ff["sw1"][None]]).transpose(1, 0, 2),
        "e3": np.concatenate([ff["w3"], ff["sw3"][None]]).transpose(1, 0, 2),
        "e2": np.concatenate([ff["w2"], ff["sw2"][None]]).reshape(NE + 1, MH // D, D, D).transpose(2, 0, 1, 3),
        "gate_w": ff["gate_w"].T,
        "gate_b": np.broadcast_to(ff["biases"], (G, GC, NE)),
        "iota": np.broadcast_to(np.arange(NE, dtype=np.float32), (G, GC, NE)),
    }
    nc = _bacc.Bacc("TRN2", target_bir_lowering=False, num_devices=1)
    feed, aps = {}, {}
    for name, v in {**arrays, **small}.items():
        feed["in_" + name] = np.ascontiguousarray(v)
        aps[name] = nc.dram_tensor("in_" + name, feed["in_" + name].shape, F32, kind="ExternalInput").ap()
    out = nc.dram_tensor("out", (NB, S, D), F32, kind="ExternalOutput").ap()
    early_fusion(nc, aps["x"], aps["txt"], aps["tok_w"], aps["tok_b"], aps, out)
    r = _run(nc, [feed], core_ids=[0])
    return r.results[0]["out"]
```

```python
from contextlib import ExitStack

import concourse.bass as bass
from concourse import mybir

F32 = mybir.dt.float32
F32R = mybir.dt.float32r
I32 = mybir.dt.int32
U32 = mybir.dt.uint32
ALU = mybir.AluOpType
ACT = mybir.ActivationFunctionType

NB, D = 16, 128
HIN, WIN = 60, 108
KSZ, STR, PAD = 7, 3, 3
HO, WO = 20, 36
TXT = 128
NIMG = HO * WO
S = NIMG + TXT
LAYERS, TAPS = 4, 4
HID = 512
HT = HID // D
NE, MH = 8, 256
EPS = 1e-5
RSQRT_SEED = 0x5F3759DF

NH = 2
ROWS_OUT = HO // NH
NHALF = ROWS_OUT * WO
ROWS_PAD = STR * (ROWS_OUT - 1) + KSZ
QW = WO + 2
HALF_IN = [(max(0, STR * ROWS_OUT * h - PAD), min(HIN, STR * ROWS_OUT * h - PAD + ROWS_PAD)) for h in range(NH)]
HALF_AT = [lo - (STR * ROWS_OUT * h - PAD) for h, (lo, _) in enumerate(HALF_IN)]

NCH = 2
CH = S // NCH
G = 106
NG = S // G
GC = CH // G
BANK = 512

def conv_phase(nc, sems, tok, x, txt, tok_w, tok_b):
    ntap = KSZ * KSZ
    wcut = [0, 25, ntap]
    with ExitStack() as mem:
        def sb(name, shape, dt=F32):
            return mem.enter_context(nc.sbuf_tensor(name, shape, dt))

        w_hi = sb("w_hi", [D, ntap, D], F32R)
        w_lo = sb("w_lo", [D, ntap, D], F32R)
        bias = sb("tok_bias", [D, 1])
        stage = [sb(f"x_stage{h}", [D, 33 * WIN]) for h in range(NH)]
        x_hi = [sb(f"x_hi{h}", [D, ROWS_PAD, STR, QW], F32R) for h in range(NH)]
        x_lo = [sb(f"x_lo{h}", [D, ROWS_PAD, STR, QW], F32R) for h in range(NH)]
        conv = [mem.enter_context(nc.psum_tensor(f"conv{h}", [D, BANK], F32)) for h in range(NH)]

        w_in = sems("w_in")
        small_in = sems("conv_small_in")
        x_in = [sems(f"x_in{h}") for h in range(NH)]
        w_hi_done = sems("w_hi_done")
        zeroed = sems("pads_zeroed")
        hi_done = [sems(f"x_hi_done{h}") for h in range(NH)]
        lo_done = [sems(f"x_lo_done{h}") for h in range(NH)]
        conv_done = [sems(f"conv_done{h}") for h in range(NH)]
        evac_done = [sems(f"conv_evacuated{h}") for h in range(NH)]

        nrow = [hi - lo for lo, hi in HALF_IN]
        cuts = [[n * k // 3 for k in range(4)] for n in nrow]

        def staged(h, a, b):
            return stage[h][:, a * WIN:b * WIN].rearrange("p (r s q) -> p r s q", s=STR, q=WO)

        def padded(buf, h, a, b):
            return buf[h][:, HALF_AT[h] + a:HALF_AT[h] + b, :, 1:1 + WO]

        with nc.Block() as block:
            @block.sync
            def _(sp):
                for k in range(2):
                    n = (wcut[k + 1] - wcut[k]) * D
                    sp.dma_start(stage[k][:, 0:n], tok_w[:, wcut[k] * D:wcut[k + 1] * D]).then_inc(w_in, 16)
                sp.dma_start(bias[:], tok_b).then_inc(small_in, 16)
                sp.dma_start(tok[:, :, NIMG:S], txt).then_inc(small_in, 16)
                with sp.Fori(0, NB) as b:
                    for h in range(NH):
                        sp.wait_ge(lo_done[h], b * 3 + 1)
                        r0, r1 = HALF_IN[h]
                        sp.dma_start(stage[h][:, 0:(r1 - r0) * WIN],
                                     x[bass.ds(b, 1), :, r0 * WIN:r1 * WIN].rearrange("o p n -> p (o n)")
                                     ).then_inc(x_in[h], 16)
                sp.wait_ge(small_in, 32)

            @block.gpsimd
            def _(pool):
                for h in range(NH):
                    nc.gpsimd.memset(x_hi[h][:].bitcast(F32), 0.0).then_inc(zeroed, 1)
                    nc.gpsimd.memset(x_lo[h][:].bitcast(F32), 0.0).then_inc(zeroed, 1)

            @block.scalar
            def _(act):
                for k in range(2):
                    act.wait_ge(w_in, 32)
                    n = (wcut[k + 1] - wcut[k]) * D
                    dst = w_hi[:, wcut[k]:wcut[k + 1], :].rearrange("p t c -> p (t c)")
                    nc.scalar.activation(dst, stage[k][:, 0:n], ACT.Copy).then_inc(w_hi_done, 1)

                def split_hi(h, b):
                    act.wait_ge(x_in[h], b * 16 + 16)
                    act.wait_ge(conv_done[h], b)
                    for k in range(3):
                        r0, r1 = cuts[h][k:k + 2]
                        nc.scalar.activation(padded(x_hi, h, r0, r1), staged(h, r0, r1),
                                             ACT.Copy).then_inc(hi_done[h], 1)

                def evacuate(h, b):
                    act.wait_ge(conv_done[h], b + 1)
                    nc.scalar.activation(tok[:, bass.ds(b, 1), h * NHALF:(h + 1) * NHALF].rearrange("p o n -> p (o n)"),
                                         conv[h][:, 0:NHALF], ACT.Identity, bias=bias[:, 0:1]).then_inc(evac_done[h], 1)

                act.wait_ge(small_in, 32)
                act.wait_ge(zeroed, 2 * NH)
                for h in range(NH):
                    act.sem_inc(evac_done[h], 1)
                for h in range(NH):
                    split_hi(h, 0)
                with act.Fori(0, NB - 1) as b:
                    for h in range(NH):
                        evacuate(h, b)
                        split_hi(h, b + 1)
                for h in range(NH):
                    evacuate(h, NB - 1)

            @block.vector
            def _(dve):
                for k in range(2):
                    dve.wait_ge(w_hi_done, k + 1)
                    n = (wcut[k + 1] - wcut[k]) * D
                    hi = w_hi[:, wcut[k]:wcut[k + 1], :].rearrange("p t c -> p (t c)")
                    lo = w_lo[:, wcut[k]:wcut[k + 1], :].rearrange("p t c -> p (t c)")
                    nc.vector.tensor_tensor(lo, stage[k][:, 0:n], hi.bitcast(F32), ALU.subtract).then_inc(lo_done[k], 1)
                dve.wait_ge(zeroed, 2 * NH)
                with dve.Fori(0, NB) as b:
                    for h in range(NH):
                        for k in range(3):
                            r0, r1 = cuts[h][k:k + 2]
                            dve.wait_ge(hi_done[h], b * 3 + k + 1)
                            nc.vector.tensor_tensor(padded(x_lo, h, r0, r1), staged(h, r0, r1),
                                                    padded(x_hi, h, r0, r1).bitcast(F32),
                                                    ALU.subtract).then_inc(lo_done[h], 1)

            @block.tensor
            def _(pe):
                def inside(kh, first):
                    ok = [r for r in range(ROWS_OUT) if 0 <= STR * (first + r) - PAD + kh < HIN]
                    return ok[0], ok[-1] + 1

                full = [(PAD, PAD), (PAD, PAD + 1)]
                rest = [(kh, kw) for kh in range(KSZ) for kw in range(KSZ) if (kh, kw) not in full]
                taps = full[:1] + rest + full[1:]
                for h in range(NH):
                    pe.wait_ge(lo_done[h], 1)
                with pe.Fori(0, NB) as b:
                    for h in range(NH):
                        pe.wait_ge(lo_done[h], b * 3 + 4)
                        pe.wait_ge(evac_done[h], b + 1)
                        for k, (kh, kw) in enumerate(taps):
                            t = kh * KSZ + kw
                            q, phase = divmod(kw - PAD, STR)
                            r0, r1 = inside(kh, h * ROWS_OUT)
                            rows = slice(kh + STR * r0, kh + STR * (r1 - 1) + 1, STR)
                            cols = slice(q + 1, q + 1 + WO)
                            hi, lo = x_hi[h][:, rows, phase, cols], x_lo[h][:, rows, phase, cols]
                            out = conv[h][:, r0 * WO:r1 * WO]
                            nc.tensor.matmul(out, w_hi[:, t, :], hi, start=(k == 0), stop=False)
                            nc.tensor.matmul(out, w_hi[:, t, :], lo, start=False, stop=False)
                            mm = nc.tensor.matmul(out, w_lo[:, t, :], hi, start=False, stop=(k == ntap - 1))
                        mm.then_inc(conv_done[h], 1)

NLN = 2 + LAYERS
STREAMS = 2 * NCH
COST = {"center": 0.72, "var": 0.7, "turn": 0.1, "spread": 0.43, "pw": 0.54, "kh": 1.08, "up": 0.54, "down": 0.71,
        "newton": 0.08, "pack_hi": 0.08, "pack_lo": 0.08, "turned": 0.18,
        "act": 0.42, "dve": 0.54, "pool": 1.1}
HOP, OWN_HOP = 0.3, 0.13
PERIOD = 206.5
SLACK = 0.1
LAGS = (0.0, 11.2, 6.5, 17.8)

def mixer_steps():
    out, index, done, free = [], {}, {}, {}

    def step(engine, kind, after, i=0, n=0, j=0):
        what = (kind, i, n, j)
        cost = COST[kind] if kind in COST else COST[engine]
        start = max([free.get(engine, 0.0)] + [done[a] + (OWN_HOP if out[index[a]][0] == engine else HOP) for a in after])
        free[engine] = done[what] = start + cost
        index[what] = len(out)
        out.append((engine, what, [index[a] for a in after], cost, start))
        return what

    def norm(i, n, centered):
        v = step("pe", "var", [step("act", "square", [centered], i, n)], i, n)
        for k in range(NEWTON):
            v = step("dve", "newton", [v], i, n, k)
        v = step("dve", "pack_lo", [step("dve", "pack_hi", [v], i, n)], i, n)
        t = step("dve", "turned", [step("pe", "turn", [v], i, n)], i, n)
        return step("dve", "normed", [step("act", "inv", [step("pe", "spread", [t], i, n)], i, n)], i, n)

    m = norm(0, 0, step("pe", "center", [step("dve", "split_lo", [step("act", "split_hi", [])])]))
    for i in range(LAYERS):
        y = step("act", "y0", [m], i)
        for k in range(TAPS - 1):
            y = step("dve", "tap", [y], i, j=k)
        pw = step("pe", "pw", [step("dve", "y_lo", [step("act", "y_hi", [y], i)], i)], i)
        if i == 0:
            lo = step("dve", "x1_lo", [step("act", "n_hi", [norm(0, 1, pw)], 0, 1)], 0, 1)
        else:
            lo = step("dve", "x_lo", [step("act", "x_hi", [pw], i)], i)
        kh = step("pe", "kh", [lo], i)
        cand = step("dve", "cand", [step("act", "g_cand", [kh], i)], i)
        take = step("dve", "take", [step("act", "g_take", [kh], i), cand], i)
        scan = step("dve", "scan", [step("act", "g_keep", [kh], i), take], i)
        lo = step("dve", "s_lo", [step("act", "s_hi", [scan], i)], i)
        xn = norm(i, 2 + i, step("pe", "center", [lo], i, 2 + i))
        lo = step("pool", "n_lo", [step("act", "n_hi", [xn], i, 2 + i)], i, 2 + i)
        ready = lo
        for j in range(HT):
            up = step("pe", "up", [ready], i, j=j)
            if j:
                step("pe", "down", [ready], i, j=j - 1)
            ready = step("dve" if j % 2 else "act", "relu", [up], i, j=j)
        down = step("pe", "down", [ready], i, j=HT - 1)
        m = step(*(("act", "out") if i < LAYERS - 1 else ("dve", "final")), [down], i)
    return out

def stream_order():
    steps = mixer_steps()
    busy, reached, ends, placed = {}, {}, {}, {}
    queue = {(q, e): [k for k, st in enumerate(steps) if st[0] == e] for e in ("pe", "act", "dve", "pool")
             for q in range(STREAMS)}

    def first_gap(q, k):
        engine, what, after, cost, _ = steps[k]
        needs = [(q, a) for a in after]
        if q % NCH and what[0] in ("tap", "scan"):
            needs.append((q - 1, k))
        if any(x not in ends for x in needs):
            return None
        t = max([LAGS[q], reached.get((q, engine), 0.0)] + [ends[x] + (OWN_HOP if steps[x[1]][0] == engine else HOP) for x in needs])
        t0, moved = t, True
        while moved:
            moved = False
            for b0, b1 in busy.setdefault(engine, []):
                for turn in (-PERIOD, 0.0, PERIOD):
                    at = t % PERIOD
                    if at < b1 + turn - 1e-9 and at + cost > b0 + turn + 1e-9:
                        t += b1 + turn - at
                        moved = True
            assert t < t0 + PERIOD
        return t

    while any(queue.values()):
        heads = [(first_gap(q, ks[0]), q, ks[0]) for (q, _), ks in queue.items() if ks]
        t, q, k = min((x for x in heads if x[0] is not None),
                      key=lambda x: (x[0] - SLACK * (x[0] - LAGS[x[1]] - steps[x[2]][4]), x[1]))
        engine, what, _, cost, _ = steps[k]
        queue[q, engine].pop(0)
        busy[engine].append((t % PERIOD, t % PERIOD + cost))
        ends[q, k] = reached[q, engine] = t + cost
        placed.setdefault(engine, []).append((t % PERIOD, q, t >= PERIOD, what))
    late = max(ends[q, k] - LAGS[q] for q, k in ends)
    assert late <= PERIOD, late
    return {e: [x[1:] for x in sorted(v)] for e, v in placed.items()}

def run_pairs(order, fori, do):
    for q, wraps, what in order:
        if not wraps:
            do(q, 0, *what)
    with fori(1, NB // 2) as it:
        for q, wraps, what in order:
            do(q, it - 1 if wraps else it, *what)
    for q, wraps, what in order:
        if wraps:
            do(q, NB // 2 - 1, *what)

NEWTON = 11

def rsqrt_step(eng, k, var, small):
    v, y, t = small
    if k == 0:
        return eng.tensor_scalar(v[:], var, EPS, None, ALU.add)
    if k == 1:
        return eng.tensor_scalar(y[:].bitcast(I32), v[:].bitcast(I32), -0.5, float(RSQRT_SEED), ALU.mult, ALU.add)
    k = (k - 2) % 3
    if k == 0:
        return eng.tensor_tensor(t[:], y[:], y[:], ALU.mult)
    if k == 1:
        return eng.scalar_tensor_tensor(out=t[:], in0=t[:], scalar=-0.5, in1=v[:], op0=ALU.mult, op1=ALU.mult)
    return eng.scalar_tensor_tensor(out=y[:], in0=t[:], scalar=1.5, in1=y[:], op0=ALU.add, op1=ALU.mult)

def mixer_phase(nc, sems, tok, p, stage, s_stage):
    order = stream_order()
    with ExitStack() as mem:
        def sb(name, shape, dt=F32):
            return mem.enter_context(nc.sbuf_tensor(name, shape, dt))

        pw_hi, pw_lo = sb("pw_hi", [D, LAYERS, D], F32R), sb("pw_lo", [D, LAYERS, D], F32R)
        f_hi, f_lo = sb("f_hi", [D, LAYERS, 2 * D], F32R), sb("f_lo", [D, LAYERS, 2 * D], F32R)
        w1_hi, w1_lo = sb("w1_hi", [D, LAYERS, HID], F32R), sb("w1_lo", [D, LAYERS, HID], F32R)
        w2 = sb("w2", [D, LAYERS, HT, D])
        cen32, cen = sb("cen32", [D, D]), sb("cen", [D, D], F32R)
        mean1 = sb("mean1", [D, 1])
        ident = sb("ident", [D, D])
        sel = sb("sel", [40, NG, D], F32R)
        dw, dwb = sb("dw", [D, LAYERS, TAPS]), sb("dwb", [D, LAYERS])
        pwb, pwb_c = sb("pwb", [D, LAYERS]), sb("pwb_c", [D, 1])
        ln1g, ln1b = sb("ln1g", [D, 1]), sb("ln1b", [D, 1])
        ln2g, ln2b = sb("ln2g", [D, LAYERS]), sb("ln2b", [D, LAYERS])
        b1, b1f = sb("b1", [D, LAYERS * HT]), sb("b1f", [D, LAYERS * HT])
        b2 = sb("b2", [D, LAYERS])

        psum = [[mem.enter_context(nc.psum_tensor(f"ps{q}_{k}", [D, BANK], F32)) for k in range(2)] for q in range(STREAMS)]

        with ExitStack() as tmp:
            def sbt(name, shape, dt=F32):
                return tmp.enter_context(nc.sbuf_tensor(name, shape, dt))

            pw32, pw0n = sbt("pw32", [D, LAYERS, D]), sbt("pw0n", [D, D])
            f32, w132 = sbt("f32", [D, LAYERS, 2 * D]), sbt("w132", [D, LAYERS, HID])
            sel32 = sbt("sel32", [40, NG, D])
            loads = [(pw32, "pw"), (pw0n, "pw0n"), (f32, "f"), (w132, "w1"), (w2, "w2"), (cen32, "cen"),
                     (mean1, "mean1"), (ident, "ident"), (sel32, "sel"), (dw, "dw"), (dwb, "dwb"), (pwb, "pwb"),
                     (ln1g, "ln1g"), (ln1b, "ln1b"), (ln2g, "ln2g"), (ln2b, "ln2b"), (b1, "b1"), (b2, "b2")]
            loaded = sems("mixer_weights_in")
            folded = sems("mixer_folded_psum")
            hi_done = sems("mixer_w_hi")
            with nc.Block() as block:
                @block.sync
                def _(sp):
                    for dst, name in loads:
                        sp.dma_start(dst[:], p[name]).then_inc(loaded, 16)

                @block.tensor
                def _(pe):
                    pe.wait_ge(loaded, 16 * len(loads))
                    nc.tensor.matmul(psum[0][0][:, 0:D], pw0n[:], cen32[:], start=True, stop=True)
                    nc.tensor.matmul(psum[0][1][:, 0:1], cen32[:], pwb[:, 0:1], start=True, stop=True)
                    for i in range(LAYERS):
                        for j in range(HT):
                            mm = nc.tensor.matmul(psum[1][0][:, i * HT + j:i * HT + j + 1],
                                                  w132[:, i, j * D:(j + 1) * D], ln2b[:, i:i + 1], start=True, stop=True)
                    mm.then_inc(folded, 1)

                @block.scalar
                def _(act):
                    act.wait_ge(loaded, 16 * len(loads))
                    nc.scalar.activation(cen[:], cen32[:], ACT.Copy)
                    nc.scalar.activation(sel[:], sel32[:], ACT.Copy)
                    nc.scalar.activation(pw_hi[:, 1:LAYERS, :], pw32[:, 1:LAYERS, :], ACT.Copy)
                    nc.scalar.activation(f_hi[:], f32[:], ACT.Copy)
                    for i in range(LAYERS):
                        nc.scalar.activation(w1_hi[:, i, :], w132[:, i, :], ACT.Copy, scale=ln2g[:, i:i + 1])
                    act.wait_ge(folded, 1)
                    nc.scalar.activation(pw_hi[:, 0, :], psum[0][0][:, 0:D], ACT.Copy)
                    nc.scalar.activation(pwb_c[:], psum[0][1][:, 0:1], ACT.Copy).then_inc(hi_done, 1)

                @block.vector
                def _(dve):
                    dve.wait_ge(hi_done, 1)
                    nc.vector.tensor_tensor(pw_lo[:, 1:LAYERS, :], pw32[:, 1:LAYERS, :],
                                            pw_hi[:, 1:LAYERS, :].bitcast(F32), ALU.subtract)
                    nc.vector.tensor_tensor(f_lo[:], f32[:], f_hi[:].bitcast(F32), ALU.subtract)
                    for i in range(LAYERS):
                        nc.vector.scalar_tensor_tensor(out=w1_lo[:, i, :], in0=w132[:, i, :], scalar=ln2g[:, i:i + 1],
                                                       in1=w1_hi[:, i, :].bitcast(F32), op0=ALU.mult, op1=ALU.subtract)
                    nc.vector.tensor_tensor(pw_lo[:, 0, :], psum[0][0][:, 0:D], pw_hi[:, 0, :].bitcast(F32), ALU.subtract)
                    nc.vector.tensor_tensor(b1f[:], psum[1][0][:, 0:LAYERS * HT], b1[:], ALU.add)

        class Stream:
            pass

        streams = []
        batch_m = [sb(f"m{s}", [D, TAPS - 1 + S]) for s in range(2)]
        for q in range(STREAMS):
            w = Stream()
            w.c = q % NCH
            w.m = batch_m[q // NCH][:, w.c * CH:w.c * CH + TAPS - 1 + CH]
            w.y = sb(f"y{q}", [D, CH])
            w.y_hi, w.y_lo = sb(f"y_hi{q}", [D, CH], F32R), sb(f"y_lo{q}", [D, CH], F32R)
            w.x_hi, w.x_lo = sb(f"xx_hi{q}", [D, CH], F32R), sb(f"xx_lo{q}", [D, CH], F32R)
            w.keep = sb(f"keep{q}", [D, CH])
            w.take = sb(f"take{q}", [D, CH])
            w.cand = sb(f"cand{q}", [D, CH])
            w.hid = sb(f"hid{q}", [D, 2, CH])
            w.small = [sb(f"rs{k}_{q}", [G, GC]) for k in range(3)]
            w.packed = sb(f"packed{q}", [G, D], F32R)
            w.turned = sb(f"turned{q}", [40, G], F32R)
            w.main, w.side = psum[q]
            w.main_done = sems(f"s{q}_main_bank")
            w.squared = sems(f"s{q}_squared")
            w.var = sems(f"s{q}_var")
            w.newton = sems(f"s{q}_newton")
            w.turned_ps = sems(f"s{q}_turned_psum")
            w.turned_done = sems(f"s{q}_turned")
            w.spread = sems(f"s{q}_spread")
            w.spread_done = sems(f"s{q}_spread_copied")
            w.normed = sems(f"s{q}_normed")
            w.n_lo = sems(f"s{q}_normed_lo")
            w.dw0 = sems(f"s{q}_dw_first")
            w.dw = sems(f"s{q}_dw_taps")
            w.y_hi_done = sems(f"s{q}_y_hi")
            w.y_lo_done = sems(f"s{q}_y_lo")
            w.x_hi_done = sems(f"s{q}_x_hi")
            w.x_lo_done = sems(f"s{q}_x_lo")
            w.kh = sems(f"s{q}_kh")
            w.gates = sems(f"s{q}_gates")
            w.take_done = sems(f"s{q}_taken")
            w.scan = sems(f"s{q}_scan")
            w.up = sems(f"s{q}_mlp_up")
            w.relu_a = sems(f"s{q}_relu_act")
            w.relu_v = sems(f"s{q}_relu_dve")
            w.down = sems(f"s{q}_mlp_down")
            w.m_done = sems(f"s{q}_mlp_out")
            streams.append(w)

        pads = sems("mixer_pads")
        NY = 1 + 2 * LAYERS
        NM = 1 + 2 * LAYERS
        NSTEP = NEWTON + 2

        def tok_chunk(it, q):
            c = q % NCH
            return tok[:, bass.ds(it * 2 + q // NCH, 1), c * CH:(c + 1) * CH].rearrange("p o n -> p (o n)")

        with nc.Block() as block:
            @block.sync
            def _(sp):
                for name, dst in stage.items():
                    sp.dma_start(dst[:], p[name]).then_inc(s_stage, 16)

            @block.gpsimd
            def _(pool):
                for m in batch_m:
                    nc.gpsimd.memset(m[:, 0:TAPS - 1], 0.0).then_inc(pads, 1)
                for w in streams:
                    nc.gpsimd.memset(w.packed[:].bitcast(F32), 0.0).then_inc(pads, 1)

                def do(q, it, kind, i, n, j):
                    w = streams[q]
                    pool.wait_ge(w.x_hi_done, (it * LAYERS + i) * 2 + 2)
                    nc.gpsimd.tensor_tensor(w.x_lo[:], w.cand[:], w.x_hi[:].bitcast(F32), ALU.subtract).then_inc(w.n_lo, 1)

                run_pairs(order["pool"], pool.Fori, do)

            @block.tensor
            def _(pe):
                def three(out, w_hi, w_lo, hi, lo):
                    nc.tensor.matmul(out, w_hi, hi, start=True, stop=False)
                    nc.tensor.matmul(out, w_hi, lo, start=False, stop=False)
                    return nc.tensor.matmul(out, w_lo, hi, start=False, stop=True)

                def do(q, it, kind, i, n, j):
                    w = streams[q]
                    e, en = it * LAYERS + i, it * NLN + n
                    ey, em = it * NY + 2 * i + 1, it * NM + 2 * i
                    main, side = w.main[:, 0:CH], w.side[:, 0:CH]
                    if kind == "center":
                        if n == 0:
                            pe.wait_ge(w.y_lo_done, it * NY + 1)
                            parts = [w.y_hi, w.y_lo]
                        else:
                            pe.wait_ge(w.y_lo_done, ey + 2)
                            parts = [w.y_hi, w.y_lo, w.x_hi, w.x_lo]
                        for k, part in enumerate(parts):
                            mm = nc.tensor.matmul(main, cen[:], part[:], start=(k == 0), stop=(k == len(parts) - 1))
                        mm.then_inc(w.main_done, 1)
                    elif kind == "var":
                        pe.wait_ge(w.squared, en + 1)
                        for g in range(GC):
                            mm = nc.tensor.matmul(w.side[0:G, g:g + 1], w.keep[:, g * G:(g + 1) * G], mean1[:], start=True,
                                                  stop=True)
                        mm.then_inc(w.var, 1)
                    elif kind == "turn":
                        pe.wait_ge(w.newton, (en + 1) * NSTEP)
                        nc.tensor.matmul(w.side[:, 0:G], w.packed[:].bitcast(F32), ident[0:G, 0:G], is_transpose=True,
                                         start=True, stop=True).then_inc(w.turned_ps, 1)
                    elif kind == "spread":
                        pe.wait_ge(w.turned_done, en + 1)
                        for g in range(GC):
                            mm = nc.tensor.matmul(w.side[:, g * G:(g + 1) * G], sel[:, g, :], w.turned[:], start=True,
                                                  stop=True)
                        mm.then_inc(w.spread, 1)
                    elif kind == "pw":
                        pe.wait_ge(w.y_lo_done, ey + 1)
                        mm = three(main, pw_hi[:, i, :], pw_lo[:, i, :], w.y_hi[:], w.y_lo[:])
                        mm.then_inc(w.main_done, 1)
                    elif kind == "kh":
                        pe.wait_ge(w.x_lo_done, e + 1)
                        for out, cols in ((side, slice(0, D)), (main, slice(D, 2 * D))):
                            mm = three(out, f_hi[:, i, cols], f_lo[:, i, cols], w.x_hi[:], w.x_lo[:])
                        mm.then_inc(w.kh, 1)
                    elif kind == "up":
                        if j == 0:
                            pe.wait_ge(w.n_lo, e + 1)
                        else:
                            pe.wait_ge(w.relu_a if j % 2 else w.relu_v, e * (HT // 2) + (j - 1) // 2 + 1)
                        cols = slice(j * D, (j + 1) * D)
                        three(side, w1_hi[:, i, cols], w1_lo[:, i, cols], w.x_hi[:], w.x_lo[:]).then_inc(w.up, 1)
                    elif kind == "down":
                        pe.wait_ge(w.relu_v if j % 2 else w.relu_a, e * (HT // 2) + j // 2 + 1)
                        nc.tensor.matmul(main, w2[:, i, j, :], w.hid[:, j % 2, :], start=(j == 0), stop=(j == HT - 1)
                                         ).then_inc(w.down, 1)

                pe.wait_ge(pads, 2 + STREAMS)
                run_pairs(order["pe"], pe.Fori, do)

            @block.scalar
            def _(act):
                def do(q, it, kind, i, n, j):
                    w = streams[q]
                    e, en = it * LAYERS + i, it * NLN + n
                    ey, em = it * NY + 2 * i + 1, it * NM + 2 * i
                    main, side = w.main[:, 0:CH], w.side[:, 0:CH]
                    op = nc.scalar.activation
                    if kind == "split_hi":
                        op(w.y_hi[:], tok_chunk(it, q), ACT.Copy).then_inc(w.y_hi_done, 1)
                    elif kind == "square":
                        act.wait_ge(w.main_done, it * NM + n + 1 if n < 2 else em + 3)
                        op(w.keep[:], main, ACT.Square, bias=pwb_c[:, 0:1] if n == 1 else 0.0).then_inc(w.squared, 1)
                    elif kind == "inv":
                        act.wait_ge(w.spread, en + 1)
                        op(w.take[:], side, ACT.Copy, scale=ln1g[:, 0:1] if n == 1 else 1.0).then_inc(w.spread_done, 1)
                    elif kind == "n_hi" and n == 1:
                        act.wait_ge(w.normed, en + 1)
                        op(w.x_hi[:], w.cand[:], ACT.Identity, bias=ln1b[:, 0:1]).then_inc(w.x_hi_done, 1)
                    elif kind == "n_hi":
                        act.wait_ge(w.normed, en + 1)
                        op(w.x_hi[:], w.cand[:], ACT.Copy).then_inc(w.x_hi_done, 1)
                    elif kind == "y0":
                        if i == 0:
                            act.wait_ge(w.normed, it * NLN + 1)
                        else:
                            act.wait_ge(w.m_done, it * (LAYERS - 1) + i)
                        if w.c < NCH - 1:
                            act.wait_ge(streams[q + 1].scan, e + 1)
                        op(w.y[:], w.m[:, TAPS - 1:], ACT.Identity, scale=dw[:, i, TAPS - 1:TAPS], bias=dwb[:, i:i + 1]
                           ).then_inc(w.dw0, 1)
                    elif kind == "y_hi":
                        act.wait_ge(w.dw, (e + 1) * (TAPS - 1) + 1)
                        op(w.y_hi[:], w.y[:], ACT.Copy).then_inc(w.y_hi_done, 1)
                    elif kind == "x_hi":
                        act.wait_ge(w.main_done, em + 2)
                        op(w.x_hi[:], main, ACT.Identity, bias=pwb[:, i:i + 1]).then_inc(w.x_hi_done, 1)
                    elif kind == "g_cand":
                        act.wait_ge(w.kh, e + 1)
                        op(w.cand[:], main, ACT.Sigmoid).then_inc(w.gates, 1)
                    elif kind == "g_take":
                        op(w.take[:], side, ACT.Sigmoid).then_inc(w.gates, 1)
                    elif kind == "g_keep":
                        op(w.keep[:], side, ACT.Sigmoid, scale=-1.0).then_inc(w.gates, 1)
                    elif kind == "s_hi":
                        act.wait_ge(w.scan, e + 2)
                        op(w.y_hi[:], w.y[:], ACT.Copy).then_inc(w.y_hi_done, 1)
                    elif kind == "relu":
                        act.wait_ge(w.up, e * HT + j + 1)
                        if j >= 2:
                            act.wait_ge(w.down, e * HT + j - 1)
                        op(w.hid[:, j % 2, :], side, ACT.Relu, bias=b1f[:, i * HT + j:i * HT + j + 1]).then_inc(w.relu_a, 1)
                    elif kind == "out":
                        act.wait_ge(w.down, (e + 1) * HT)
                        if w.c < NCH - 1:
                            act.wait_ge(streams[q + 1].dw, (e + 1) * (TAPS - 1) + 1)
                        op(w.m[:, TAPS - 1:], main, ACT.Identity, bias=b2[:, i:i + 1]).then_inc(w.m_done, 1)

                act.wait_ge(pads, 2 + STREAMS)
                run_pairs(order["act"], act.Fori, do)

            @block.vector
            def _(dve):
                tt, stt = nc.vector.tensor_tensor, nc.vector.scalar_tensor_tensor

                def do(q, it, kind, i, n, j):
                    w = streams[q]
                    e, en = it * LAYERS + i, it * NLN + n
                    ey, em = it * NY + 2 * i + 1, it * NM + 2 * i
                    main, side = w.main[:, 0:CH], w.side[:, 0:CH]
                    if kind == "split_lo":
                        dve.wait_ge(w.y_hi_done, it * NY + 1)
                        tt(w.y_lo[:], tok_chunk(it, q), w.y_hi[:].bitcast(F32), ALU.subtract).then_inc(w.y_lo_done, 1)
                    elif kind == "newton":
                        if j == 0:
                            dve.wait_ge(w.var, en + 1)
                        else:
                            dve.wait_ge(w.newton, en * NSTEP + j)
                        rsqrt_step(nc.vector, j, w.side[0:G, 0:GC], w.small).then_inc(w.newton, 1)
                    elif kind == "pack_hi":
                        dve.wait_ge(w.newton, en * NSTEP + NEWTON)
                        nc.vector.tensor_copy(w.packed[:, 0:GC], w.small[1][:]).then_inc(w.newton, 1)
                    elif kind == "pack_lo":
                        dve.wait_ge(w.newton, en * NSTEP + NEWTON + 1)
                        tt(w.packed[:, 32:32 + GC], w.small[1][:], w.packed[:, 0:GC].bitcast(F32), ALU.subtract
                           ).then_inc(w.newton, 1)
                    elif kind == "turned":
                        dve.wait_ge(w.turned_ps, en + 1)
                        nc.vector.tensor_copy(w.turned[:], w.side[0:40, 0:G]).then_inc(w.turned_done, 1)
                    elif kind == "normed":
                        dve.wait_ge(w.spread_done, en + 1)
                        if n == 0:
                            if w.c < NCH - 1:
                                dve.wait_ge(streams[q + 1].dw, it * LAYERS * (TAPS - 1) + 1)
                            tt(w.m[:, TAPS - 1:], main, w.take[:], ALU.mult).then_inc(w.normed, 1)
                        elif n == 1:
                            stt(out=w.cand[:], in0=main, scalar=pwb_c[:, 0:1], in1=w.take[:], op0=ALU.add, op1=ALU.mult
                                ).then_inc(w.normed, 1)
                        else:
                            tt(w.cand[:], main, w.take[:], ALU.mult).then_inc(w.normed, 1)
                    elif kind == "x1_lo":
                        dve.wait_ge(w.x_hi_done, e * 2 + 1)
                        stt(out=w.x_lo[:], in0=w.cand[:], scalar=ln1b[:, 0:1], in1=w.x_hi[:].bitcast(F32), op0=ALU.add,
                            op1=ALU.subtract).then_inc(w.x_lo_done, 1)
                    elif kind == "tap":
                        if j == 0:
                            dve.wait_ge(w.dw0, e + 1)
                            if w.c:
                                if i == 0:
                                    dve.wait_ge(streams[q - 1].normed, it * NLN + 1)
                                else:
                                    dve.wait_ge(streams[q - 1].m_done, it * (LAYERS - 1) + i)
                        else:
                            dve.wait_ge(w.dw, e * (TAPS - 1) + j + 1)
                        stt(out=w.y[:], in0=w.m[:, j:j + CH], scalar=dw[:, i, j:j + 1], in1=w.y[:], op0=ALU.mult, op1=ALU.add
                            ).then_inc(w.dw, 1)
                    elif kind == "y_lo":
                        dve.wait_ge(w.y_hi_done, ey + 1)
                        tt(w.y_lo[:], w.y[:], w.y_hi[:].bitcast(F32), ALU.subtract).then_inc(w.y_lo_done, 1)
                    elif kind == "x_lo":
                        dve.wait_ge(w.x_hi_done, e * 2 + 1)
                        stt(out=w.x_lo[:], in0=main, scalar=pwb[:, i:i + 1], in1=w.x_hi[:].bitcast(F32), op0=ALU.add,
                            op1=ALU.subtract).then_inc(w.x_lo_done, 1)
                    elif kind == "cand":
                        dve.wait_ge(w.gates, e * 3 + 1)
                        stt(out=w.cand[:], in0=main, scalar=0.5, in1=w.cand[:], op0=ALU.add, op1=ALU.max
                            ).then_inc(w.take_done, 1)
                    elif kind == "take":
                        dve.wait_ge(w.gates, e * 3 + 2)
                        dve.wait_ge(w.take_done, e * 2 + 1)
                        tt(w.take[:], w.take[:], w.cand[:], ALU.mult).then_inc(w.take_done, 1)
                    elif kind == "scan":
                        dve.wait_ge(w.gates, e * 3 + 3)
                        dve.wait_ge(w.take_done, e * 2 + 2)
                        if w.c:
                            dve.wait_ge(streams[q - 1].scan, e + 2)
                        first = streams[q - 1].y[:, CH - 1:CH] if w.c else 0.5
                        nc.vector.tensor_tensor_scan(w.y[:], w.keep[:], w.take[:], first, ALU.mult, ALU.add
                                                     ).then_inc(w.scan, 1)
                    elif kind == "s_lo":
                        dve.wait_ge(w.y_hi_done, ey + 2)
                        tt(w.y_lo[:], w.y[:], w.y_hi[:].bitcast(F32), ALU.subtract).then_inc(w.y_lo_done, 1)
                    elif kind == "relu":
                        dve.wait_ge(w.up, e * HT + j + 1)
                        if j >= 2:
                            dve.wait_ge(w.down, e * HT + j - 1)
                        nc.vector.tensor_scalar(w.hid[:, j % 2, :], side, b1f[:, i * HT + j:i * HT + j + 1], 0.0, ALU.add,
                                                ALU.max).then_inc(w.relu_v, 1)
                    elif kind == "final":
                        dve.wait_ge(w.down, (e + 1) * HT)
                        stt(out=tok_chunk(it, q), in0=main, scalar=b2[:, i:i + 1], in1=tok_chunk(it, q), op0=ALU.add,
                            op1=ALU.add)

                for w in streams:
                    dve.sem_inc(w.dw, 1)
                    dve.sem_inc(w.scan, 1)
                dve.wait_ge(pads, 2 + STREAMS)
                run_pairs(order["dve"], dve.Fori, do)

def moe_staging(nc, sems, mem):
    def sb(name, shape):
        return mem.enter_context(nc.sbuf_tensor(name, shape, F32))

    stage = {"e1": sb("e1_32", [D, NE + 1, MH]), "e3": sb("e3_32", [D, NE + 1, MH]),
             "e2": sb("e2_32", [D, NE + 1, MH // D, D])}
    return stage, sems("moe_experts_in")

def moe_phase(nc, sems, tok, out, p, stage, s_stage):
    NX = NE + 1
    HALVES = MH // D
    UNITS = NX * HALVES
    SCALED = NE * HALVES
    HI_LAG, DOWN_LAG, DEPTH = 2, 4, 4
    expert = [NE] + list(range(NE))
    with ExitStack() as mem:
        def sb(name, shape, dt=F32):
            return mem.enter_context(nc.sbuf_tensor(name, shape, dt))

        w1_hi, w1_lo = sb("e1_hi", [D, NX, MH], F32R), sb("e1_lo", [D, NX, MH], F32R)
        w3_hi, w3_lo = sb("e3_hi", [D, NX, MH], F32R), sb("e3_lo", [D, NX, MH], F32R)
        w2_hi, w2_lo = sb("e2_hi", [D, NX, HALVES, D], F32R), sb("e2_lo", [D, NX, HALVES, D], F32R)
        gate_w, gate_b = sb("gate_w", [D, NE]), sb("gate_b", [G, GC, NE])
        iota = sb("iota_e", [G, GC, NE])
        cen32, cen = sb("mcen32", [D, D]), sb("mcen", [D, D], F32R)
        mean1, ident = sb("mmean1", [D, 1]), sb("mident", [D, D])
        sel = sb("msel", [40, NG, D], F32R)

        s_w = sems("moe_weights_in")
        s_whi = sems("moe_w_hi")
        w132, w332, w232 = stage["e1"], stage["e3"], stage["e2"]
        with ExitStack() as tmp:
            sel32 = tmp.enter_context(nc.sbuf_tensor("msel32", [40, NG, D], F32))
            loads = [(gate_w, "gate_w"), (gate_b, "gate_b"), (iota, "iota"), (cen32, "cen"), (mean1, "mean1"),
                     (ident, "ident"), (sel32, "sel")]
            with nc.Block() as block:
                @block.sync
                def _(sp):
                    for dst, name in loads:
                        sp.dma_start(dst[:], p[name]).then_inc(s_w, 16)

                @block.scalar
                def _(act):
                    act.wait_ge(s_stage, 16 * len(stage))
                    nc.scalar.activation(w1_hi[:], w132[:], ACT.Copy).then_inc(s_whi, 1)
                    nc.scalar.activation(w3_hi[:], w332[:], ACT.Copy).then_inc(s_whi, 1)
                    nc.scalar.activation(w2_hi[:], w232[:], ACT.Copy).then_inc(s_whi, 1)
                    act.wait_ge(s_w, 16 * len(loads))
                    nc.scalar.activation(cen[:], cen32[:], ACT.Copy)

                @block.gpsimd
                def _(pool):
                    pool.wait_ge(s_w, 16 * len(loads))
                    nc.gpsimd.tensor_copy(sel[:], sel32[:])

                @block.vector
                def _(dve):
                    dve.wait_ge(s_stage, 16 * len(stage))
                    for k, (lo, full, hi) in enumerate(((w1_lo, w132, w1_hi), (w3_lo, w332, w3_hi), (w2_lo, w232, w2_hi))):
                        dve.wait_ge(s_whi, k + 1)
                        nc.vector.tensor_tensor(lo[:], full[:], hi[:].bitcast(F32), ALU.subtract)

        t_hi, t_lo = sb("t_hi", [D, CH], F32R), sb("t_lo", [D, CH], F32R)
        xc, sq, xn = sb("xc", [D, CH]), sb("msq", [D, CH]), sb("mxn", [D, CH])
        n_hi = [sb(f"mn_hi{c}", [D, CH], F32R) for c in range(NCH)]
        n_lo = [sb(f"mn_lo{c}", [D, CH], F32R) for c in range(NCH)]
        small = [sb(f"mrs{k}", [G, GC]) for k in range(3)]
        packed, turned = sb("mpacked", [G, D], F32R), sb("mturned", [40, G], F32R)
        biased, raw = sb("biased", [G, GC, NE]), sb("raw", [G, GC, NE])
        top_b, top_r = sb("top_biased", [G, GC, NE]), sb("top_raw", [G, GC, NE])
        index, indexf = sb("top_index", [G, GC, NE], U32), sb("top_indexf", [G, GC, NE])
        prob, psumt, prec = sb("prob", [G, GC, 2]), sb("prob_sum", [G, GC]), sb("prob_rec", [G, GC])
        pn = sb("prob_n", [G, GC, 2])
        mag, is_far, is_near, inv_mag = (sb(f"score_{n}", [G, GC, 2]) for n in ("abs", "far", "near", "inv_abs"))
        silu_s, tanh_s, near_s, far_s = (sb(f"score_{n}", [G, GC, 2]) for n in ("silu", "tanh", "sig_near", "sig_far"))
        fence = sb("fence", [G, 2])
        comb, comb2 = sb("comb", [G, GC, NE]), sb("comb2", [G, GC, NE])
        packed_c, turned_c = sb("packed_c", [G, GC, D], F32R), sb("turned_c", [40, CH], F32R)
        weight = [sb(f"weight{k}", [D, CH]) for k in range(2)]
        silu = [sb(f"silu{k}", [D, CH]) for k in range(2)]
        prod = [sb(f"prod{k}", [D, CH]) for k in range(DEPTH)]
        scaled = [sb(f"scaled{k}", [D, CH]) for k in range(DEPTH)]
        h_hi = [sb(f"h_hi{k}", [D, CH], F32R) for k in range(DEPTH)]
        h_lo = [sb(f"h_lo{k}", [D, CH], F32R) for k in range(DEPTH)]
        total = sb("total", [D, CH])
        rows = [sb(f"rows{c}", [G, GC, D]) for c in range(NCH)]
        acc = [mem.enter_context(nc.psum_tensor(f"acc{c}", [D, BANK], F32)) for c in range(NCH)]
        gate_ps = [mem.enter_context(nc.psum_tensor(f"up1_{k}", [D, BANK], F32)) for k in range(2)]
        lin_ps = [mem.enter_context(nc.psum_tensor(f"up3_{k}", [D, BANK], F32)) for k in range(2)]
        cbank = mem.enter_context(nc.psum_tensor("cbank", [D, BANK], F32))
        nbank = mem.enter_context(nc.psum_tensor("nbank", [D, BANK], F32))

        s_pad = sems("moe_pads")
        s_thi, s_tlo = sems("moe_t_hi"), sems("moe_t_lo")
        s_cen, s_xc, s_sq, s_var = sems("moe_centered"), sems("moe_xc"), sems("moe_squared"), sems("moe_var")
        s_newton, s_packed = sems("moe_newton"), sems("moe_packed")
        s_turnps, s_turn = sems("moe_turned_psum"), sems("moe_turned")
        s_spread, s_xn = sems("moe_spread"), sems("moe_normed")
        s_nhi, s_nlo = sems("moe_n_hi"), sems("moe_n_lo")
        s_gate, s_route, s_prob = sems("moe_scores"), sems("moe_route_steps"), sems("moe_prob")
        s_cturnps, s_cturn = sems("moe_comb_turned_psum"), sems("moe_comb_turned")
        s_cspread, s_weight = sems("moe_comb_spread"), sems("moe_weight")
        s_up, s_silu, s_prod = sems("moe_up"), sems("moe_silu"), sems("moe_prod")
        s_scaled = sems("moe_scaled")
        s_hhi, s_hlo = sems("moe_hidden_hi"), sems("moe_hidden_lo")
        s_acc, s_total = sems("moe_summed"), sems("moe_total")
        s_read = sems("moe_last_buffer_read")
        s_rowps, s_rows = sems("moe_rows_psum"), sems("moe_rows")
        s_out = [sems(f"moe_out_stored{c}") for c in range(NCH)]

        def tok_chunk(b, c):
            return tok[:, bass.ds(b, 1), c * CH:(c + 1) * CH].rearrange("p o n -> p (o n)")

        def before(b, c):
            return (b, 0) if c else (b - 1, 1)

        def after(b, c):
            return (b + 1, 0) if c else (b, 1)

        def run_chunks(fori, chunk):
            chunk(0, 0, True, False)
            with fori(0, NB - 1) as b:
                chunk(b, 1, False, False)
                chunk(b + 1, 0, False, False)
            chunk(NB - 1, 1, False, True)

        SPREAD_AT = {2 * x + 1: x for x in range(1, NX)}

        ROWS_AT = 15

        with nc.Block() as block:
            @block.sync
            def _(sp):
                def store(b, c):
                    sp.wait_ge(s_rows, b * 2 + c + 2)
                    sp.dma_start(out[bass.ds(b, 1), c * CH:(c + 1) * CH, :].rearrange("o (g t) d -> t (o g) d", t=G),
                                 rows[c][:]).then_inc(s_out[c], 16)

                for c in range(NCH):
                    sp.sem_inc(s_out[c], 16)
                with sp.Fori(0, NB) as b:
                    for c in range(NCH):
                        store(b, c)
                for c in range(NCH):
                    sp.wait_ge(s_out[c], 16 * NB + 16)

            @block.gpsimd
            def _(pool):
                nc.gpsimd.memset(packed[:].bitcast(F32), 0.0).then_inc(s_pad, 1)
                nc.gpsimd.memset(packed_c[:].bitcast(F32), 0.0).then_inc(s_pad, 1)

                def prepare(b, c, step):
                    q = b * 2 + c
                    if step == "t_lo":
                        pool.wait_ge(s_thi, q + 1)
                        nc.gpsimd.tensor_tensor(t_lo[:], tok_chunk(b, c), t_hi[:].bitcast(F32), ALU.subtract
                                                ).then_inc(s_tlo, 1)
                    elif step == "n_lo":
                        pool.wait_ge(s_nhi, q + 1)
                        nc.gpsimd.tensor_tensor(n_lo[c][:], xn[:], n_hi[c][:].bitcast(F32), ALU.subtract
                                                ).then_inc(s_nlo, 1)

                at = {0: "t_lo", 12: "n_lo"}

                def chunk(b, c, first, last):
                    q = b * 2 + c
                    for u in range(UNITS):
                        x, k = u // HALVES, (2 * c + u) % DEPTH
                        if u >= HALVES:
                            pool.wait_ge(s_prod, q * UNITS + u + 1)
                            if u % HALVES == 0:
                                pool.wait_ge(s_weight, q * NE + x)
                            nc.gpsimd.tensor_tensor(scaled[k][:], prod[k][:], weight[x % 2][:], ALU.mult
                                                    ).then_inc(s_scaled, 1)
                        if u in at and not last:
                            prepare(*after(b, c), at[u])

                for step in at.values():
                    prepare(0, 0, step)
                run_chunks(pool.Fori, chunk)

            @block.scalar
            def _(act):
                op = nc.scalar.activation

                def split(b, c, s):
                    U = (b * 2 + c) * UNITS + s
                    u, k = s % UNITS, (2 * c + s) % DEPTH
                    if u < HALVES:
                        act.wait_ge(s_prod, U + 1)
                        op(h_hi[k][:], prod[k][:], ACT.Copy).then_inc(s_hhi, 1)
                    else:
                        done = (b * 2 + c) * SCALED + (s - HALVES if s >= 0 else s)
                        act.wait_ge(s_scaled, done + 1)
                        op(h_hi[k][:], scaled[k][:], ACT.Copy).then_inc(s_hhi, 1)

                def prepare(b, c, step):
                    q = b * 2 + c
                    if step == "t_hi":
                        op(t_hi[:], tok_chunk(b, c), ACT.Copy).then_inc(s_thi, 1)
                    elif step == "square":
                        act.wait_ge(s_cen, q + 1)
                        op(xc[:], nbank[:, 0:CH], ACT.Copy).then_inc(s_xc, 1)
                        act.wait_ge(s_xc, q + 1)
                        op(sq[:], xc[:], ACT.Square).then_inc(s_sq, 1)
                    elif step == "n_hi":
                        act.wait_ge(s_xn, q + 1)
                        op(n_hi[c][:], xn[:], ACT.Copy).then_inc(s_nhi, 1)
                    elif step == "prob":
                        act.wait_ge(s_route, q * ROUTE + SORTED)
                        op(silu_s[:], top_r[:, :, 0:2], ACT.Silu)
                        op(tanh_s[:], top_r[:, :, 0:2], ACT.Tanh, scale=0.5).then_inc(s_prob, 1)

                at = {0: "t_hi", 2: "square", 11: "n_hi", 13: "prob"}

                def chunk(b, c, first, last):
                    q = b * 2 + c
                    for s in range(UNITS):
                        act.wait_ge(s_up, q * UNITS + s + 1)
                        op(silu[s % 2][:], gate_ps[s % 2][:, 0:CH], ACT.Silu).then_inc(s_silu, 1)
                        if s >= HI_LAG or not first:
                            split(b, c, s - HI_LAG)
                        if s in SPREAD_AT:
                            x = SPREAD_AT[s]
                            act.wait_ge(s_cspread, q * NE + x)
                            op(weight[x % 2][:], cbank[:, 0:CH], ACT.Copy).then_inc(s_weight, 1)
                        if s in at and not last:
                            prepare(*after(b, c), at[s])
                        if s == ROWS_AT and not first:
                            send(*before(b, c))

                def send(b, c):
                    q = b * 2 + c
                    act.wait_ge(s_rowps, q + 1)
                    act.wait_ge(s_out[c], b * 16 + 16)
                    op(rows[c][:].rearrange("t g d -> t (g d)"), nbank[0:G, :], ACT.Copy).then_inc(s_rows, 1)

                act.sem_inc(s_rows, 1)
                for step in at.values():
                    prepare(0, 0, step)
                run_chunks(act.Fori, chunk)
                for s in range(UNITS - HI_LAG, UNITS):
                    if s == UNITS - 1:
                        act.wait_ge(s_read, NB * NCH)
                    split(NB - 1, 1, s)
                send(NB - 1, 1)

            @block.vector
            def _(dve):
                tt, stt = nc.vector.tensor_tensor, nc.vector.scalar_tensor_tensor

                def one(col, like=NE):
                    return col.unsqueeze(2).to_broadcast([G, GC, like])

                def make(b, c, s, first):
                    U, k = (b * 2 + c) * UNITS + s, (2 * c + s) % DEPTH
                    if s >= DEPTH or not first:
                        dve.wait_ge(s_hlo, U - DEPTH + 1)
                    dve.wait_ge(s_silu, U + 1)
                    tt(prod[k][:], lin_ps[s % 2][:, 0:CH], silu[s % 2][:], ALU.mult).then_inc(s_prod, 1)

                def rest(b, c, s):
                    k = (2 * c + s) % DEPTH
                    full = prod[k] if s % UNITS < HALVES else scaled[k]
                    dve.wait_ge(s_hhi, (b * 2 + c) * UNITS + s + 1)
                    tt(h_lo[k][:], full[:], h_hi[k][:].bitcast(F32), ALU.subtract).then_inc(s_hlo, 1)

                def newton(b, c, k):
                    q = b * 2 + c
                    if k == 0:
                        dve.wait_ge(s_var, q + 1)
                    elif k <= NEWTON:
                        dve.wait_ge(s_newton, q * NEWTON + k)
                    else:
                        dve.wait_ge(s_packed, q * 2 + 1)
                    if k < NEWTON:
                        rsqrt_step(nc.vector, k, nbank[0:G, 0:GC], small).then_inc(s_newton, 1)
                    elif k == NEWTON:
                        nc.vector.tensor_copy(packed[:, 0:GC], small[1][:]).then_inc(s_packed, 1)
                    else:
                        tt(packed[:, 32:32 + GC], small[1][:], packed[:, 0:GC].bitcast(F32), ALU.subtract
                           ).then_inc(s_packed, 1)

                def route(b, c, part):
                    q = b * 2 + c
                    k = [{0: 0, 1: SORTED, 2: SORTED + 4, 3: SORTED + 8, 4: SORTED + 11}[part]]

                    def link(ins):
                        k[0] += 1
                        ins.then_inc(s_route, 1)
                        dve.wait_ge(s_route, q * ROUTE + k[0])

                    if part == 0:
                        dve.wait_ge(s_gate, q + 1)
                        scores = nbank[0:G, 0:GC * NE].rearrange("t (g e) -> t g e", e=NE)
                        tt(biased[:], scores, gate_b[:], ALU.add)
                        link(nc.vector.tensor_copy(raw[:], scores))
                        nc.vector.memset(fence[:, 0:1], 0.0)
                        for g in range(GC):
                            nc.vector.max(top_b[:, g, :], biased[:, g, :])
                            ins = nc.vector.max(top_r[:, g, :], raw[:, g, :])
                        link(ins)
                        nc.vector.memset(fence[:, 1:2], 0.0)
                    elif part == 1:
                        for g in range(GC):
                            ins = nc.vector.max_index(index[:, g, :], top_b[:, g, :], biased[:, g, :])
                        link(ins)
                        link(nc.vector.tensor_copy(indexf[:], index[:]))
                        tt(comb[:], iota[:], one(indexf[:, :, 0]), ALU.is_equal)
                        tt(comb2[:], iota[:], one(indexf[:, :, 1]), ALU.is_equal)
                        link(stt(out=mag[:], in0=top_r[:, :, 0:2], scalar=-1.0, in1=top_r[:, :, 0:2], op0=ALU.mult,
                                 op1=ALU.max))
                        nc.vector.tensor_scalar(is_far[:], mag[:], 1.0, None, ALU.is_gt)
                        nc.vector.tensor_scalar(is_near[:], mag[:], 1.0, None, ALU.is_le)
                        link(nc.vector.tensor_scalar(inv_mag[:], mag[:], 1.0, None, ALU.max))
                    elif part == 2:
                        link(nc.vector.reciprocal(inv_mag[:], inv_mag[:]))
                        dve.wait_ge(s_prob, q + 1)
                        nc.vector.tensor_scalar(near_s[:], tanh_s[:], 0.5, 0.5, ALU.mult, ALU.add)
                        stt(out=far_s[:], in0=silu_s[:], scalar=-1.0, in1=silu_s[:], op0=ALU.mult, op1=ALU.max)
                        link(tt(is_far[:], is_far[:], inv_mag[:], ALU.mult))
                        tt(near_s[:], near_s[:], is_near[:], ALU.mult)
                        link(tt(far_s[:], far_s[:], is_far[:], ALU.mult))
                        link(tt(prob[:], near_s[:], far_s[:], ALU.add))
                    elif part == 3:
                        link(tt(psumt[:], prob[:, :, 0], prob[:, :, 1], ALU.add))
                        link(nc.vector.reciprocal(prec[:], psumt[:]))
                        link(tt(pn[:], prob[:], one(prec[:], 2), ALU.mult))
                    elif part == 4:
                        tt(comb[:], comb[:], one(pn[:, :, 0]), ALU.mult)
                        link(tt(comb2[:], comb2[:], one(pn[:, :, 1]), ALU.mult))
                        link(tt(comb[:], comb[:], comb2[:], ALU.add))
                        link(nc.vector.tensor_copy(packed_c[:, :, 0:NE], comb[:]))
                        link(tt(packed_c[:, :, 32:32 + NE], comb[:], packed_c[:, :, 0:NE].bitcast(F32), ALU.subtract))
                        assert k[0] == ROUTE

                def prepare(b, c, step):
                    q = b * 2 + c
                    if step == "turned":
                        dve.wait_ge(s_turnps, q + 1)
                        nc.vector.tensor_copy(turned[:], nbank[0:40, 0:G]).then_inc(s_turn, 1)
                    elif step == "xn":
                        dve.wait_ge(s_spread, q + 1)
                        dve.wait_ge(s_xc, q + 1)
                        tt(xn[:], nbank[:, 0:CH], xc[:], ALU.mult).then_inc(s_xn, 1)

                at = {8: "turned", 10: "xn"}
                NEWTON_AT, A_SLOT, ROUTE_AT = 4, (NEWTON + 2 + 1) // 2, 12

                def finish(b, c):
                    dve.wait_ge(s_acc, b * 2 + c + 1)
                    tt(total[:], acc[c][:, 0:CH], tok_chunk(b, c), ALU.add).then_inc(s_total, 1)

                def chunk(b, c, first, last):
                    q = b * 2 + c
                    for s in range(UNITS):
                        steps = list(range(NEWTON + 2))[max(s - NEWTON_AT, 0) * A_SLOT:max(s - NEWTON_AT + 1, 0) * A_SLOT]
                        if last:
                            steps = []
                        make(b, c, s, first)
                        for k in steps[:A_SLOT // 2]:
                            newton(*after(b, c), k)
                        if s == 1:
                            dve.wait_ge(s_cturnps, q + 1)
                            nc.vector.tensor_copy(turned_c[:], cbank[0:40, 0:CH]).then_inc(s_cturn, 1)
                        if s in at and not last:
                            prepare(*after(b, c), at[s])
                        if s >= HI_LAG or not first:
                            rest(b, c, s - HI_LAG)
                        for k in steps[A_SLOT // 2:]:
                            newton(*after(b, c), k)
                        if s == 4 and not first:
                            finish(*before(b, c))
                        if ROUTE_AT <= s < ROUTE_AT + 5 and not last:
                            route(*after(b, c), s - ROUTE_AT)

                dve.sem_inc(s_total, 1)
                dve.wait_ge(s_pad, 2)
                for k in range(NEWTON + 2):
                    newton(0, 0, k)
                for step in ("turned", "xn"):
                    prepare(0, 0, step)
                for part in range(5):
                    route(0, 0, part)
                run_chunks(dve.Fori, chunk)
                for s in range(UNITS - HI_LAG, UNITS):
                    rest(NB - 1, 1, s)
                finish(NB - 1, 1)

            @block.tensor
            def _(pe):
                def three(o, hi, lo, v_hi, v_lo, start=True, stop=True):
                    nc.tensor.matmul(o, hi, v_hi, start=start, stop=False)
                    nc.tensor.matmul(o, hi, v_lo, start=False, stop=False)
                    return nc.tensor.matmul(o, lo, v_hi, start=False, stop=stop)

                def up(b, c, s, first):
                    q, x, r = b * 2 + c, s // HALVES, s % HALVES
                    e, cols = expert[x], slice(r * D, (r + 1) * D)
                    if s == 0:
                        pe.wait_ge(s_nlo, q + 1)
                    if s >= 2 or not first:
                        pe.wait_ge(s_prod, q * UNITS + s - 1)
                    three(gate_ps[s % 2][:, 0:CH], w1_hi[:, e, cols], w1_lo[:, e, cols], n_hi[c][:], n_lo[c][:])
                    three(lin_ps[s % 2][:, 0:CH], w3_hi[:, e, cols], w3_lo[:, e, cols], n_hi[c][:], n_lo[c][:]
                          ).then_inc(s_up, 1)

                def down(b, c, s):
                    q, u, k = b * 2 + c, s % UNITS, (2 * c + s) % DEPTH
                    bank = acc[c if s >= 0 else 1 - c]
                    x, r = u // HALVES, u % HALVES
                    if u == 0 and not (isinstance(b, int) and b == 0 and c == 0):
                        pe.wait_ge(s_total, q)
                    pe.wait_ge(s_hlo, q * UNITS + s + 1)
                    mm = three(bank[:, 0:CH], w2_hi[:, expert[x], r, :], w2_lo[:, expert[x], r, :], h_hi[k][:], h_lo[k][:],
                               start=(u == 0), stop=(u == UNITS - 1))
                    if u == UNITS - 1:
                        mm.then_inc(s_acc, 1)
                    if u == UNITS - 1 - DEPTH:
                        mm.then_inc(s_read, 1)

                def prepare(b, c, step):
                    q = b * 2 + c
                    if step == "center":
                        pe.wait_ge(s_tlo, q + 1)
                        nc.tensor.matmul(nbank[:, 0:CH], cen[:], t_hi[:], start=True, stop=False)
                        nc.tensor.matmul(nbank[:, 0:CH], cen[:], t_lo[:], start=False, stop=True).then_inc(s_cen, 1)
                    elif step == "var":
                        pe.wait_ge(s_sq, q + 1)
                        for g in range(GC):
                            mm = nc.tensor.matmul(nbank[0:G, g:g + 1], sq[:, g * G:(g + 1) * G], mean1[:], start=True,
                                                  stop=True)
                        mm.then_inc(s_var, 1)
                    elif step == "turn":
                        pe.wait_ge(s_packed, q * 2 + 2)
                        nc.tensor.matmul(nbank[:, 0:G], packed[:].bitcast(F32), ident[0:G, 0:G], is_transpose=True,
                                         start=True, stop=True).then_inc(s_turnps, 1)
                    elif step == "spread":
                        pe.wait_ge(s_turn, q + 1)
                        for g in range(GC):
                            mm = nc.tensor.matmul(nbank[:, g * G:(g + 1) * G], sel[:, g, :], turned[:], start=True, stop=True)
                        mm.then_inc(s_spread, 1)
                    elif step == "gate":
                        pe.wait_ge(s_xn, q + 1)
                        for g in range(GC):
                            mm = nc.tensor.matmul(nbank[0:G, g * NE:(g + 1) * NE], xn[:, g * G:(g + 1) * G], gate_w[:],
                                                  start=True, stop=True)
                        mm.then_inc(s_gate, 1)

                def spread(q, x):
                    if x > 1:
                        pe.wait_ge(s_weight, q * NE + x - 1)
                    else:
                        pe.wait_ge(s_cturn, q + 1)
                    nc.tensor.matmul(cbank[:, 0:CH], sel[:, x - 1, :], turned_c[:], start=True, stop=True
                                     ).then_inc(s_cspread, 1)

                def by_token(b, c):
                    pe.wait_ge(s_total, b * 2 + c + 2)
                    for g in range(GC):
                        mm = nc.tensor.matmul(nbank[0:G, g * D:(g + 1) * D], total[:, g * G:(g + 1) * G], ident[:],
                                              start=True, stop=True)
                    mm.then_inc(s_rowps, 1)

                at = {2: "center", 4: "var", 8: "turn", 10: "spread", 12: "gate"}

                def chunk(b, c, first, last):
                    q = b * 2 + c
                    for s in range(UNITS):
                        if s == 1:
                            pe.wait_ge(s_route, (q + 1) * ROUTE)
                            if not first:
                                pe.wait_ge(s_weight, q * NE)
                            for g in range(GC):
                                mm = nc.tensor.matmul(cbank[:, g * G:(g + 1) * G], packed_c[:, g, :].bitcast(F32),
                                                      ident[0:G, 0:G], is_transpose=True, start=True, stop=True)
                            mm.then_inc(s_cturnps, 1)
                        if s in SPREAD_AT:
                            spread(q, SPREAD_AT[s])
                        if s in at and not last:
                            if at[s] == "center" and not first:
                                pe.wait_ge(s_rows, q)
                            prepare(*after(b, c), at[s])
                        if s == ROWS_AT and not first:
                            if not last:
                                pe.wait_ge(s_route, (q + 1) * ROUTE + 1)
                            by_token(*before(b, c))
                        up(b, c, s, first)
                        if s >= DOWN_LAG or not first:
                            down(b, c, s - DOWN_LAG)

                for step in at.values():
                    prepare(0, 0, step)
                run_chunks(pe.Fori, chunk)
                for s in range(UNITS - DOWN_LAG, UNITS):
                    down(NB - 1, 1, s)
                by_token(NB - 1, 1)

SORTED, ROUTE = 2, 17

def early_fusion(nc, x, txt, tok_w, tok_b, p, out):
    with ExitStack() as ctx:
        def sems(name):
            return ctx.enter_context(nc.semaphore(name))

        tok = ctx.enter_context(nc.sbuf_tensor("tok", [D, NB, S], F32))
        conv_phase(nc, sems, tok, x, txt, tok_w, tok_b)
        with ExitStack() as staging:
            stage, s_stage = moe_staging(nc, sems, staging)
            mixer_phase(nc, sems, tok, p, stage, s_stage)
            moe_phase(nc, sems, tok, out, p, stage, s_stage)

def kernel(**inputs):
    import numpy as np
    import concourse.bacc as _bacc
    from concourse.bass_utils import run_bass_kernel_spmd as _run

    a = {k: np.asarray(v) for k, v in inputs.items()}
    at = {k[len("L0_attn_"):]: v for k, v in a.items() if k.startswith("L0_attn_")}
    ff = {k[len("L0_ffn_"):]: v for k, v in a.items() if k.startswith("L0_ffn_")}
    sel = np.zeros((40, NG, D), np.float32)
    for g in range(NG):
        sel[g, g] = sel[32 + g, g] = 1.0
    arrays = {
        "x": a["x"].reshape(NB, D, HIN, WO, STR).transpose(0, 1, 2, 4, 3).reshape(NB, D, HIN * WIN),
        "txt": a["txt"].transpose(2, 0, 1),
        "tok_w": a["L0_tok_W"].reshape(D, D, KSZ * KSZ).transpose(1, 2, 0).reshape(D, KSZ * KSZ * D),
        "tok_b": a["L0_tok_b"].reshape(D, 1),
    }
    small = {
        "pw": at["conv_pw_w"].transpose(2, 0, 1),
        "pw0n": at["conv_pw_w"][0],
        "f": at["f_w"].transpose(2, 0, 1),
        "w1": at["mlp_w1"].transpose(2, 0, 1),
        "w2": at["mlp_w2"].reshape(LAYERS, D, HT, D).transpose(3, 0, 2, 1),
        "cen": (np.eye(D) - 1.0 / D).astype(np.float32),
        "mean1": np.full((D, 1), 1.0 / D, np.float32),
        "ident": np.eye(D, dtype=np.float32),
        "sel": sel,
        "dw": at["conv_dw_w"].transpose(2, 0, 1),
        "dwb": at["conv_dw_b"].T,
        "pwb": at["conv_pw_b"].T,
        "ln1g": at["ln1_g"].reshape(D, 1),
        "ln1b": at["ln1_b"].reshape(D, 1),
        "ln2g": at["ln2_g"].T,
        "ln2b": at["ln2_b"].T,
        "b1": at["mlp_b1"].reshape(LAYERS * HT, D).T,
        "b2": at["mlp_b2"].T,
        "e1": np.concatenate([ff["w1"], ff["sw1"][None]]).transpose(1, 0, 2),
        "e3": np.concatenate([ff["w3"], ff["sw3"][None]]).transpose(1, 0, 2),
        "e2": np.concatenate([ff["w2"], ff["sw2"][None]]).reshape(NE + 1, MH // D, D, D).transpose(2, 0, 1, 3),
        "gate_w": ff["gate_w"].T,
        "gate_b": np.broadcast_to(ff["biases"], (G, GC, NE)),
        "iota": np.broadcast_to(np.arange(NE, dtype=np.float32), (G, GC, NE)),
    }
    nc = _bacc.Bacc("TRN2", target_bir_lowering=False, num_devices=1)
    feed, aps = {}, {}
    for name, v in {**arrays, **small}.items():
        feed["in_" + name] = np.ascontiguousarray(v)
        aps[name] = nc.dram_tensor("in_" + name, feed["in_" + name].shape, F32, kind="ExternalInput").ap()
    out = nc.dram_tensor("out", (NB, S, D), F32, kind="ExternalOutput").ap()
    early_fusion(nc, aps["x"], aps["txt"], aps["tok_w"], aps["tok_b"], aps, out)
    r = _run(nc, [feed], core_ids=[0])
    return r.results[0]["out"]
```
